# Optimizing a Trainium2 kernel written in Bass

```python
import numpy as np
import jax
import jax.numpy as jnp

def _softmax(x, axis=-1):
    return jax.nn.softmax(x, axis=axis)

def _gelu(x):
    return jax.nn.gelu(x, approximate=True)

def _silu(x):
    return jax.nn.silu(x)

def _sigmoid(x):
    return jax.nn.sigmoid(x)

def _layernorm(x, axis=-1, eps=1e-05):
    m = jnp.mean(x, axis=axis, keepdims=True)
    v = jnp.var(x, axis=axis, keepdims=True)
    return (x - m) / jnp.sqrt(v + eps)

def _scatter_add(tgt, idx, src, axis=0):
    return tgt.at[idx].add(src)

def _segment_sum(src, seg, n):
    return jax.ops.segment_sum(src, seg, n)
kernel_name = 'mk_adaln_d2_jaxref_r4_12dddb'

def setup_inputs(seed: int=0):
    np.random.seed(seed)
    _w = jnp.asarray

    def _L0_attn_setup():
        import jax, jax.numpy as jnp
        import numpy as np
        import math
        B, T, C = (2, 512, 256)
        H, L = (16, 64)
        DH = C // H
        DHE = DH // 2
        THETA = 10000.0

        def _rope_cache(t, dim):
            inv_freq = 1.0 / THETA ** (jnp.arange(0, dim, 2, dtype=jnp.float32) / dim)
            freqs = jnp.arange(t, dtype=jnp.float32)[:, None] * inv_freq[None, :]
            emb = jnp.concatenate((freqs, freqs), axis=-1)
            return (jnp.cos(emb), jnp.sin(emb))

        def _apply_rope(x, cos, sin):
            x1 = x[..., 0::2]
            x2 = x[..., 1::2]
            rot = jnp.stack((-x2, x1), axis=-1).reshape(x.shape)
            return x * cos[None, None] + rot * sin[None, None]
        key = jax.random.key(seed)
        ks = jax.random.split(key, 10)
        s = 0.02
        return {'x': jax.random.normal(ks[0], (B, T, C), jnp.float32), 'Wq_down': jax.random.normal(ks[1], (C, H * L), jnp.float32) * s, 'Wk_down': jax.random.normal(ks[2], (C, H * L), jnp.float32) * s, 'Wv_down': jax.random.normal(ks[3], (C, H * L), jnp.float32) * s, 'Wq_up_c': jax.random.normal(ks[4], (L, DHE), jnp.float32) * s, 'Wq_up_e': jax.random.normal(ks[5], (L, DHE), jnp.float32) * s, 'Wk_up_c': jax.random.normal(ks[6], (L, DHE), jnp.float32) * s, 'Wk_up_e': jax.random.normal(ks[7], (L, DHE), jnp.float32) * s, 'Wv_up': jax.random.normal(ks[8], (L, DH), jnp.float32) * s, 'Wc': jax.random.normal(ks[9], (C, C), jnp.float32) * s}
    _L0_attn_in = _L0_attn_setup()

    def _L0_ffn_setup():
        import jax, jax.numpy as jnp
        import numpy as np
        D_MODEL = 256
        M = 64
        INNER = 16
        key = jax.random.key(seed)
        ks = jax.random.split(key, 9)

        def init(k, shape, fan_in):
            bound = 1.0 / np.sqrt(fan_in)
            return jax.random.uniform(k, shape, jnp.float32, -bound, bound)
        x = jax.random.normal(ks[0], (16, 1024, D_MODEL), dtype=jnp.float32)
        Win = init(ks[1], (D_MODEL, M), D_MODEL)
        bin_ = init(ks[2], (M,), D_MODEL)
        W1 = init(ks[3], (M, INNER), 1)
        b1 = init(ks[4], (M, INNER), 1)
        W2 = init(ks[5], (M, INNER), INNER)
        b2 = init(ks[6], (M,), INNER)
        Wout = init(ks[7], (M, D_MODEL), M)
        bout = init(ks[8], (D_MODEL,), M)
        return {'x': x, 'Win': Win, 'bin_': bin_, 'W1': W1, 'b1': b1, 'W2': W2, 'b2': b2, 'Wout': Wout, 'bout': bout}
    _L0_ffn_in = _L0_ffn_setup()
    _L0_c = _w((lambda *s: np.random.randn(*s).astype(np.float32) * 0.05)(8, 256))
    _L0_wmod = _w((lambda *s: np.random.randn(*s).astype(np.float32) * 0.05)(256, 6 * 256) * 256 ** (-0.5))

    def _L1_attn_setup():
        import jax, jax.numpy as jnp
        import numpy as np
        B, L = (4, 512)
        D_MODEL, D_INNER, D_STATE, DT_RANK, D_CONV = (256, 512, 16, 64, 4)
        key = jax.random.key(seed)
        ks = jax.random.split(key, 10)
        s = lambda k, shape, sc: jax.random.normal(k, shape, dtype=jnp.float32) * sc
        return {'x': s(ks[0], (B, L, D_MODEL), 1.0), 'W_in': s(ks[1], (2 * D_INNER, D_MODEL), D_MODEL ** (-0.5)), 'conv_w': s(ks[2], (D_INNER, D_CONV), D_CONV ** (-0.5)), 'conv_b': s(ks[3], (D_INNER,), 0.02), 'A_log': jnp.log(jnp.arange(1, D_STATE + 1, dtype=jnp.float32)), 'D': jnp.ones((D_INNER,), dtype=jnp.float32), 'W_x': s(ks[4], (DT_RANK + 2 * D_STATE, D_INNER), D_INNER ** (-0.5)), 'W_dt': s(ks[5], (D_INNER, DT_RANK), DT_RANK ** (-0.5)), 'b_dt': s(ks[6], (D_INNER,), 0.02) - 4.0, 'W_out': s(ks[7], (D_MODEL, D_INNER), D_INNER ** (-0.5))}
    _L1_attn_in = _L1_attn_setup()

    def _L1_ffn_setup():
        import jax, jax.numpy as jnp
        import numpy as np
        D_MODEL = 256
        EXPANSION = 4
        D_HIDDEN = D_MODEL * EXPANSION
        NUM_STAGES = int(np.log2(D_HIDDEN))

        def butterfly(y, weights, dim):
            lead = y.shape[:-1]
            for stage in range(weights.shape[0]):
                s = 2 ** stage
                nb = dim // (2 * s)
                yr = y.reshape(*lead, nb, 2, s)
                a = yr[..., 0, :]
                b = yr[..., 1, :]
                w = weights[stage].reshape(nb, s, 2, 2)
                na = w[..., 0, 0] * a + w[..., 0, 1] * b
                nb2 = w[..., 1, 0] * a + w[..., 1, 1] * b
                y = jnp.stack([na, nb2], axis=-2).reshape(*lead, dim)
            return y
        key = jax.random.key(seed)
        ks = jax.random.split(key, 6)
        B, S = (4, 512)
        x = jax.random.normal(ks[0], (B, S, D_MODEL), jnp.float32)
        W_exp = jax.random.normal(ks[1], (D_MODEL, D_HIDDEN), jnp.float32) * 0.02
        b_exp = jnp.zeros((D_HIDDEN,), jnp.float32)
        up_weights = jax.random.normal(ks[2], (NUM_STAGES, D_HIDDEN // 2, 2, 2), jnp.float32) * 0.02
        up_bias = jnp.zeros((D_HIDDEN,), jnp.float32)
        down_weights = jax.random.normal(ks[3], (NUM_STAGES, D_HIDDEN // 2, 2, 2), jnp.float32) * 0.02
        W_con = jax.random.normal(ks[4], (D_HIDDEN, D_MODEL), jnp.float32) * 0.02
        b_con = jnp.zeros((D_MODEL,), jnp.float32)
        down_bias = jnp.zeros((D_MODEL,), jnp.float32)
        return dict(x=x, W_exp=W_exp, b_exp=b_exp, up_weights=up_weights, up_bias=up_bias, down_weights=down_weights, W_con=W_con, b_con=b_con, down_bias=down_bias)
    _L1_ffn_in = _L1_ffn_setup()
    _L1_c = _w((lambda *s: np.random.randn(*s).astype(np.float32) * 0.05)(8, 256))
    _L1_wmod = _w((lambda *s: np.random.randn(*s).astype(np.float32) * 0.05)(256, 6 * 256) * 256 ** (-0.5))
    _d = {'L0_attn_x': _L0_attn_in['x'], 'L0_attn_Wq_down': _L0_attn_in['Wq_down'], 'L0_attn_Wk_down': _L0_attn_in['Wk_down'], 'L0_attn_Wv_down': _L0_attn_in['Wv_down'], 'L0_attn_Wq_up_c': _L0_attn_in['Wq_up_c'], 'L0_attn_Wq_up_e': _L0_attn_in['Wq_up_e'], 'L0_attn_Wk_up_c': _L0_attn_in['Wk_up_c'], 'L0_attn_Wk_up_e': _L0_attn_in['Wk_up_e'], 'L0_attn_Wv_up': _L0_attn_in['Wv_up'], 'L0_attn_Wc': _L0_attn_in['Wc'], 'L0_ffn_Win': _L0_ffn_in['Win'], 'L0_ffn_bin_': _L0_ffn_in['bin_'], 'L0_ffn_W1': _L0_ffn_in['W1'], 'L0_ffn_b1': _L0_ffn_in['b1'], 'L0_ffn_W2': _L0_ffn_in['W2'], 'L0_ffn_b2': _L0_ffn_in['b2'], 'L0_ffn_Wout': _L0_ffn_in['Wout'], 'L0_ffn_bout': _L0_ffn_in['bout'], 'L0_c': _L0_c, 'L0_wmod': _L0_wmod, 'L1_attn_W_in': _L1_attn_in['W_in'], 'L1_attn_conv_w': _L1_attn_in['conv_w'], 'L1_attn_conv_b': _L1_attn_in['conv_b'], 'L1_attn_A_log': _L1_attn_in['A_log'], 'L1_attn_D': _L1_attn_in['D'], 'L1_attn_W_x': _L1_attn_in['W_x'], 'L1_attn_W_dt': _L1_attn_in['W_dt'], 'L1_attn_b_dt': _L1_attn_in['b_dt'], 'L1_attn_W_out': _L1_attn_in['W_out'], 'L1_ffn_W_exp': _L1_ffn_in['W_exp'], 'L1_ffn_b_exp': _L1_ffn_in['b_exp'], 'L1_ffn_up_weights': _L1_ffn_in['up_weights'], 'L1_ffn_up_bias': _L1_ffn_in['up_bias'], 'L1_ffn_down_weights': _L1_ffn_in['down_weights'], 'L1_ffn_W_con': _L1_ffn_in['W_con'], 'L1_ffn_b_con': _L1_ffn_in['b_con'], 'L1_ffn_down_bias': _L1_ffn_in['down_bias'], 'L1_c': _L1_c, 'L1_wmod': _L1_wmod}
    _x0 = _d['L0_attn_x']
    _d['L0_attn_x'] = jax.random.normal(jax.random.fold_in(jax.random.key(seed), 1), (8, 1024, 256), dtype=_x0.dtype)
    del _x0
    return _d

def reference(L0_attn_x, L0_attn_Wq_down, L0_attn_Wk_down, L0_attn_Wv_down, L0_attn_Wq_up_c, L0_attn_Wq_up_e, L0_attn_Wk_up_c, L0_attn_Wk_up_e, L0_attn_Wv_up, L0_attn_Wc, L0_ffn_Win, L0_ffn_bin_, L0_ffn_W1, L0_ffn_b1, L0_ffn_W2, L0_ffn_b2, L0_ffn_Wout, L0_ffn_bout, L0_c, L0_wmod, L1_attn_W_in, L1_attn_conv_w, L1_attn_conv_b, L1_attn_A_log, L1_attn_D, L1_attn_W_x, L1_attn_W_dt, L1_attn_b_dt, L1_attn_W_out, L1_ffn_W_exp, L1_ffn_b_exp, L1_ffn_up_weights, L1_ffn_up_bias, L1_ffn_down_weights, L1_ffn_W_con, L1_ffn_b_con, L1_ffn_down_bias, L1_c, L1_wmod):

    def _L0_attn_ref(x, Wq_down, Wk_down, Wv_down, Wq_up_c, Wq_up_e, Wk_up_c, Wk_up_e, Wv_up, Wc):
        import jax, jax.numpy as jnp
        import numpy as np
        import math
        B, T, C = (2, 512, 256)
        H, L = (16, 64)
        DH = C // H
        DHE = DH // 2
        THETA = 10000.0

        def _rope_cache(t, dim):
            inv_freq = 1.0 / THETA ** (jnp.arange(0, dim, 2, dtype=jnp.float32) / dim)
            freqs = jnp.arange(t, dtype=jnp.float32)[:, None] * inv_freq[None, :]
            emb = jnp.concatenate((freqs, freqs), axis=-1)
            return (jnp.cos(emb), jnp.sin(emb))

        def _apply_rope(x, cos, sin):
            x1 = x[..., 0::2]
            x2 = x[..., 1::2]
            rot = jnp.stack((-x2, x1), axis=-1).reshape(x.shape)
            return x * cos[None, None] + rot * sin[None, None]
        b, t, c = x.shape
        q_lat = (x @ Wq_down).reshape(b, t, H, L)
        k_lat = (x @ Wk_down).reshape(b, t, H, L)
        v_lat = (x @ Wv_down).reshape(b, t, H, L)
        q_c = jnp.einsum('bthl,ld->bhtd', q_lat, Wq_up_c)
        q_e = jnp.einsum('bthl,ld->bhtd', q_lat, Wq_up_e)
        k_c = jnp.einsum('bthl,ld->bhtd', k_lat, Wk_up_c)
        k_e = jnp.einsum('bthl,ld->bhtd', k_lat, Wk_up_e)
        v = jnp.einsum('bthl,ld->bhtd', v_lat, Wv_up)
        cos, sin = _rope_cache(t, DHE)
        q = jnp.concatenate([q_c, _apply_rope(q_e, cos, sin)], axis=-1)
        k = jnp.concatenate([k_c, _apply_rope(k_e, cos, sin)], axis=-1)
        scale = 1.0 / math.sqrt(DH)
        scores = jnp.einsum('bhqd,bhkd->bhqk', q, k) * scale
        causal = jnp.tril(jnp.ones((t, t), dtype=bool))
        scores = jnp.where(causal[None, None], scores, -jnp.inf)
        att = jax.nn.softmax(scores, axis=-1)
        y = jnp.einsum('bhqk,bhkd->bhqd', att, v)
        y = y.transpose(0, 2, 1, 3).reshape(b, t, c)
        return y @ Wc

    def _L0_ffn_ref(x, Win, bin_, W1, b1, W2, b2, Wout, bout):
        import jax, jax.numpy as jnp
        import numpy as np
        D_MODEL = 256
        M = 64
        INNER = 16
        s = jnp.einsum('btd,dm->btm', x, Win) + bin_
        h = jax.nn.relu(s[..., None] * W1 + b1)
        g = jnp.einsum('btmh,mh->btm', h, W2) + b2
        out = jnp.einsum('btm,md->btd', g, Wout) + bout
        return out

    def _L1_attn_ref(x, W_in, conv_w, conv_b, A_log, D, W_x, W_dt, b_dt, W_out):
        import jax, jax.numpy as jnp
        import numpy as np
        B, L = (4, 512)
        D_MODEL, D_INNER, D_STATE, DT_RANK, D_CONV = (256, 512, 16, 64, 4)
        Bb, Ll, _ = x.shape
        xz = x @ W_in.T
        xr, z = jnp.split(xz, 2, axis=-1)
        xc = jax.lax.conv_general_dilated(xr.transpose(0, 2, 1), conv_w[:, None, :], window_strides=(1,), padding=[(D_CONV - 1, 0)], dimension_numbers=('NCH', 'OIH', 'NCH'), feature_group_count=D_INNER) + conv_b[None, :, None]
        xs = jax.nn.silu(xc.transpose(0, 2, 1))
        x_dbl = xs @ W_x.T
        dt_r, b_sel, c_sel = jnp.split(x_dbl, [DT_RANK, DT_RANK + D_STATE], axis=-1)
        dt = jax.nn.softplus(dt_r @ W_dt.T + b_dt)
        a_diag = -jnp.exp(A_log)

        def step(h, inp):
            dt_t, b_t, c_t, x_t = inp
            a_bar = jnp.exp(dt_t[:, :, None] * a_diag)
            h = a_bar * h + (dt_t * x_t)[:, :, None] * b_t[:, None, :]
            y = jnp.einsum('bds,bs->bd', h, c_t) + D * x_t
            return (h, y)
        h0 = jnp.zeros((Bb, D_INNER, D_STATE), dtype=x.dtype)
        _, ys = jax.lax.scan(step, h0, (dt.transpose(1, 0, 2), b_sel.transpose(1, 0, 2), c_sel.transpose(1, 0, 2), xs.transpose(1, 0, 2)))
        y = ys.transpose(1, 0, 2)
        return y * jax.nn.silu(z) @ W_out.T

    def _L1_ffn_ref(x, W_exp, b_exp, up_weights, up_bias, down_weights, W_con, b_con, down_bias):
        import jax, jax.numpy as jnp
        import numpy as np
        D_MODEL = 256
        EXPANSION = 4
        D_HIDDEN = D_MODEL * EXPANSION
        NUM_STAGES = int(np.log2(D_HIDDEN))

        def butterfly(y, weights, dim):
            lead = y.shape[:-1]
            for stage in range(weights.shape[0]):
                s = 2 ** stage
                nb = dim // (2 * s)
                yr = y.reshape(*lead, nb, 2, s)
                a = yr[..., 0, :]
                b = yr[..., 1, :]
                w = weights[stage].reshape(nb, s, 2, 2)
                na = w[..., 0, 0] * a + w[..., 0, 1] * b
                nb2 = w[..., 1, 0] * a + w[..., 1, 1] * b
                y = jnp.stack([na, nb2], axis=-2).reshape(*lead, dim)
            return y
        h = jnp.einsum('bsd,dh->bsh', x, W_exp) + b_exp
        h = butterfly(h, up_weights, D_HIDDEN)
        h = jax.nn.gelu(h + up_bias, approximate=False)
        h = butterfly(h, down_weights, D_HIDDEN)
        y = jnp.einsum('bsh,hd->bsd', h, W_con) + b_con
        return y + down_bias
    x = L0_attn_x
    mod = (_silu(L0_c) @ L0_wmod).reshape(L0_c.shape[0], 6, 1, -1)
    sa, ca, ga, sb, cb, gb = (mod[:, 0], mod[:, 1], mod[:, 2], mod[:, 3], mod[:, 4], mod[:, 5])
    ga = (2 * (ga >= 0) - 1) * jnp.maximum(jnp.abs(ga), 0.25)
    gb = (2 * (gb >= 0) - 1) * jnp.maximum(jnp.abs(gb), 0.25)
    h = _layernorm(x, axis=-1) * (1 + ca) + sa
    x = x + ga * _L0_attn_ref(h, L0_attn_Wq_down, L0_attn_Wk_down, L0_attn_Wv_down, L0_attn_Wq_up_c, L0_attn_Wq_up_e, L0_attn_Wk_up_c, L0_attn_Wk_up_e, L0_attn_Wv_up, L0_attn_Wc)
    h = _layernorm(x, axis=-1) * (1 + cb) + sb
    x = x + gb * _L0_ffn_ref(h, L0_ffn_Win, L0_ffn_bin_, L0_ffn_W1, L0_ffn_b1, L0_ffn_W2, L0_ffn_b2, L0_ffn_Wout, L0_ffn_bout)
    mod = (_silu(L1_c) @ L1_wmod).reshape(L1_c.shape[0], 6, 1, -1)
    sa, ca, ga, sb, cb, gb = (mod[:, 0], mod[:, 1], mod[:, 2], mod[:, 3], mod[:, 4], mod[:, 5])
    ga = (2 * (ga >= 0) - 1) * jnp.maximum(jnp.abs(ga), 0.25)
    gb = (2 * (gb >= 0) - 1) * jnp.maximum(jnp.abs(gb), 0.25)
    h = _layernorm(x, axis=-1) * (1 + ca) + sa
    x = x + ga * _L1_attn_ref(h, L1_attn_W_in, L1_attn_conv_w, L1_attn_conv_b, L1_attn_A_log, L1_attn_D, L1_attn_W_x, L1_attn_W_dt, L1_attn_b_dt, L1_attn_W_out)
    h = _layernorm(x, axis=-1) * (1 + cb) + sb
    x = x + gb * _L1_ffn_ref(h, L1_ffn_W_exp, L1_ffn_b_exp, L1_ffn_up_weights, L1_ffn_up_bias, L1_ffn_down_weights, L1_ffn_W_con, L1_ffn_b_con, L1_ffn_down_bias)
    return x

_drawn_inputs = setup_inputs


def setup_inputs(seed=0):
    import zlib

    import numpy as np

    out = dict(_drawn_inputs(seed))
    spreads = {'L1_attn_D': (1.0, 0.6),
     'L1_ffn_b_exp': (0.0, 0.1),
     'L1_ffn_up_bias': (0.0, 0.1),
     'L1_ffn_b_con': (0.0, 2.0),
     'L1_ffn_down_bias': (0.0, 2.0)}
    factors = {'L0_attn_Wq_down': 8.0,
     'L0_attn_Wk_down': 8.0,
     'L0_attn_Wv_down': 8.0,
     'L0_attn_Wq_up_c': 8.0,
     'L0_attn_Wq_up_e': 8.0,
     'L0_attn_Wk_up_c': 8.0,
     'L0_attn_Wk_up_e': 8.0,
     'L0_attn_Wv_up': 8.0,
     'L0_attn_Wc': 8.0,
     'L0_ffn_Win': 3.371,
     'L0_ffn_bin_': 8.0,
     'L0_ffn_W1': 3.329,
     'L0_ffn_bout': 3.2,
     'L1_attn_conv_b': 8.0,
     'L1_attn_A_log': 7.531,
     'L1_attn_W_x': 3.621,
     'L1_attn_W_dt': 8.0,
     'L1_attn_b_dt': 8.0}
    for name, (base, spread) in spreads.items():
        noise = np.random.default_rng([zlib.crc32(name.encode()), seed]).standard_normal(out[name].shape)
        drawn = base * np.exp(spread * noise) if base else spread * noise
        out[name] = jnp.asarray(drawn.astype(out[name].dtype))
    for name, factor in factors.items():
        out[name] = (out[name] * factor).astype(out[name].dtype)
    return out
```

```python
from contextlib import ExitStack

import concourse.bass as bass
from concourse import mybir

P = 128
ALU = mybir.AluOpType
ACT = mybir.ActivationFunctionType
F32 = mybir.dt.float32
BF16 = mybir.dt.bfloat16
AX_X = mybir.AxisListType.X

MASKED = -1e30
LN_EPS = 1e-5
HALF = 512

OWN_STEPS = {"dve": 50, "act": 4, "pool": 6}


class Count:

    def __init__(self, sem, per, unit=1, start=0):
        self.sem, self.per, self.unit, self.start, self.made = sem, per, unit, start, 0

    def step(self, ins):
        self.made += 1
        ins.then_inc(self.sem, self.unit)

    def at(self, b, n):
        return b * (self.per * self.unit) + n * self.unit + self.start


def adaln_kernel(nc, t):
    B, T, C = t["L0_attn_x"].shape
    H, L, DH, DE = 16, 64, 16, 8
    NT, CT, NH = T // P, C // P, T // HALF
    SCALE = float(DH) ** -0.5
    M, J = t["L0_ffn_W1"].shape
    DI, TAPS = t["L1_attn_conv_w"].shape
    R = t["L1_attn_W_dtT"].shape[0]
    S = t["L1_attn_A_log"].shape[0]
    DTL = DI // P
    F = t["L1_ffn_W_exp"].shape[1]
    FT = F // P
    LEVELS = t["up_w"].shape[0]
    PIECES = 3
    KROWS = 6 * DH
    NEAR = KROWS + PIECES
    HG = 4
    BLOCKS = [(g * HG + h, q, k) for g in range(H // HG) for q in range(NT) for k in range(q + 1) for h in range(HG)]
    PER_CHUNK = 8
    CHUNKS = len(BLOCKS) // PER_CHUNK
    SPARTS = [(h, q, a, min(a + HALF, (q + 1) * P)) for h in range(H) for q in range(NT)
              for a in range(0, (q + 1) * P, HALF)]
    half_ends = [n // PER_CHUNK for n, (h, q, k) in enumerate(BLOCKS) if k == q and q % 4 == 3 and h % HG == HG - 1]
    HRING, HBANKS = 7, 6

    with ExitStack() as ctx:
        def sb(name, shape, dt=F32):
            return ctx.enter_context(nc.sbuf_tensor(name, shape, dt))

        sems = {}

        def ev(name):
            if name not in sems:
                sems[name] = ctx.enter_context(nc.semaphore(name))
            return sems[name]

        counts = []

        def count(name, per, unit=1, start=0):
            counts.append((name, Count(ev(name), per, unit, start)))
            return counts[-1][1]

        PS = ctx.enter_context(nc.psum_tensor("PS", [P, 8, 512], F32))

        ident = sb("ident", [P, P])
        identb = sb("identb", [P, P], BF16)
        mask_qk = sb("mask_qk", [P, P], BF16)
        mask_kq = sb("mask_kq", [P, P], BF16)
        ones = sb("ones", [P, 1])
        cos = sb("cos", [P, T])
        sin = sb("sin", [P, T])
        w_qk = sb("w_qk", [P, CT, 2, 3, H * DE])
        w_v = sb("w_v", [P, CT, C])
        w_c = sb("w_c", [P, CT, C])
        w_in0 = sb("w_in0", [P, CT, M])
        bin2 = sb("bin2", [P, 1])
        w1 = sb("w1", [P, J])
        b1 = sb("b1", [P, J])
        w2 = sb("w2", [P, J])
        diag_w2 = sb("diag_w2", [P, J, P])
        b2 = sb("b2", [P, 1])
        w_out0 = sb("w_out0", [P, C])
        bias_out0 = sb("bias_out0", [P, C])
        w_in1 = sb("w_in1", [P, CT, 2 * DI])
        conv_w = sb("conv_w", [P, DTL, TAPS])
        conv_b = sb("conv_b", [P, DTL])
        a_neg = sb("a_neg", [P, S])
        d_col = sb("d_col", [P, DTL])
        diag_d = sb("diag_d", [P, DTL, P])
        w_x = sb("w_x", [P, DTL, R + 2 * S])
        w_xb = sb("w_xb", [P, DTL, 96])
        w_dt = sb("w_dt", [R, DI])
        b_dt = sb("b_dt", [P, DTL])
        w_out1 = sb("w_out1", [P, DTL, C])
        sel = sb("sel", [96, S, P], BF16)
        w_exp = sb("w_exp", [P, CT, F])
        gelu_b = sb("gelu_b", [P, FT])
        w_con = sb("w_con", [P, FT, C])
        bias_out1 = sb("bias_out1", [P, C])
        mod_col = sb("mod_col", [P, 2, 4, CT, B])
        mod_b = sb("mod_b", [P, 2, 4, CT])
        gates = sb("gates", [P, 4, C])
        bias_g = sb("bias_g", [P, C])
        X = sb("X", [P, NT, C])
        hT = sb("hT", [P, CT, T])
        bn = sb("bn", [P, NT, 6])
        mv = sb("mv", [P, NT, 2])
        spare = sb("spare", [P, 1])
        rstd = sb("rstd", [P, 4, NT])
        slots = sb("slots", [P, H * NT, 2])
        negm = sb("negm", [P, H * NT])
        n_rest = sb("n_rest", [P, P])
        n_pieces = sb("n_pieces", [P, PIECES, P], BF16)
        recip = sb("recip", [P, 2, NT])
        c_t = sb("c_t", [P, NT, S])
        b_st = sb("b_st", [96, T], BF16)

        ARENA = 25600
        arena = sb("arena", [P, ARENA])

        def part(at, cols, dt=F32, rows=P):
            words = cols if dt == F32 else cols // 2
            assert at + words <= ARENA, (at, words)
            v = arena[0:rows, at:at + words]
            return v if dt == F32 else v.bitcast(dt)

        at = 0
        bd = part(at, 3 * 48).rearrange("p (m n) -> p m n", m=3)
        at += 144
        wT = part(at, 3 * 8 * C).rearrange("p (m k c) -> p m k c", m=3, k=8)
        mod_row = part(at, 2 * 6 * C, rows=B).rearrange("p (l n) -> p l n", l=2)
        at += 3 * 8 * C
        cT = part(at, 2 * CT * B).rearrange("p (l k b) -> p l k b", l=2, k=CT)
        at += 2 * CT * B
        wmod = part(at, 2 * CT * 6 * C).rearrange("p (l k n) -> p l k n", l=2, k=CT)
        at += 2 * CT * 6 * C
        bf_w = [part(at + 2048 * i, 4 * (F // 2)).rearrange("p (i j n) -> p i j n", i=2, j=2) for i in range(2)]
        at += 4096
        bf_t = [[part(at + 1024 * (3 * i + j), CT * F // 2).rearrange("p (k n) -> p k n", k=CT)
                 for j in range(3)] for i in range(2)]
        at += 6144
        bexp = part(at, F)
        at += F
        ones_row = part(at, 384, BF16)
        at += 192
        dn_bias = part(at, C)
        up_bias = part(at + C, FT)
        xn = part(0, NT * C).rearrange("p (i c) -> p i c", i=NT)
        q_st = part(0, H * T, BF16).rearrange("p (h t) -> p h t", h=H)
        k_st = part(8192, H * T, BF16).rearrange("p (h t) -> p h t", h=H)
        qk_f = part(8192, 2 * T).rearrange("p (e t) -> p e t", e=2)
        qk_rest = part(8192 + 2048, 2 * T).rearrange("p (e t) -> p e t", e=2)
        pieces = part(8192 + 4096, PIECES * 2 * T, BF16).rearrange("p (n e t) -> p n e t", n=PIECES, e=2)
        rope_t = part(8192 + 4096 + 3072, T)
        V_COLS = NT * H * (DH + 1)
        v_flat = part(16384, V_COLS + 16)
        v_aug = v_flat[:, 0:V_COLS].rearrange("p (i h d) -> p i h d", i=NT, h=H)
        P_AT, P_RING = 16384 + V_COLS + 16, 4
        pT = [part(P_AT + i * PER_CHUNK * P, PER_CHUNK * P) for i in range(P_RING)]
        y_at = part(P_AT + P_RING * PER_CHUNK * P, NT * C).rearrange("p (i c) -> p i c", i=NT)
        oT = [part(P_AT + P_RING * PER_CHUNK * P + NT * C + HALF * i, HALF) for i in range(1)]
        o_rec = recip[:, :, :].rearrange("p a i -> p (a i)").rearrange("p (i h) -> p i h", h=HG)
        w_g = part(8192, FT * C).rearrange("p (k c) -> p k c", k=FT)
        yT = part(0, CT * T).rearrange("p (k t) -> p k t", k=CT)
        s0, g0 = part(0, HALF), part(512, HALF)
        r0 = [part(1024 + HALF * i, HALF) for i in range(4)]
        h_r = [part(T * i, T) for i in range(HRING)]
        bb = [part(T * (HRING + i), T) for i in range(2)]
        xs = part(0, DTL * T).rearrange("p (d t) -> p d t", d=DTL)
        conv_t = [part(4096 + T * i, T) for i in range(2)]
        at = T * (HRING + 2)
        dt_t = part(at, DTL * T).rearrange("p (d t) -> p d t", d=DTL)
        dtx = part(at + DTL * T, DTL * T).rearrange("p (d t) -> p d t", d=DTL)
        y_s = part(at + 2 * DTL * T, NT * DI).rearrange("p (i d) -> p i d", i=NT)
        at += 3 * DTL * T
        a_r = [part(at + i * T, T) for i in range(2)]
        u_r = [part(at + (2 + i) * T, T) for i in range(2)]
        sp_e = [part(4096 + T * (2 + i), T) for i in range(2)]
        sp_l = [part(4096 + T * 4, T), u_r[0]]
        sp_c = [a_r[1], u_r[1]]
        dtr = a_r[0][0:R, :]
        b_p1 = a_r[1][0:96, :].bitcast(BF16)[:, 0:T]
        b_rest = u_r[1][0:96, :]
        z_r = [part(i * DI, DI) for i in range(2)]
        yg = [part((2 + i) * DI, DI) for i in range(2)]
        ygT = [part((4 + i) * DI, DI).rearrange("p (d t) -> p d t", d=DTL) for i in range(2)]
        gl = part(0, FT * T).rearrange("p (f t) -> p f t", f=FT)

        def dram(name, shape, dt=F32):
            return nc.dram_tensor(name, shape, dt, kind="Internal").ap()

        gate_d = dram("gate_d", (4, B, C))
        qk_d = dram("qk_d", (2, PIECES, H, 2 * DE, T), BF16)
        ones_d = dram("ones_d", (P, 384), BF16)
        negm_d = dram("negm_d", (PIECES, H * NT, P), BF16)

        x_loaded = count("x_loaded", 1, 16)
        g_loaded = count("g_loaded", 1, 16)
        x_stored = count("x_stored", 1, 16, start=16)
        mod_b_ready = count("mod_b_ready", 1)
        own = {e: count(f"{e}_own", OWN_STEPS[e]) for e in OWN_STEPS}
        stats_ready = count("stats_ready", 4)
        rsq_ready = count("rsq_ready", 4)
        xn_ready = count("xn_ready", 4 * NT)
        hT_psum = count("hT_psum", 4 * NT)
        hT_ready = count("hT_ready", 4 * CT * NH)
        qk_psum = count("qk_psum", 6)
        qk_c_read = count("qk_c_read", 2)
        qk_er_read = count("qk_er_read", 2)
        v_psum = count("v_psum", NT)
        v_ready = count("v_ready", NT)
        roped = count("roped", 2)
        piece1 = count("piece1", 2)
        rest1 = count("rest1", 2)
        piece2 = count("piece2", 2)
        piece3 = count("piece3", 2)
        pieces_out = count("pieces_out", 4 * PIECES, 16)
        stacks_in = count("stacks_in", 13, 16)
        smax_psum = count("smax_psum", len(SPARTS))
        smax_read = count("smax_read", len(SPARTS))
        negm_ready = count("negm_ready", 1)
        negm_T = count("negm_T", 1)
        negm_split = count("negm_split", 1)
        negm_out = count("negm_out", 1, 16)
        negm_in = count("negm_in", 1, 16)
        s_psum = count("s_psum", CHUNKS)
        p_ready = count("p_ready", CHUNKS)
        pv_done = count("pv_done", CHUNKS)
        oT_ready = count("oT_ready", NH * H // HG)
        o_psum = count("o_psum", NH * H // HG)
        o_read = count("o_read", NH * H // HG)
        yT_psum = count("yT_psum", CT * NH)
        yT_ready = count("yT_ready", CT * NH)
        w_g_ready = count("w_g_ready", 4)
        x_biased = count("x_biased", 2)
        res_psum = count("res_psum", 4 * NT)
        x_added = count("x_added", 4 * NT, start=1)
        s0_psum = count("s0_psum", 1)
        s0_ready = count("s0_ready", 1)
        r0_ready = count("r0_ready", J)
        r0_used = count("r0_used", J)
        g0_ready = count("g0_ready", 1)
        xr_psum = count("xr_psum", DTL)
        conv0 = count("conv0", DTL)
        conv_done = count("conv_done", DTL)
        xs_ready = count("xs_ready", DTL)
        xd_psum = count("xd_psum", 2)
        dtr_ready = count("dtr_ready", 1)
        b_split = count("b_split", 1)
        c_psum = count("c_psum", 1)
        dt_psum = count("dt_psum", DTL)
        dt_max = count("dt_max", DTL)
        dt_abs = count("dt_abs", DTL)
        dt_exp = count("dt_exp", DTL)
        dt_ln = count("dt_ln", DTL)
        dt_corr = count("dt_corr", DTL)
        dt_ready = count("dt_ready", DTL)
        dtx_ready = count("dtx_ready", DTL)
        d_psum = count("d_psum", NT)
        d_read = count("d_read", NT)
        bb_psum = count("bb_psum", S)
        bb_ready = count("bb_ready", S)
        a_ready = count("a_ready", S * DTL)
        u_ready = count("u_ready", S * DTL)
        h_ready = count("h_ready", S * DTL)
        h_T = count("h_T", S * NT)
        y_added = count("y_added", S * NT)
        z_psum = count("z_psum", NT)
        z_ready = count("z_ready", NT)
        yg_ready = count("yg_ready", NT)
        ygT_psum = count("ygT_psum", NT)
        ygT_ready = count("ygT_ready", NT)
        f_psum = count("f_psum", FT * NH)
        f_ready = count("f_ready", FT * NH)

        last_of = {
            "load": [(x_loaded, 1), (mod_b_ready, 1)],
            "ln_a0": [(hT_ready, CT * NH)],
            "qkv": [(piece3, 2), (v_ready, NT)],
            "max": [(negm_split, 1)],
            "attend": [(o_read, NH * H // HG)],
            "project": [(x_added, NT)],
            "ln_b0": [(hT_ready, 2 * CT * NH)],
            "ffn0": [(x_added, 2 * NT)],
            "ln_a1": [(hT_ready, 3 * CT * NH)],
            "xproj": [(d_read, NT), (dtx_ready, DTL)],
            "scan": [(y_added, S * NT)],
            "out": [(x_added, 3 * NT)],
            "ln_b1": [(hT_ready, 4 * CT * NH)],
            "ffn1": [(x_added, 0)],
        }

        def begins(eng, b, name):
            names = list(last_of)
            for c, n in last_of[names[names.index(name) - 1]]:
                eng.wait_ge(c.sem, c.at(b, n))

        def own_step(engine, eng, b, ins):
            o = own[engine]
            o.step(ins)
            eng.wait_ge(o.sem, o.at(b, o.made))

        block = ctx.enter_context(nc.Block())

        @block.sync
        def _(sp):
            loads = [0]

            def pre(dst, src):
                loads[0] += 1
                sp.dma_start(dst, src).then_inc(ev("pre_loads"), 16)

            sp.wait_ge(ev("cleared"), 2)
            for m, n in enumerate("qkv"):
                pre(wT[:, m], t[f"W{n}T"].rearrange("(k p) c -> p k c", p=P))
            for h in range(2):
                rows = slice(L * h, L * h + L)
                for m, n in enumerate("qk"):
                    pre(bd[rows, m, DE * h:DE * h + DE], t[f"L0_attn_W{n}_up_c"])
                    pre(bd[rows, m, 16 + DE * h:16 + DE * h + DE], t[f"L0_attn_W{n}_up_e"])
                pre(bd[rows, 2, DH * h:DH * h + DH], t["L0_attn_Wv_up"])
                pre(bin2[rows, :], t["L0_ffn_bin_"].rearrange("(m o) -> m o", o=1))
                pre(b2[rows, :], t["L0_ffn_b2"].rearrange("(m o) -> m o", o=1))
                pre(w1[rows, :], t["L0_ffn_W1"])
                pre(b1[rows, :], t["L0_ffn_b1"])
                pre(w2[rows, :], t["L0_ffn_W2"])
                pre(w_out0[rows, :], t["L0_ffn_Wout"])
            for l in range(2):
                pre(cT[:, l], t[f"L{l}_cT"].rearrange("(k p) b -> p k b", p=P))
                pre(wmod[:, l], t[f"L{l}_wmod"].rearrange("(k p) n -> p k n", p=P))
            pre(cos[:, :], t["cos"])
            pre(sin[:, :], t["sin"])
            pre(w_c[:, :, :], t["L0_attn_Wc"].rearrange("(k p) n -> p k n", p=P))
            pre(w_in0[:, :, :], t["L0_ffn_Win"].rearrange("(k p) n -> p k n", p=P))
            pre(bias_out0[:, :], t["L0_ffn_bout"].partition_broadcast(P))
            pre(w_in1[:, :, :], t["L1_attn_W_inT"].rearrange("(k p) n -> p k n", p=P))
            pre(conv_w[:, :, :], t["L1_attn_conv_w"].rearrange("(k p) n -> p k n", p=P))
            pre(conv_b[:, :], t["conv_b"])
            pre(b_dt[:, :], t["b_dt"])
            pre(d_col[:, :], t["D"])
            pre(a_neg[:, :], t["L1_attn_A_log"].partition_broadcast(P))
            w_xT = t["L1_attn_W_xT"].rearrange("(k p) n -> p k n", p=P)
            pre(w_x[:, :, :], w_xT)
            for q in range(PIECES):
                pre(w_xb[:, :, 32 * q:32 * q + S], w_xT[:, :, R:R + S])
            pre(w_dt[:, :], t["L1_attn_W_dtT"])
            pre(w_out1[:, :, :], t["L1_attn_W_outT"].rearrange("(k p) n -> p k n", p=P))
            pre(w_exp[:, :, :], t["L1_ffn_W_exp"].rearrange("(k p) n -> p k n", p=P))
            pre(bexp, t["L1_ffn_b_exp"].partition_broadcast(P))
            pre(w_con[:, :, :].rearrange("p f c -> p (f c)").rearrange("p (k n) -> p k n", k=CT),
                t["L1_ffn_W_conT"].rearrange("(k p) n -> p k n", p=P))
            pre(up_bias, t["up_bias"])
            pre(bias_out1[:, :], t["L1_ffn_b_con"].partition_broadcast(P))
            pre(dn_bias, t["L1_ffn_down_bias"].partition_broadcast(P))
            assert loads[0] == N_LOADS, loads[0]
            sp.wait_ge(ev("ones_row_set"), 1)
            sp.dma_start(ones_d, ones_row).then_inc(ev("ones_out"), 16)
            for i in range(LEVELS):
                for side, (name, level) in enumerate((("up", i), ("down", LEVELS - 1 - i))):
                    if i:
                        sp.wait_ge(ev(f"{name}_level"), i)
                    sp.dma_start(bf_w[side].rearrange("p i j n -> p (i j n)"),
                                 t[f"{name}_w"][level].partition_broadcast(P)).then_inc(ev(f"{name}_weights"), 16)
            sp.wait_ge(ev("mod_rows"), 1)
            for g in range(4):
                l, kind = g // 2, (2, 5)[g % 2]
                sp.dma_start(gate_d[g], mod_row[:, l, kind * C:kind * C + C]).then_inc(ev("gates_out"), 16)
            sp.wait_ge(ev("ones_out"), 16)

            with sp.Fori(0, B, 1) as b:
                value = {(c.sem.name, n): sp.snap(c.at(b, n)) for c, n in (
                    (piece3, 1), (piece3, 2), (pieces_out, 4 * PIECES), (negm_split, 1), (negm_out, 1))}

                def wait(c, n):
                    sp.wait_ge(c.sem, value[c.sem.name, n])

                for m in range(2):
                    wait(piece3, m + 1)
                    for n in range(PIECES):
                        for e in range(2):
                            pieces_out.step(sp.dma_start(qk_d[m][n][:, DE * e:DE * e + DE, :], pieces[:, n, e, :]))
                wait(pieces_out, 4 * PIECES)
                for (r0_, r1_), first in (((0, 3), 0), ((3, 5), 1), ((5, 6), 2)):
                    n = r1_ - r0_
                    one = qk_d[0][first].rearrange("h r t -> r h t")
                    for j in range(n):
                        stacks_in.step(sp.dma_start(q_st[DH * (r0_ + j):DH * (r0_ + j + 1)], one))
                row = 0
                for n in (3, 2, 1):
                    for j in range(n):
                        stacks_in.step(sp.dma_start(k_st[DH * row:DH * row + DH],
                                                    qk_d[1][j].rearrange("h r t -> r h t")))
                        row += 1
                stacks_in.step(sp.dma_start(k_st[KROWS:NEAR].rearrange("n h t -> n (h t)"),
                                            ones_d.rearrange("a c -> (a c)").rearrange("(n x) -> n x", n=PIECES)))
                wait(negm_split, 1)
                negm_out.step(sp.dma_start(negm_d.rearrange("n g q -> g n q"), n_pieces[:, :, :]))
                wait(negm_out, 1)
                negm_in.step(sp.dma_start(q_st[KROWS:NEAR].rearrange("n h t -> n (h t)"),
                                          negm_d.rearrange("n g q -> n (g q)")))

        @block.gpsimd
        def _(pool):
            pool.memset(bd.rearrange("p m n -> p (m n)"), 0.0).then_inc(ev("cleared"), 1)
            pool.memset(w_xb[:, :, :], 0.0).then_inc(ev("cleared"), 1)
            pool.memset(ident[:, :], 0.0).then_inc(ev("made"), 1)
            pool.memset(mask_qk[:, :], 0.0).then_inc(ev("made"), 1)
            pool.memset(mask_kq[:, :], 0.0).then_inc(ev("made"), 1)
            pool.memset(sel[:, :, :], 0.0).then_inc(ev("made"), 1)
            pool.memset(ones[:, :], 1.0).then_inc(ev("made"), 1)
            pool.memset(slots[:, :, :], MASKED).then_inc(ev("made"), 1)
            pool.memset(ones_row, 1.0).then_inc(ev("ones_row_set"), 1)
            pool.wait_ge(ev("made"), 6)
            pool.affine_select(out=ident[:, :], in_=ident[:, :], compare_op=ALU.not_equal, fill=1.0, base=0,
                               pattern=[[-1, P]], channel_multiplier=1).then_inc(ev("made"), 1)
            pool.affine_select(out=mask_qk[:, :], in_=mask_qk[:, :], compare_op=ALU.is_ge, fill=MASKED, base=0,
                               pattern=[[-1, P]], channel_multiplier=1).then_inc(ev("made"), 1)
            pool.affine_select(out=mask_kq[:, :], in_=mask_kq[:, :], compare_op=ALU.is_ge, fill=MASKED, base=0,
                               pattern=[[1, P]], channel_multiplier=-1).then_inc(ev("made"), 1)
            for q in range(PIECES):
                pool.affine_select(out=sel[:, :, :], in_=sel[:, :, :], compare_op=ALU.not_equal, fill=1.0,
                                   base=-32 * q, pattern=[[-1, S], [0, P]],
                                   channel_multiplier=1).then_inc(ev("made"), 1)
                pool.wait_ge(ev("made"), 10 + q)
            pool.tensor_copy(identb[:, :], ident[:, :]).then_inc(ev("made"), 1)
            pool.wait_ge(ev("pre_loads"), 16 * N_LOADS)
            pool.tensor_tensor(bias_out1[:, :], bias_out1[:, :], dn_bias, ALU.add).then_inc(ev("made"), 1)
            steps = [0]

            def low(ins):
                steps[0] += 1
                ins.then_inc(ev("low"), 1)
                pool.wait_ge(ev("low"), steps[0])

            D = w_con[:, :, :].rearrange("p f c -> p (f c)")
            for i in range(LEVELS):
                s = 2 ** (LEVELS - 1 - i)
                pool.wait_ge(ev("down_weights"), 16 * (i + 1))
                last = butterfly_level(pool, D, CT, s, bf_w[1], bf_t[1], True, low)
                last.then_inc(ev("down_level"), 1)
                pool.wait_ge(ev("down_level"), i + 1)

            with pool.Fori(0, B, 1) as b:
                pool.wait_ge(g_loaded.sem, g_loaded.at(b, 1))
                begins(pool, b, "project")
                ins = pool.tensor_tensor(w_g[:, 0:CT, :], w_c[:, :, :],
                                         gates[:, 0:1, :].broadcast_to([P, CT, C]), ALU.mult)
                w_g_ready.step(ins)
                pool.wait_ge(w_g_ready.sem, w_g_ready.at(b, 1))

                begins(pool, b, "ffn0")
                w_g_ready.step(pool.tensor_tensor(w_g[:, 0, :], w_out0[:, :], gates[:, 1, :], ALU.mult))
                own_step("pool", pool, b, pool.tensor_tensor(bias_g[:, :], bias_out0[:, :], gates[:, 1, :], ALU.mult))
                x_biased.step(pool.tensor_tensor(X[:, :, :], X[:, :, :],
                                                 bias_g[:, :].unsqueeze(1).broadcast_to([P, NT, C]), ALU.add))
                pool.wait_ge(x_biased.sem, x_biased.at(b, 1))

                begins(pool, b, "xproj")
                for d in range(DTL):
                    pool.wait_ge(dt_corr.sem, dt_corr.at(b, d + 1))
                    pool.wait_ge(dt_ln.sem, dt_ln.at(b, d + 1))
                    own_step("pool", pool, b, pool.tensor_tensor(sp_l[d % 2], sp_l[d % 2], sp_c[d % 2], ALU.add))
                    pool.wait_ge(dt_max.sem, dt_max.at(b, d + 1))
                    ins = pool.tensor_tensor(dt_t[:, d], dt_t[:, d], sp_l[d % 2], ALU.add)
                    dt_ready.step(ins)
                    pool.wait_ge(dt_ready.sem, dt_ready.at(b, d + 1))

                begins(pool, b, "scan")
                for s in range(S):
                    pool.wait_ge(bb_ready.sem, bb_ready.at(b, s + 1))
                    for d in range(DTL):
                        n = s * DTL + d
                        if n >= 2:
                            pool.wait_ge(h_ready.sem, h_ready.at(b, n - 1))
                        u_ready.step(pool.tensor_tensor(u_r[n % 2], dtx[:, d], bb[s % 2], ALU.mult))

                begins(pool, b, "out")
                w_g_ready.step(pool.tensor_tensor(w_g[:, 0:DTL, :], w_out1[:, :, :],
                                                  gates[:, 2:3, :].broadcast_to([P, DTL, C]), ALU.mult))

                begins(pool, b, "ffn1")
                w_g_ready.step(pool.tensor_tensor(w_g[:, :, :], w_con[:, :, :],
                                                  gates[:, 3:4, :].broadcast_to([P, FT, C]), ALU.mult))
                own_step("pool", pool, b, pool.tensor_tensor(bias_g[:, :], bias_out1[:, :], gates[:, 3, :], ALU.mult))
                x_biased.step(pool.tensor_tensor(X[:, :, :], X[:, :, :],
                                                 bias_g[:, :].unsqueeze(1).broadcast_to([P, NT, C]), ALU.add))
                pool.wait_ge(x_biased.sem, x_biased.at(b, 2))

        @block.scalar
        def _(act):
            A = nc.scalar.activation
            act.sem_inc(x_stored.sem, x_stored.start)
            act.sem_inc(x_added.sem, x_added.start)
            act.wait_ge(ev("pre_loads"), 16 * N_LOADS)
            A(cT, cT, ACT.Silu).then_inc(ev("c_silu"), 1)
            A(a_neg[:, :], a_neg[:, :], ACT.Exp).then_inc(ev("a_exp"), 1)
            act.wait_ge(ev("a_exp"), 1)
            A(a_neg[:, :], a_neg[:, :], ACT.Copy, scale=-1.0).then_inc(ev("a_exp"), 1)
            act.wait_ge(ev("mod_psum"), 2)
            for l in range(2):
                for n in range(3):
                    last = A(mod_row[:, l, n * 512:n * 512 + 512], PS[0:B, 3 * l + n, :], ACT.Copy)
            last.then_inc(ev("mod_copied"), 1)
            act.wait_ge(ev("a_exp"), 2)
            act.wait_ge(ev("gates_out"), 64)

            with act.Fori(0, B, 1) as b:
                act.wait_ge(x_stored.sem, x_stored.at(b, 0))
                begins(act, b, "load")
                x_loaded.step(act.dma_start(X[:, :, :], t["L0_attn_x"][b].rearrange("(i p) c -> p i c", p=P)))
                g_loaded.step(act.dma_start(gates[:, :, :], gate_d[:, b].partition_broadcast(P)))

                def ln(n, name):
                    l, kind = n // 2, (n % 2) * 2
                    begins(act, b, name)
                    act.wait_ge(stats_ready.sem, stats_ready.at(b, n + 1))
                    own_step("act", act, b, A(rstd[:, 1], rstd[:, 0], ACT.Ln))
                    rsq_ready.step(A(rstd[:, 2], rstd[:, 1], ACT.Exp, scale=-0.5))
                    for g in range(NH):
                        act.wait_ge(hT_psum.sem, hT_psum.at(b, n * NT + (g + 1) * NT // NH))
                        for k in range(CT):
                            ins = A(hT[:, k, g * HALF:(g + 1) * HALF], PS[:, 2 * k + g, :], ACT.Identity,
                                    bias=mod_b[:, l, kind + 1, k:k + 1], scale=mod_b[:, l, kind, k:k + 1])
                            hT_ready.step(ins)
                    act.wait_ge(hT_ready.sem, hT_ready.at(b, (n + 1) * CT * NH))

                ln(0, "ln_a0")

                begins(act, b, "qkv")
                for m in range(2):
                    act.wait_ge(qk_psum.sem, qk_psum.at(b, 3 * m + 1))
                    if m:
                        act.wait_ge(piece3.sem, piece3.at(b, 1))
                    qk_c_read.step(A(qk_f[:, 0, :], PS[:, (0, 6)[m]:(0, 6)[m] + 2, :].rearrange("p a n -> p (a n)"), ACT.Copy))
                    act.wait_ge(roped.sem, roped.at(b, m + 1))
                    act.wait_ge(qk_c_read.sem, qk_c_read.at(b, m + 1))
                    if m:
                        act.wait_ge(pieces_out.sem, pieces_out.at(b, 2 * PIECES))
                    piece1.step(A(pieces[:, 0], qk_f, ACT.Copy))
                    act.wait_ge(rest1.sem, rest1.at(b, m + 1))
                    piece2.step(A(pieces[:, 1], qk_rest, ACT.Copy))
                for i in range(NT):
                    act.wait_ge(v_psum.sem, v_psum.at(b, i + 1))
                    ins = A(v_aug[:, i, :, 0:DH], PS[:, 4 + i % 4, 0:C].rearrange("p (h d) -> p h d", h=H), ACT.Copy)
                    v_ready.step(ins)
                act.wait_ge(v_ready.sem, v_ready.at(b, NT))

                begins(act, b, "attend")
                for g in range(CHUNKS):
                    act.wait_ge(s_psum.sem, s_psum.at(b, g + 1))
                    if g >= P_RING:
                        act.wait_ge(pv_done.sem, pv_done.at(b, g - P_RING + 1))
                    ins = A(pT[g % P_RING], PS[:, 2 * (g % 2):2 * (g % 2) + 2, :].rearrange("p a n -> p (a n)"),
                            ACT.Exp, scale=SCALE)
                    p_ready.step(ins)
                act.wait_ge(p_ready.sem, p_ready.at(b, CHUNKS))

                begins(act, b, "project")
                for g in range(NH):
                    for k in range(CT):
                        act.wait_ge(yT_psum.sem, yT_psum.at(b, g * CT + k + 1))
                        yT_ready.step(A(yT[:, k, g * HALF:(g + 1) * HALF], PS[:, 2 * k + g, :], ACT.Copy))
                act.wait_ge(yT_ready.sem, yT_ready.at(b, CT * NH))

                ln(1, "ln_b0")

                begins(act, b, "ffn0")
                act.wait_ge(s0_psum.sem, s0_psum.at(b, 1))
                s0_ready.step(A(s0, PS[:, 0, :], ACT.Identity, bias=bin2[:, 0:1]))
                act.wait_ge(s0_ready.sem, s0_ready.at(b, 1))
                for j in range(J):
                    if j >= 4:
                        act.wait_ge(r0_used.sem, r0_used.at(b, j - 3))
                    r0_ready.step(A(r0[j % 4], s0, ACT.Relu, bias=b1[:, j:j + 1], scale=w1[:, j:j + 1]))
                act.wait_ge(r0_used.sem, r0_used.at(b, J))
                g0_ready.step(A(g0, PS[:, 1, :], ACT.Identity, bias=b2[:, 0:1]))
                act.wait_ge(g0_ready.sem, g0_ready.at(b, 1))

                ln(2, "ln_a1")

                begins(act, b, "xproj")

                def conv_start(d):
                    act.wait_ge(xr_psum.sem, xr_psum.at(b, d + 1))
                    if d >= 2:
                        act.wait_ge(xs_ready.sem, xs_ready.at(b, d - 1))
                    conv0.step(A(conv_t[d % 2], PS[:, 2 * (d % 2):2 * (d % 2) + 2, :].rearrange("p a n -> p (a n)"),
                                 ACT.Identity, bias=conv_b[:, d:d + 1], scale=conv_w[:, d, TAPS - 1:TAPS]))

                def conv_end(d):
                    act.wait_ge(conv_done.sem, conv_done.at(b, d + 1))
                    xs_ready.step(A(xs[:, d], conv_t[d % 2], ACT.Silu))

                conv_start(0)
                for d in range(1, DTL):
                    conv_start(d)
                    conv_end(d - 1)
                conv_end(DTL - 1)
                act.wait_ge(xd_psum.sem, xd_psum.at(b, 1))
                dtr_ready.step(A(dtr, PS[0:R, 4:6, :].rearrange("p a n -> p (a n)"), ACT.Copy))
                for d in range(DTL):
                    psum = PS[:, 2 * (d % 2):2 * (d % 2) + 2, :].rearrange("p a n -> p (a n)")
                    act.wait_ge(dt_psum.sem, dt_psum.at(b, d + 1))
                    if d == 1:
                        act.wait_ge(b_split.sem, b_split.at(b, 1))
                    if d >= 2:
                        act.wait_ge(dt_corr.sem, dt_corr.at(b, d - 1))
                        act.wait_ge(dt_ready.sem, dt_ready.at(b, d - 1))
                    act.wait_ge(dt_max.sem, dt_max.at(b, d + 1))
                    dt_abs.step(A(sp_e[d % 2], psum, ACT.Abs, bias=b_dt[:, d:d + 1]))
                    act.wait_ge(dt_abs.sem, dt_abs.at(b, d + 1))
                    dt_exp.step(A(sp_e[d % 2], sp_e[d % 2], ACT.Exp, scale=-1.0))
                    act.wait_ge(dt_exp.sem, dt_exp.at(b, d + 1))
                    dt_ln.step(A(sp_l[d % 2], sp_e[d % 2], ACT.Ln, bias=1.0))
                for i in range(NT):
                    act.wait_ge(d_psum.sem, d_psum.at(b, i + 1))
                    d_read.step(A(y_s[:, i], PS[:, 5 + i % 3, :], ACT.Copy))
                act.wait_ge(d_read.sem, d_read.at(b, NT))

                begins(act, b, "scan")

                def bb_copy(s):
                    act.wait_ge(bb_psum.sem, bb_psum.at(b, s + 1))
                    if s >= 2:
                        act.wait_ge(u_ready.sem, u_ready.at(b, (s - 1) * DTL))
                    bb_ready.step(A(bb[s % 2], PS[:, 6:8, :].rearrange("p a n -> p (a n)"), ACT.Copy))

                bb_copy(0)
                for s in range(S):
                    for d in range(DTL):
                        n = s * DTL + d
                        if n >= 2:
                            act.wait_ge(h_ready.sem, h_ready.at(b, n - 1))
                        a_ready.step(A(a_r[n % 2], dt_t[:, d], ACT.Exp, scale=a_neg[:, s:s + 1]))
                        if d == 1 and s + 1 < S:
                            bb_copy(s + 1)
                act.wait_ge(a_ready.sem, a_ready.at(b, S * DTL))

                begins(act, b, "out")
                for i in range(NT + 1):
                    if i < NT:
                        act.wait_ge(z_psum.sem, z_psum.at(b, i + 1))
                        if i >= 2:
                            act.wait_ge(yg_ready.sem, yg_ready.at(b, i - 1))
                        z_ready.step(A(z_r[i % 2], PS[:, i % 2, :], ACT.Silu))
                    if i >= 1:
                        j = i - 1
                        act.wait_ge(ygT_psum.sem, ygT_psum.at(b, j + 1))
                        if j >= 2:
                            act.wait_ge(res_psum.sem, res_psum.at(b, 2 * NT + j - 1))
                        ygT_ready.step(A(ygT[j % 2].rearrange("p d t -> p (d t)"), PS[:, 2 + j % 2, :], ACT.Copy))
                act.wait_ge(ygT_ready.sem, ygT_ready.at(b, NT))

                ln(3, "ln_b1")

                begins(act, b, "ffn1")
                for g in range(NH):
                    for f in range(FT):
                        n = g * FT + f
                        act.wait_ge(f_psum.sem, f_psum.at(b, n + 1))
                        f_ready.step(A(gl[:, f, g * HALF:(g + 1) * HALF], PS[:, n % 4, :], ACT.Gelu,
                                       bias=gelu_b[:, f:f + 1]))
                act.wait_ge(x_added.sem, x_added.at(b, 4 * NT))
                x_stored.step(act.dma_start(t["out"][b].rearrange("(i p) c -> p i c", p=P), X[:, :, :]))
            act.wait_ge(x_stored.sem, x_stored.at(B, 0))

        @block.vector
        def _(dve):
            V = nc.vector
            steps = [0]

            def up(ins):
                steps[0] += 1
                ins.then_inc(ev("up"), 1)
                dve.wait_ge(ev("up"), steps[0])

            dve.wait_ge(ev("pre_loads"), 16 * N_LOADS)
            for m in range(2):
                e = bd[:, m, 16:32].rearrange("p (n two) -> p n two", two=2)
                r = bd[:, m, 32:48].rearrange("p (n two) -> p n two", two=2)
                V.tensor_scalar(r[:, :, 0], e[:, :, 1], -1.0, None, ALU.mult).then_inc(ev("bd_ready"), 1)
                V.tensor_copy(r[:, :, 1], e[:, :, 0]).then_inc(ev("bd_ready"), 1)
            dve.wait_ge(ev("made"), 14)
            for j in range(J):
                V.tensor_scalar(diag_w2[:, j], ident[:, :], w2[:, j:j + 1], None, ALU.mult)
            for d in range(DTL):
                up(V.tensor_scalar(diag_d[:, d], ident[:, :], d_col[:, d:d + 1], None, ALU.mult))
            dve.wait_ge(ev("fold_psum"), 1)
            for k in range(CT):
                for m in range(2):
                    src = PS[:, 2 * m + k, 0:384].rearrange("p (a n j) -> p a n j", a=8, n=3)
                    for n in range(3):
                        V.tensor_copy(w_qk[:, k, m, n, :].rearrange("p (a j) -> p a j", a=8), src[:, :, n, :])
                last = V.tensor_copy(w_v[:, k, :], PS[:, 4 + k, 0:C])
            last.then_inc(ev("folded"), 1)
            dve.wait_ge(ev("mod_copied"), 1)
            for l in range(2):
                for kind in (2, 5):
                    g = mod_row[:, l, kind * C:kind * C + C]
                    sign, size = bf_t[0][0][0:B, 0, 0:C], bf_t[0][1][0:B, 0, 0:C]
                    up(V.tensor_scalar(sign, g, 0.0, 2.0, ALU.is_ge, ALU.mult))
                    up(V.scalar_tensor_tensor(out=size, in0=g, scalar=-1.0, in1=g, op0=ALU.mult, op1=ALU.max))
                    up(V.tensor_scalar(size, size, 0.25, None, ALU.max))
                    up(V.scalar_tensor_tensor(out=g, in0=sign, scalar=1.0, in1=size, op0=ALU.subtract, op1=ALU.mult))
            V.memset(recip[:, 0, 0:1], 0.0).then_inc(ev("mod_rows"), 1)
            dve.wait_ge(ev("mod_T"), 1)
            cols = mod_col[:, :, :, :, :].rearrange("p l n k b -> p (l n k b)").rearrange("p (a two x) -> p a two x", two=2, x=CT * B)
            src = PS[:, 6, 0:2 * 4 * CT * B].rearrange("p (a two x) -> p a two x", two=2, x=CT * B)
            V.tensor_scalar(cols[:, :, 0, :], src[:, :, 0, :], 1.0, None, ALU.add)
            V.tensor_copy(cols[:, :, 1, :], src[:, :, 1, :]).then_inc(ev("mod_ready"), 1)
            U = w_exp[:, :, :].rearrange("p k n -> p (k n)")
            for i in range(LEVELS):
                dve.wait_ge(ev("up_weights"), 16 * (i + 1))
                up(butterfly_level(dve, U, CT, 2 ** i, bf_w[0], bf_t[0], False, up))
                butterfly_level(dve, bexp, 1, 2 ** i, bf_w[0], bf_t[0], False, up).then_inc(ev("up_level"), 1)
                dve.wait_ge(ev("up_level"), i + 1)
            dve.wait_ge(ev("down_T"), 1)
            V.tensor_copy(w_con[:, :, :].rearrange("p f c -> p (f c)"), PS[:, 0:4, :].rearrange("p a n -> p (a n)"))
            V.tensor_tensor(gelu_b[:, :], PS[:, 4, 0:FT], up_bias, ALU.add).then_inc(ev("bf_ready"), 1)
            dve.wait_ge(ev("bf_ready"), 1)
            dve.wait_ge(ev("mod_ready"), 1)

            with dve.Fori(0, B, 1) as b:
                def wait(c, n):
                    dve.wait_ge(c.sem, c.at(b, n))

                def own_(ins):
                    own_step("dve", dve, b, ins)

                begins(dve, b, "load")
                mod_b_ready.step(V.tensor_copy(mod_b[:, :, :, :].rearrange("p l n k -> p (l n k)"),
                                               mod_col[:, :, :, :, bass.ds(b, 1)].rearrange("p l n k b -> p (l n k b)")))
                wait(x_loaded, 1)

                def ln(n, name):
                    begins(dve, b, name)
                    for i in range(NT):
                        last = V.bn_stats(bn[:, i], X[:, i])
                    own_(last)
                    V.memset(spare[:, :], 0.0)
                    for i in range(NT):
                        last = V.bn_aggr(mv[:, i], bn[:, i])
                    own_(last)
                    var = rstd[:, 0]
                    stats_ready.step(V.tensor_scalar(var, mv[:, :, 1], LN_EPS, None, ALU.add))
                    wait(rsq_ready, n + 1)
                    r, y = rstd[:, 2], rstd[:, 3]
                    own_(V.tensor_tensor(y, r, r, ALU.mult))
                    own_(V.tensor_tensor(y, y, var, ALU.mult))
                    own_(V.tensor_scalar(y, y, -0.5, 1.5, ALU.mult, ALU.add))
                    own_(V.tensor_tensor(r, r, y, ALU.mult))
                    for i in range(NT):
                        xn_ready.step(V.tensor_scalar(xn[:, i], X[:, i], mv[:, i, 0:1], r[:, i:i + 1],
                                                      ALU.subtract, ALU.mult))
                    wait(xn_ready, (n + 1) * NT)

                ln(0, "ln_a0")

                begins(dve, b, "qkv")
                v_one = v_aug[:, :, :, DH:DH + 1].rearrange("p i h o -> p (i h) o")
                V.memset(v_one, 1.0)
                V.memset(v_flat[:, V_COLS:V_COLS + 16], 0.0)
                for m in range(2):
                    e = PS[:, (2, 0)[m]:(2, 0)[m] + 2, :].rearrange("p a n -> p (a n)")
                    r = PS[:, (4, 2)[m]:(4, 2)[m] + 2, :].rearrange("p a n -> p (a n)")
                    wait(qk_psum, 3 * m + 2)
                    V.tensor_tensor(qk_f[:, 1, :], e, cos[:, :], ALU.mult)
                    wait(qk_psum, 3 * m + 3)
                    ins = V.tensor_tensor(rope_t, r, sin[:, :], ALU.mult)
                    qk_er_read.step(ins)
                    wait(qk_er_read, m + 1)
                    roped.step(V.tensor_tensor(qk_f[:, 1, :], qk_f[:, 1, :], rope_t, ALU.add))
                    wait(roped, m + 1)
                    wait(piece1, m + 1)
                    rest1.step(V.tensor_tensor(qk_rest, qk_f, pieces[:, 0], ALU.subtract))
                    wait(rest1, m + 1)
                    wait(piece2, m + 1)
                    piece3.step(V.tensor_tensor(pieces[:, 2], qk_rest, pieces[:, 1], ALU.subtract))
                wait(piece3, 2)

                begins(dve, b, "max")
                for n, (h, q, a, z) in enumerate(SPARTS):
                    wait(smax_psum, n + 1)
                    smax_read.step(V.tensor_reduce(slots[:, h * NT + q, a // HALF:a // HALF + 1],
                                                   PS[:, n % 8, 0:z - a], AX_X, ALU.max))
                wait(smax_read, len(SPARTS))
                negm_ready.step(V.tensor_reduce(negm[:, :], slots[:, :, :], AX_X, ALU.max, negate=True))
                wait(negm_T, 1)
                own_(V.tensor_copy(n_pieces[:, 0], PS[:, 0, 0:P]))
                own_(V.tensor_tensor(n_rest[:, :], PS[:, 0, 0:P], n_pieces[:, 0], ALU.subtract))
                own_(V.tensor_copy(n_pieces[:, 1], n_rest[:, :]))
                negm_split.step(V.tensor_tensor(n_pieces[:, 2], n_rest[:, :], n_pieces[:, 1], ALU.subtract))
                wait(negm_split, 1)

                begins(dve, b, "attend")
                for n in range(NH * H // HG):
                    hg, half = n // NH, n % NH
                    wait(pv_done, half_ends[n] + 1)
                    if n >= 1:
                        wait(o_psum, n)
                    oT_ready.step(V.tensor_copy(oT[0], PS[:, 4 + half, :]))
                    wait(o_psum, n + 1)
                    o = PS[:, 6 + half, :].rearrange("p (i h d) -> p i h d", i=4, h=HG)
                    own_(V.reciprocal(o_rec, o[:, :, :, DH]))
                    for i in range(4):
                        ins = V.tensor_tensor(
                            y_at[:, 4 * half + i, hg * HG * DH:(hg + 1) * HG * DH].rearrange("p (h d) -> p h d", h=HG),
                            o[:, i, :, 0:DH], o_rec[:, i, :].unsqueeze(2).broadcast_to([P, HG, DH]), ALU.mult)
                    o_read.step(ins)

                def add_residual(n, i, bank):
                    wait(res_psum, n * NT + i + 1)
                    x_added.step(V.tensor_tensor(X[:, i], X[:, i], PS[:, bank, 0:C], ALU.add))

                begins(dve, b, "project")
                for i in range(NT):
                    add_residual(0, i, 4 + i % 4)
                wait(x_added, NT)

                ln(1, "ln_b0")

                begins(dve, b, "ffn0")
                wait(x_biased, 1)
                for i in range(NT):
                    add_residual(1, i, 4 + i % 4)
                wait(x_added, 2 * NT)

                ln(2, "ln_a1")

                begins(dve, b, "xproj")
                for d in range(DTL):
                    xr = PS[:, 2 * (d % 2):2 * (d % 2) + 2, :].rearrange("p a n -> p (a n)")
                    wait(conv0, d + 1)
                    for j in range(1, TAPS):
                        ins = V.scalar_tensor_tensor(out=conv_t[d % 2][:, j:T], in0=xr[:, 0:T - j],
                                                     scalar=conv_w[:, d, TAPS - 1 - j:TAPS - j],
                                                     in1=conv_t[d % 2][:, j:T], op0=ALU.mult, op1=ALU.add)
                        if j < TAPS - 1:
                            own_(ins)
                        else:
                            conv_done.step(ins)
                psb = PS[:, 6:8, :].rearrange("p a n -> p (a n)")
                wait(xd_psum, 2)
                own_(V.tensor_copy(b_p1, psb[0:96]))
                V.tensor_copy(b_st[0:32, :], psb[0:32])
                V.tensor_tensor(b_rest[32:64], psb[32:64], b_p1[32:64], ALU.subtract)
                own_(V.tensor_tensor(b_rest[64:96], psb[64:96], b_p1[64:96], ALU.subtract))
                V.tensor_copy(b_st[32:64, :], b_rest[32:64])
                own_(V.tensor_copy(b_p1[64:96], b_rest[64:96]))
                b_split.step(V.tensor_tensor(b_st[64:96, :], b_rest[64:96], b_p1[64:96], ALU.subtract))
                wait(c_psum, 1)
                V.tensor_copy(c_t[:, :, :], PS[:, 4, 0:NT * S].rearrange("p (i s) -> p i s", i=NT))
                wait(b_split, 1)
                for d in range(DTL):
                    psum = PS[:, 2 * (d % 2):2 * (d % 2) + 2, :].rearrange("p a n -> p (a n)")
                    e, c = sp_e[d % 2], sp_c[d % 2]
                    wait(dt_psum, d + 1)
                    dt_max.step(V.tensor_scalar(dt_t[:, d], psum, b_dt[:, d:d + 1], 0.0, ALU.add, ALU.max))
                    wait(dt_exp, d + 1)
                    if d >= 2:
                        wait(dt_ready, d - 1)
                    own_(V.tensor_scalar(c, e, 1.0, -1.0, ALU.add, ALU.add))
                    dt_corr.step(V.tensor_tensor(c, e, c, ALU.subtract))
                    if d >= 1:
                        wait(dt_ready, d)
                        dtx_ready.step(V.tensor_tensor(dtx[:, d - 1], dt_t[:, d - 1], xs[:, d - 1], ALU.mult))
                wait(dt_ready, DTL)
                dtx_ready.step(V.tensor_tensor(dtx[:, DTL - 1], dt_t[:, DTL - 1], xs[:, DTL - 1], ALU.mult))
                wait(dtx_ready, DTL)

                begins(dve, b, "scan")

                def add_y(s, i):
                    n = s * NT + i
                    wait(h_T, n + 1)
                    if s:
                        wait(y_added, n - NT + 1)
                    y_added.step(V.scalar_tensor_tensor(out=y_s[:, i], in0=PS[:, n % HBANKS, :],
                                                        scalar=c_t[:, i, s:s + 1], in1=y_s[:, i],
                                                        op0=ALU.mult, op1=ALU.add))

                for s in range(S):
                    for d in range(DTL):
                        n = s * DTL + d
                        wait(a_ready, n + 1)
                        wait(u_ready, n + 1)
                        if n >= HRING:
                            wait(h_T, ((n - HRING) // DTL + 1) * NT)
                        h_ready.step(V.tensor_tensor_scan(h_r[n % HRING], a_r[n % 2], u_r[n % 2], 0.0,
                                                          ALU.mult, ALU.add))
                        if s:
                            for i in range(d * NT // DTL, (d + 1) * NT // DTL):
                                add_y(s - 1, i)
                for i in range(NT):
                    add_y(S - 1, i)
                wait(y_added, S * NT)

                begins(dve, b, "out")
                for i in range(NT + 2):
                    if i < NT:
                        wait(z_ready, i + 1)
                        if i >= 2:
                            wait(ygT_psum, i - 1)
                        yg_ready.step(V.tensor_tensor(yg[i % 2], y_s[:, i], z_r[i % 2], ALU.mult))
                    if i >= 2:
                        add_residual(2, i - 2, 4 + i % 2)
                wait(x_added, 3 * NT)

                ln(3, "ln_b1")

                begins(dve, b, "ffn1")
                wait(x_biased, 2)
                for i in range(NT):
                    add_residual(3, i, 4 + i % 4)
                wait(x_added, 4 * NT)

        @block.tensor
        def _(pe):
            mm, tr = nc.tensor.matmul, nc.tensor.transpose
            pe.wait_ge(ev("pre_loads"), 16 * N_LOADS)
            pe.wait_ge(ev("bd_ready"), 4)
            for k in range(CT):
                for m in range(3):
                    w = 32 if m == 2 else 48
                    for a in range(8):
                        last = mm(PS[:, 4 + k if m == 2 else 2 * m + k, a * w:(a + 1) * w],
                                  wT[:, m, a, k * P:(k + 1) * P], bd[:, m, 0:w], start=True, stop=True)
            last.then_inc(ev("fold_psum"), 1)
            pe.wait_ge(ev("folded"), 1)
            pe.wait_ge(ev("c_silu"), 1)
            for l in range(2):
                for n in range(3):
                    for k in range(CT):
                        last = mm(PS[0:B, 3 * l + n, :], cT[:, l, k, :], wmod[:, l, k, n * 512:(n + 1) * 512],
                                  start=(k == 0), stop=(k == CT - 1))
                last.then_inc(ev("mod_psum"), 1)
            pe.wait_ge(ev("mod_rows"), 1)
            pe.wait_ge(ev("made"), 14)
            for l in range(2):
                for n, kind in enumerate((1, 0, 4, 3)):
                    for k in range(CT):
                        c = kind * C + k * P
                        o = ((l * 4 + n) * CT + k) * B
                        last = tr(PS[:, 6, o:o + B], mod_row[:, l, c:c + P], ident[0:B, 0:B])
            last.then_inc(ev("mod_T"), 1)
            pe.wait_ge(ev("down_level"), LEVELS)
            D = w_con[:, :, :].rearrange("p f c -> p (f c)").rearrange("p (k n) -> p k n", k=CT)
            for f in range(FT):
                for k in range(CT):
                    tr(PS[:, f // 2, (f % 2) * C + k * P:(f % 2) * C + (k + 1) * P],
                       D[:, k, f * P:(f + 1) * P], ident[:, :])
            pe.wait_ge(ev("up_level"), LEVELS)
            for f in range(FT):
                last = mm(PS[:, 4, f:f + 1], bexp[0:1, f * P:(f + 1) * P], ones[0:1, 0:1], start=True, stop=True)
            last.then_inc(ev("down_T"), 1)
            pe.wait_ge(ev("bf_ready"), 1)

            with pe.Fori(0, B, 1) as b:
                def wait(c, n):
                    pe.wait_ge(c.sem, c.at(b, n))

                def ln(n, name):
                    begins(pe, b, name)
                    for i in range(NT):
                        wait(xn_ready, n * NT + i + 1)
                        for k in range(CT):
                            last = tr(PS[:, 2 * k + i // 4, (i % 4) * P:(i % 4 + 1) * P],
                                      xn[:, i, k * P:(k + 1) * P], ident[:, :])
                        hT_psum.step(last)
                    wait(hT_ready, (n + 1) * CT * NH)

                ln(0, "ln_a0")

                begins(pe, b, "qkv")
                for m in range(2):
                    for n in range(3):
                        bank = ((0, 2, 4), (6, 0, 2))[m][n]
                        if m and n == 1:
                            wait(qk_c_read, 1)
                        if m and n == 2:
                            wait(qk_er_read, 1)
                        for g in range(NH):
                            for k in range(CT):
                                last = mm(PS[:, bank + g, :], w_qk[:, k, m, n, :], hT[:, k, g * HALF:(g + 1) * HALF],
                                          start=(k == 0), stop=(k == CT - 1))
                        qk_psum.step(last)
                for i in range(NT):
                    if i == 2:
                        wait(qk_c_read, 2)
                    if i >= 4:
                        wait(v_ready, i - 3)
                    for k in range(CT):
                        last = mm(PS[:, 4 + i % 4, 0:C], hT[:, k, i * P:(i + 1) * P], w_v[:, k, :],
                                  start=(k == 0), stop=(k == CT - 1))
                    v_psum.step(last)
                wait(qk_er_read, 2)

                begins(pe, b, "max")
                wait(v_ready, NT)
                wait(stacks_in, 13)
                for n, (h, q, a, z) in enumerate(SPARTS):
                    if n >= 8:
                        wait(smax_read, n - 7)
                    diag = z == (q + 1) * P
                    last = mm(PS[:, n % 8, 0:z - a], q_st[0:KROWS, h, q * P:(q + 1) * P], k_st[0:KROWS, h, a:z],
                              start=True, stop=not diag)
                    if diag:
                        last = mm(PS[:, n % 8, z - a - P:z - a], identb[:, :], mask_qk[:, :], start=False, stop=True)
                    smax_psum.step(last)
                wait(negm_ready, 1)
                negm_T.step(tr(PS[:, 0, 0:P], negm[:, :], ident[:, :]))
                wait(negm_split, 1)

                begins(pe, b, "attend")
                wait(negm_in, 1)
                done = 0
                LAG = 2

                def scores(g):
                    if g >= 2:
                        wait(p_ready, g - 1)
                    for n in range(PER_CHUNK):
                        h, q, k = BLOCKS[PER_CHUNK * g + n]
                        o = PS[:, 2 * (g % 2) + n // 4, (n % 4) * P:(n % 4 + 1) * P]
                        last = mm(o, k_st[0:NEAR, h, k * P:(k + 1) * P], q_st[0:NEAR, h, q * P:(q + 1) * P],
                                  start=True, stop=k < q)
                        if k == q:
                            last = mm(o, identb[:, :], mask_kq[:, :], start=False, stop=True)
                    s_psum.step(last)

                def turn(n):
                    wait(oT_ready, n + 1)
                    if n >= NH:
                        wait(o_read, n - NH + 1)
                    for i in range(4):
                        last = tr(PS[:, 6 + n % NH, i * P:(i + 1) * P], oT[0][:, i * P:(i + 1) * P], ident[:, :])
                    o_psum.step(last)

                for g in range(CHUNKS + LAG):
                    if g < CHUNKS:
                        scores(g)
                    if g >= LAG + 1 and g - LAG - 1 in half_ends:
                        turn(half_ends.index(g - LAG - 1))
                    if g >= LAG:
                        wait(p_ready, g - LAG + 1)
                        for n in range(PER_CHUNK * (g - LAG), PER_CHUNK * (g - LAG + 1)):
                            h, q, k = BLOCKS[n]
                            hg, r = h // HG, 32 * (h % HG)
                            if hg and k == 0 and q % 4 == 0 and r == 0:
                                wait(oT_ready, NH * (hg - 1) + q // 4 + 1)
                            v = (k * H + h) * (DH + 1)
                            last = mm(PS[r:r + 32, 4 + q // 4, (q % 4) * P:(q % 4 + 1) * P], v_flat[:, v:v + 32],
                                      pT[(n // PER_CHUNK) % P_RING][:, (n % PER_CHUNK) * P:(n % PER_CHUNK + 1) * P],
                                      start=(k == 0), stop=(k == q), tile_position=(0, r))
                        pv_done.step(last)
                turn(NH * H // HG - 1)

                begins(pe, b, "project")
                for g in range(NH):
                    for k in range(CT):
                        for i in range(4):
                            last = tr(PS[:, 2 * k + g, i * P:(i + 1) * P],
                                      y_at[:, 4 * g + i, k * P:(k + 1) * P], ident[:, :])
                        yT_psum.step(last)
                wait(w_g_ready, 1)
                for i in range(NT):
                    wait(yT_ready, CT * (i // 4 + 1))
                    if i >= 4:
                        wait(x_added, i - 3)
                    for k in range(CT):
                        last = mm(PS[:, 4 + i % 4, 0:C], yT[:, k, i * P:(i + 1) * P], w_g[:, k, :],
                                  start=(k == 0), stop=(k == CT - 1))
                    res_psum.step(last)
                wait(x_added, NT)

                ln(1, "ln_b0")

                begins(pe, b, "ffn0")
                for g in range(NH):
                    for k in range(CT):
                        last = mm(PS[M * g:M * g + M, 0, :], w_in0[:, k, :], hT[:, k, g * HALF:(g + 1) * HALF],
                                  start=(k == 0), stop=(k == CT - 1))
                s0_psum.step(last)
                for j in range(J):
                    wait(r0_ready, j + 1)
                    last = mm(PS[:, 1, :], diag_w2[:, j], r0[j % 4], start=(j == 0), stop=(j == J - 1))
                    r0_used.step(last)
                wait(g0_ready, 1)
                wait(w_g_ready, 2)
                for i in range(NT):
                    rows = slice(M * (i // 4), M * (i // 4) + M)
                    if i >= 4:
                        wait(x_added, NT + i - 3)
                    res_psum.step(mm(PS[:, 4 + i % 4, 0:C], g0[rows, (i % 4) * P:(i % 4 + 1) * P], w_g[rows, 0, :],
                                     start=True, stop=True))
                wait(x_added, 2 * NT)

                ln(2, "ln_a1")

                begins(pe, b, "xproj")
                for d in range(DTL):
                    if d >= 2:
                        wait(conv_done, d - 1)
                    for g in range(NH):
                        for k in range(CT):
                            last = mm(PS[:, 2 * (d % 2) + g, :], w_in1[:, k, d * P:(d + 1) * P],
                                      hT[:, k, g * HALF:(g + 1) * HALF], start=(k == 0), stop=(k == CT - 1))
                    xr_psum.step(last)
                wait(xs_ready, DTL)
                for g in range(NH):
                    for d in range(DTL):
                        last = mm(PS[0:R, 4 + g, :], w_x[:, d, 0:R], xs[:, d, g * HALF:(g + 1) * HALF],
                                  start=(d == 0), stop=(d == DTL - 1))
                xd_psum.step(last)
                for g in range(NH):
                    for d in range(DTL):
                        last = mm(PS[0:96, 6 + g, :], w_xb[:, d, :], xs[:, d, g * HALF:(g + 1) * HALF],
                                  start=(d == 0), stop=(d == DTL - 1))
                xd_psum.step(last)
                wait(dtr_ready, 1)
                for i in range(NT):
                    for d in range(DTL):
                        last = mm(PS[:, 4, i * S:(i + 1) * S], xs[:, d, i * P:(i + 1) * P], w_x[:, d, R + S:R + 2 * S],
                                  start=(d == 0), stop=(d == DTL - 1))
                c_psum.step(last)
                for d in range(DTL):
                    if d >= 2:
                        wait(dt_abs, d - 1)
                        wait(dt_max, d - 1)
                    for g in range(NH):
                        last = mm(PS[:, 2 * (d % 2) + g, :], w_dt[:, d * P:(d + 1) * P],
                                  dtr[:, g * HALF:(g + 1) * HALF], start=True, stop=True)
                    dt_psum.step(last)
                wait(b_split, 1)
                for i in range(NT):
                    if i >= 3:
                        wait(d_read, i - 2)
                    for d in range(DTL):
                        last = mm(PS[:, 5 + i % 3, d * P:(d + 1) * P], xs[:, d, i * P:(i + 1) * P], diag_d[:, d],
                                  start=True, stop=True)
                    d_psum.step(last)
                wait(d_read, NT)

                begins(pe, b, "scan")

                def spread_b(s):
                    if s:
                        wait(bb_ready, s)
                    for g in range(NH):
                        last = mm(PS[:, 6 + g, :], sel[:, s], b_st[:, g * HALF:(g + 1) * HALF], start=True, stop=True)
                    bb_psum.step(last)

                spread_b(0)
                for s in range(S):
                    if s + 1 < S:
                        spread_b(s + 1)
                    wait(h_ready, (s + 1) * DTL)
                    for i in range(NT):
                        n = s * NT + i
                        if n >= HBANKS:
                            wait(y_added, n - HBANKS + 1)
                        for d in range(DTL):
                            last = tr(PS[:, n % HBANKS, d * P:(d + 1) * P],
                                      h_r[(s * DTL + d) % HRING][:, i * P:(i + 1) * P], ident[:, :])
                        h_T.step(last)
                wait(y_added, S * NT)

                begins(pe, b, "out")
                wait(w_g_ready, 3)
                for i in range(NT + 2):
                    if i < NT:
                        if i >= 2:
                            wait(z_ready, i - 1)
                        for k in range(CT):
                            last = mm(PS[:, i % 2, :], hT[:, k, i * P:(i + 1) * P], w_in1[:, k, DI:2 * DI],
                                      start=(k == 0), stop=(k == CT - 1))
                        z_psum.step(last)
                    if 1 <= i <= NT:
                        j = i - 1
                        wait(yg_ready, j + 1)
                        if j >= 2:
                            wait(ygT_ready, j - 1)
                        for d in range(DTL):
                            last = tr(PS[:, 2 + j % 2, d * P:(d + 1) * P], yg[j % 2][:, d * P:(d + 1) * P], ident[:, :])
                        ygT_psum.step(last)
                    if i >= 2:
                        j = i - 2
                        wait(ygT_ready, j + 1)
                        if j >= 2:
                            wait(x_added, 2 * NT + j - 1)
                        for d in range(DTL):
                            last = mm(PS[:, 4 + j % 2, 0:C], ygT[j % 2][:, d], w_g[:, d, :],
                                      start=(d == 0), stop=(d == DTL - 1))
                        res_psum.step(last)
                wait(x_added, 3 * NT)

                ln(3, "ln_b1")

                begins(pe, b, "ffn1")
                for g in range(NH):
                    for f in range(FT):
                        n = g * FT + f
                        if n >= 4:
                            wait(f_ready, n - 3)
                        for k in range(CT):
                            last = mm(PS[:, n % 4, :], w_exp[:, k, f * P:(f + 1) * P], hT[:, k, g * HALF:(g + 1) * HALF],
                                      start=(k == 0), stop=(k == CT - 1))
                        f_psum.step(last)
                wait(w_g_ready, 4)
                for i in range(NT):
                    wait(f_ready, FT * (i // 4 + 1))
                    if i >= 4:
                        wait(x_added, 3 * NT + i - 3)
                    for f in range(FT):
                        last = mm(PS[:, 4 + i % 4, 0:C], gl[:, f, i * P:(i + 1) * P], w_g[:, f, :],
                                  start=(f == 0), stop=(f == FT - 1))
                    res_psum.step(last)
                wait(x_added, 4 * NT)

        wrong = {n: c.made for n, c in counts if c.made != c.per}
        assert not wrong, wrong


def butterfly_level(eng, x, k, s, w, tmp, transposed, step):
    n = x.shape[1] // k
    v = x.rearrange("p (a two s) -> p a two s", two=2, s=s)
    a, b = v[:, :, 0, :], v[:, :, 1, :]
    na = n // (2 * s)

    def weight(i, j):
        i, j = (j, i) if transposed else (i, j)
        return w[:, i, j, :].rearrange("p (a s) -> p a s", s=s)

    def tile(j):
        return tmp[j].rearrange("p k n -> p (k n)")[:, 0:k * n // 2].rearrange("p (a s) -> p a s", s=s)

    def times(dst, src, wt):
        for c in range(k):
            r = slice(c * na, (c + 1) * na)
            ins = eng.tensor_tensor(dst[:, r, :], src[:, r, :], wt, ALU.mult)
            if c < k - 1:
                step(ins)
        return ins

    t0, t1, t2 = (tile(j) for j in range(3))
    step(times(t0, a, weight(0, 0)))
    step(times(t1, b, weight(0, 1)))
    step(times(t2, a, weight(1, 0)))
    step(eng.tensor_tensor(a, t0, t1, ALU.add))
    step(times(t0, b, weight(1, 1)))
    return eng.tensor_tensor(b, t2, t0, ALU.add)


N_LOADS = 52

_LAYOUT = {
    "WqT": ("L0_attn_Wq_down", lambda a: a.T), "WkT": ("L0_attn_Wk_down", lambda a: a.T),
    "WvT": ("L0_attn_Wv_down", lambda a: a.T), "L0_cT": ("L0_c", lambda a: a.T), "L1_cT": ("L1_c", lambda a: a.T),
    "L1_attn_W_inT": ("L1_attn_W_in", lambda a: a.T), "L1_attn_W_xT": ("L1_attn_W_x", lambda a: a.T),
    "L1_attn_W_dtT": ("L1_attn_W_dt", lambda a: a.T), "L1_attn_W_outT": ("L1_attn_W_out", lambda a: a.T),
    "L1_ffn_W_conT": ("L1_ffn_W_con", lambda a: a.T),
    "conv_b": ("L1_attn_conv_b", lambda a: a.reshape(-1, P).T), "b_dt": ("L1_attn_b_dt", lambda a: a.reshape(-1, P).T),
    "D": ("L1_attn_D", lambda a: a.reshape(-1, P).T), "up_bias": ("L1_ffn_up_bias", lambda a: a.reshape(-1, P).T),
    "up_w": ("L1_ffn_up_weights", lambda a: a.transpose(0, 2, 3, 1).reshape(a.shape[0], -1)),
    "down_w": ("L1_ffn_down_weights", lambda a: a.transpose(0, 2, 3, 1).reshape(a.shape[0], -1)),
}
_AS_THEY_COME = [
    "L0_attn_x", "L0_attn_Wq_up_c", "L0_attn_Wq_up_e", "L0_attn_Wk_up_c", "L0_attn_Wk_up_e", "L0_attn_Wv_up",
    "L0_attn_Wc", "L0_ffn_Win", "L0_ffn_bin_", "L0_ffn_W1", "L0_ffn_b1", "L0_ffn_W2", "L0_ffn_b2", "L0_ffn_Wout",
    "L0_ffn_bout", "L0_wmod", "L1_wmod", "L1_attn_conv_w", "L1_attn_A_log", "L1_ffn_W_exp", "L1_ffn_b_exp",
    "L1_ffn_b_con", "L1_ffn_down_bias",
]


def kernel(**inputs):
    import numpy as np
    import concourse.bacc as _bacc
    from concourse import mybir as _mybir
    from concourse.bass_utils import run_bass_kernel_spmd as _run

    nc = _bacc.Bacc("TRN2", target_bir_lowering=False, num_devices=1)
    arrays, t = {}, {}

    def give(name, a):
        a = np.ascontiguousarray(a)
        arrays[f"in_{name}"] = a
        t[name] = nc.dram_tensor(f"in_{name}", a.shape, _mybir.dt.from_np(a.dtype), kind="ExternalInput").ap()

    for name in _AS_THEY_COME:
        give(name, np.asarray(inputs[name]))
    for name, (source, layout) in _LAYOUT.items():
        give(name, layout(np.asarray(inputs[source])))
    T, DE = inputs["L0_attn_x"].shape[1], 8
    inv = (1.0 / np.float32(10000.0) ** (np.arange(0, DE, 2, dtype=np.float32) / np.float32(DE))).astype(np.float32)
    angle = (np.arange(T, dtype=np.float32)[:, None] * inv[None, :]).astype(np.float32)
    rows = np.tile(np.concatenate([angle, angle], axis=1).T, (16, 1))
    give("cos", np.cos(rows).astype(np.float32))
    give("sin", np.sin(rows).astype(np.float32))
    shape = inputs["L0_attn_x"].shape
    t["out"] = nc.dram_tensor("out_0", shape, _mybir.dt.float32, kind="ExternalOutput").ap()
    adaln_kernel(nc, t)
    r = _run(nc, [arrays], core_ids=[0])
    return r.results[0]["out_0"]
```

```python
from contextlib import ExitStack

import concourse.bass as bass
from concourse import mybir

P = 128
ALU = mybir.AluOpType
ACT = mybir.ActivationFunctionType
F32 = mybir.dt.float32
BF16 = mybir.dt.bfloat16
I32 = mybir.dt.int32
AX_X = mybir.AxisListType.X

MASKED = -1e30
LN_EPS = 1e-5
HALF = 512

OWN_STEPS = {"dve": 91, "pool": 2}


class Count:

    def __init__(self, sem, per, unit=1, start=0):
        self.sem, self.per, self.unit, self.start, self.made = sem, per, unit, start, 0

    def step(self, ins):
        self.made += 1
        ins.then_inc(self.sem, self.unit)

    def at(self, b, n):
        return b * (self.per * self.unit) + n * self.unit + self.start


def adaln_kernel(nc, t):
    B, T, C = t["L0_attn_x"].shape
    H, L, DH, DE = 16, 64, 16, 8
    NT, CT, NH = T // P, C // P, T // HALF
    SCALE = float(DH) ** -0.5
    M, J = t["L0_ffn_W1"].shape
    DI, TAPS = t["L1_attn_conv_w"].shape
    R = t["L1_attn_W_dtT"].shape[0]
    S = t["L1_attn_A_log"].shape[0]
    DTL = DI // P
    F = t["L1_ffn_W_exp"].shape[1]
    FT = F // P
    LEVELS = t["up_w"].shape[0]
    PIECES = 3
    PIECE_OF = ((0, 0, 0, 1, 1, 2), (0, 1, 2, 0, 1, 0))
    KROWS = len(PIECE_OF[0]) * DH
    NEAR = KROWS + PIECES
    HG = 4
    BLOCKS = [(g * HG + h, q, k) for g in range(H // HG) for q in range(NT) for k in range(q + 1) for h in range(HG)]
    PER_CHUNK = 8
    CHUNKS = len(BLOCKS) // PER_CHUNK
    SPARTS = [(h, q, a, min(a + HALF, (q + 1) * P)) for h in range(H) for q in range(NT)
              for a in range(0, (q + 1) * P, HALF)]
    half_ends = [n // PER_CHUNK for n, (h, q, k) in enumerate(BLOCKS) if k == q and q % 4 == 3 and h % HG == HG - 1]
    GROUP_CHUNKS, MAXES, LAG = CHUNKS * HG // H, len(SPARTS) * HG // H, 2
    MAX_STEPS = MAXES // 4
    STEPS = GROUP_CHUNKS + CHUNKS + LAG + 1
    HRING, HBANKS, ZBANK = 7, 5, 5
    OUT_BANKS = (ZBANK, 3)
    assert ((S - 1) * NT + OUT_BANKS[1]) % HBANKS == OUT_BANKS[1] and OUT_BANKS[1] + HBANKS >= NT
    XR = R + 2 * S
    B_ROWS = (R, XR, XR + S)
    assert XR % 32 == 0 and XR + 2 * S == P
    MAX_BANKS = (6, 7, 0, 1, 2, 3)

    def max_bank(n):
        return MAX_BANKS[n % len(MAX_BANKS)] if n < MAXES else MAX_BANKS[n % 2]

    with ExitStack() as ctx:
        def sb(name, shape, dt=F32):
            return ctx.enter_context(nc.sbuf_tensor(name, shape, dt))

        sems = {}

        def ev(name):
            if name not in sems:
                sems[name] = ctx.enter_context(nc.semaphore(name))
            return sems[name]

        counts = []

        def count(name, per, unit=1, start=0):
            counts.append((name, Count(ev(name), per, unit, start)))
            return counts[-1][1]

        PS = ctx.enter_context(nc.psum_tensor("PS", [P, 8, 512], F32))

        ident = sb("ident", [P, P])
        identb = sb("identb", [P, P], BF16)
        mask_qk = sb("mask_qk", [P, P], BF16)
        mask_kq = sb("mask_kq", [P, P], BF16)
        ones = sb("ones", [P, 1])
        cos = sb("cos", [P, T])
        sin = sb("sin", [P, T])
        w_qk = sb("w_qk", [P, CT, 2, 3, H * DE])
        w_v = sb("w_v", [P, CT, C])
        w_c = sb("w_c", [P, CT, C])
        w_in0 = sb("w_in0", [P, CT, M])
        bin2 = sb("bin2", [P, 1])
        w1 = sb("w1", [P, J])
        b1 = sb("b1", [P, J])
        w2 = sb("w2", [P, J])
        diag_w2 = sb("diag_w2", [P, J, P])
        b2 = sb("b2", [P, 1])
        w_out0 = sb("w_out0", [P, C])
        bias_out0 = sb("bias_out0", [P, C])
        w_in1 = sb("w_in1", [P, CT, 2 * DI])
        conv_w = sb("conv_w", [P, DTL, TAPS])
        conv_b = sb("conv_b", [P, DTL])
        a_neg = sb("a_neg", [P, S])
        d_all = sb("d_all", [P, DI])
        w_x = sb("w_x", [P, DTL, P])
        w_dt = sb("w_dt", [R, DI])
        b_dt = sb("b_dt", [P, DTL])
        w_out1 = sb("w_out1", [P, DTL, C])
        sel = sb("sel", [P, S, P], BF16)
        w_exp = sb("w_exp", [P, CT, F])
        gelu_b = sb("gelu_b", [P, FT])
        w_con = sb("w_con", [P, FT, C])
        bias_out1 = sb("bias_out1", [P, C])
        mod_col = sb("mod_col", [P, 2, 4, CT, B])
        mod_b = sb("mod_b", [P, 2, 4, CT])
        gates = sb("gates", [P, 4, C])
        bias_g = sb("bias_g", [P, C])
        X = sb("X", [P, NT, C])
        hT = sb("hT", [P, CT, T])
        bn = sb("bn", [P, NT, 6])
        mv = sb("mv", [P, NT, 2])
        spare = sb("spare", [P, 1])
        less = sb("less", [P, 2])
        norm = sb("norm", [P, 6, NT])
        slots = sb("slots", [P, H * NT, 2])
        negm = sb("negm", [P, HG * NT])
        n_rest = sb("n_rest", [HG * NT, P])
        n_pieces = sb("n_pieces", [HG * NT, PIECES, P], BF16)
        recip = sb("recip", [P, 2, NT])
        c_t = sb("c_t", [P, NT, S])
        b_st = sb("b_st", [P, T], BF16)

        z_first = sb("z_first", [P, 5, DI])
        z_tiles = [z_first[:, i] for i in range(5)]
        z_tiles += [hT[:, k, 0:DI] for k in range(CT)] + [hT[:, :, DI:DI + DI // CT]]
        assert len(z_tiles) == NT and DI + DI // CT <= 6 * P

        ARENA = 25856
        arena = sb("arena", [P, ARENA])

        def part(at, cols, dt=F32, rows=P):
            words = cols if dt == F32 else cols // 2
            assert at + words <= ARENA, (at, words)
            v = arena[0:rows, at:at + words]
            return v if dt == F32 else v.bitcast(dt)

        at = 0
        bd = part(at, 3 * 48).rearrange("p (m n) -> p m n", m=3)
        at += 144
        wT = part(at, 3 * 8 * C).rearrange("p (m k c) -> p m k c", m=3, k=8)
        mod_row = part(at, 2 * 6 * C, rows=B).rearrange("p (l n) -> p l n", l=2)
        at += 3 * 8 * C
        cT = part(at, 2 * CT * B).rearrange("p (l k b) -> p l k b", l=2, k=CT)
        at += 2 * CT * B
        wmod = part(at, 2 * CT * 6 * C).rearrange("p (l k n) -> p l k n", l=2, k=CT)
        at += 2 * CT * 6 * C
        bf_w = {n: [v.rearrange("p (i j n) -> p i j n", i=2, j=2) for v in (
                part(at + 2048 * i, 4 * (F // 2)), other[:, :, :].rearrange("p a n -> p (a n)"))]
                for i, (n, other) in enumerate((("up", X), ("down", hT)))}
        at += 4096
        bf_t = [[part(at + 1024 * (3 * i + j), CT * F // 2).rearrange("p (k n) -> p k n", k=CT)
                 for j in range(3)] for i in range(2)]
        at += 6144
        bexp = part(at, F)
        at += F
        ones_row = part(at, 384, BF16)
        at += 192
        dn_bias = part(at, C)
        up_bias = part(at + C, FT)
        xn = part(10240, NT * C).rearrange("p (i c) -> p i c", i=NT)
        q_st = part(0, H * T, BF16).rearrange("p (h t) -> p h t", h=H)
        k_st = part(8192, H * T, BF16).rearrange("p (h t) -> p h t", h=H)
        V_COLS = NT * H * (DH + 1)
        v_flat = part(16384, V_COLS + 16)
        v_aug = v_flat[:, 0:V_COLS].rearrange("p (i h d) -> p i h d", i=NT, h=H)
        P_AT, P_RING = 16384 + V_COLS + 16, 4
        rope_e, rope_r, qk_rest, pieces = [], [], [], []
        for at in (8192, P_AT):
            rope_e.append(part(at, T))
            rope_r.append(part(at + T, T))
            qk_rest.append(part(at + 2 * T, 2 * T).rearrange("p (e t) -> p e t", e=2))
            pieces.append(part(at + 4 * T, PIECES * 2 * T, BF16).rearrange("p (n e t) -> p n e t", n=PIECES, e=2))
        pT = [part(P_AT + i * PER_CHUNK * P, PER_CHUNK * P) for i in range(P_RING)]
        y_at = part(P_AT + P_RING * PER_CHUNK * P, NT * C).rearrange("p (i c) -> p i c", i=NT)
        oT = [part(P_AT + P_RING * PER_CHUNK * P + NT * C + HALF * i, HALF) for i in range(1)]
        o_rec = recip[:, :, :].rearrange("p a i -> p (a i)").rearrange("p (i h) -> p i h", h=HG)
        w_g = part(8192, FT * C).rearrange("p (k c) -> p k c", k=FT)
        yT = part(0, CT * T).rearrange("p (k t) -> p k t", k=CT)
        s0, g0 = part(0, HALF), part(512, HALF)
        r0 = [part(1024 + HALF * i, HALF) for i in range(4)]
        h_r = [part(T * i, T) for i in range(HRING)]
        bb = [part(T * (HRING + i), T) for i in range(2)]
        xs = part(0, DTL * T).rearrange("p (d t) -> p d t", d=DTL)
        conv_t = [part(4096 + T * i, T) for i in range(2)]
        at = T * (HRING + 2)
        dt_t = part(at, DTL * T).rearrange("p (d t) -> p d t", d=DTL)
        dtx = part(at + DTL * T, DTL * T).rearrange("p (d t) -> p d t", d=DTL)
        y_s = part(at + 2 * DTL * T, NT * DI).rearrange("p (i d) -> p i d", i=NT)
        at += 3 * DTL * T
        a_r = [part(at + i * T, T) for i in range(2)]
        u_r = [part(at + (2 + i) * T, T) for i in range(2)]
        sp_e = [part(4096 + T * i, T) for i in (2, 3, 0, 1)]
        sp_c = [a_r[1], u_r[1]]
        x_rows = dtx[0:XR, 3]
        b_rest = dtx[:, 2]
        b_piece = dtx[:, 1].bitcast(BF16)[:, 0:T]
        yg = [part((2 + i) * DI, DI) for i in range(2)]
        ygT = [part((4 + i) * DI, DI).rearrange("p (d t) -> p d t", d=DTL) for i in range(2)]
        gl = part(0, FT * T).rearrange("p (f t) -> p f t", f=FT)

        def qk_psum_c(m):
            return PS[:, (0, 6)[m]:(0, 6)[m] + 2, :].rearrange("p a n -> p (a n)")

        def half_tiles(h):
            return slice(h * NT // NH, (h + 1) * NT // NH)

        def tokens(x, b, h):
            return x[b].rearrange("(i p) c -> p i c", p=P)[:, half_tiles(h), :]

        def dram(name, shape, dt=F32):
            return nc.dram_tensor(name, shape, dt, kind="Internal").ap()

        gate_d = dram("gate_d", (4, B, C))
        ones_d = dram("ones_d", (P, 384), BF16)

        x_loaded = [count(f"x_loaded_{h}", 1, 16) for h in range(NH)]
        g_loaded = count("g_loaded", 1, 16)
        x_stored = [count(f"x_stored_{h}", 1, 16, start=16) for h in range(NH)]
        mod_b_ready = count("mod_b_ready", 1)
        own = {e: count(f"{e}_own", OWN_STEPS[e]) for e in OWN_STEPS}
        norm_ready = count("norm_ready", 4)
        xn_even = count("xn_even", 4 * NT // 2)
        xn_odd = count("xn_odd", 4 * NT // 2)
        hT_psum = count("hT_psum", 4 * NT)
        hT_ready = count("hT_ready", 4 * CT * NH)
        qk_psum = count("qk_psum", 6)
        qk_e_read = count("qk_e_read", 2)
        qk_r_read = count("qk_r_read", 2)
        v_psum = count("v_psum", NT)
        v_ready = count("v_ready", NT)
        roped = count("roped", 2)
        piece1 = count("piece1", 4)
        rest1 = count("rest1", 4)
        piece2 = count("piece2", 4)
        piece3 = count("piece3", 4)
        stacks_in = count("stacks_in", 4 * len(PIECE_OF[0]) + 1, 16)
        smax_psum = count("smax_psum", len(SPARTS))
        smax_read = count("smax_read", len(SPARTS))
        negm_ready = count("negm_ready", H // HG)
        negm_T = count("negm_T", H // HG)
        negm_split = count("negm_split", H // HG)
        negm_in = count("negm_in", PIECES * H // HG, 16)
        s_psum = count("s_psum", CHUNKS)
        p_ready = count("p_ready", CHUNKS)
        pv_done = count("pv_done", CHUNKS)
        oT_ready = count("oT_ready", NH * H // HG)
        o_psum = count("o_psum", NH * H // HG)
        o_read = count("o_read", NH * H // HG)
        yT_psum = count("yT_psum", CT * NH)
        yT_ready = count("yT_ready", CT * NH)
        w_g_ready = count("w_g_ready", 4)
        x_biased = count("x_biased", 2)
        res_psum = count("res_psum", 4 * NT)
        x_added = count("x_added", 4 * NT, start=1)
        s0_psum = count("s0_psum", 1)
        s0_ready = count("s0_ready", 1)
        r0_ready = count("r0_ready", J)
        r0_used = count("r0_used", J)
        g0_ready = count("g0_ready", 1)
        xr_psum = count("xr_psum", DTL)
        conv0 = count("conv0", DTL)
        conv_done = count("conv_done", DTL)
        xs_ready = count("xs_ready", DTL)
        xd_psum = count("xd_psum", 1)
        x_rows_ready = count("x_rows_ready", 1)
        b_split = count("b_split", 1)
        c_psum = count("c_psum", 1)
        dt_psum = count("dt_psum", DTL)
        dt_max = count("dt_max", DTL)
        dt_abs = count("dt_abs", DTL)
        dt_exp = count("dt_exp", DTL)
        dt_ln = count("dt_ln", DTL)
        dt_corr = count("dt_corr", DTL)
        dt_sum = count("dt_sum", DTL)
        dt_ready = count("dt_ready", DTL)
        dtx_ready = count("dtx_ready", DTL)
        d_psum = count("d_psum", NT)
        d_read = count("d_read", NT)
        bb_psum = count("bb_psum", S)
        bb_ready = count("bb_ready", S)
        a_ready = count("a_ready", S * DTL)
        u_ready = count("u_ready", S * DTL)
        h_ready = count("h_ready", S * DTL)
        h_T = count("h_T", S * NT)
        y_added = count("y_added", S * NT)
        z_psum = count("z_psum", NT)
        z_kept = count("z_kept", NT)
        z_ready = count("z_ready", NT)
        yg_ready = count("yg_ready", NT)
        ygT_psum = count("ygT_psum", NT)
        ygT_ready = count("ygT_ready", NT)
        f_psum = count("f_psum", FT * NH)
        f_ready = count("f_ready", FT * NH)

        last_of = {
            "load": [(mod_b_ready, 1)],
            "ln_a0": [(hT_ready, CT * NH)],
            "qkv": [(piece3, 4), (v_ready, NT)],
            "attend": [(o_read, NH * H // HG)],
            "project": [(x_added, NT)],
            "ln_b0": [(hT_ready, 2 * CT * NH)],
            "ffn0": [(x_added, 2 * NT)],
            "ln_a1": [(hT_ready, 3 * CT * NH)],
            "xproj": [(d_read, NT), (dtx_ready, DTL)],
            "out": [(x_added, 3 * NT)],
            "ln_b1": [(hT_ready, 4 * CT * NH)],
            "ffn1": [(x_added, 0)],
        }

        def begins(eng, b, name):
            names = list(last_of)
            for c, n in last_of[names[names.index(name) - 1]]:
                eng.wait_ge(c.sem, c.at(b, n))

        def own_step(engine, eng, b, ins):
            o = own[engine]
            o.step(ins)
            eng.wait_ge(o.sem, o.at(b, o.made))

        block = ctx.enter_context(nc.Block())

        @block.sync
        def _(sp):
            for dst, src in (
                    (w_con[:, :, :].rearrange("p f c -> p (f c)").rearrange("p (k n) -> p k n", k=CT),
                     t["L1_ffn_W_conT"].rearrange("(k p) n -> p k n", p=P)),
                    (w_exp[:, :, :], t["L1_ffn_W_exp"].rearrange("(k p) n -> p k n", p=P)),
                    (bexp, t["L1_ffn_b_exp"].partition_broadcast(P)),
                    (up_bias, t["up_bias"]),
                    (bias_out1[:, :], t["L1_ffn_b_con"].partition_broadcast(P)),
                    (dn_bias, t["L1_ffn_down_bias"].partition_broadcast(P))):
                sp.dma_start(dst, src).then_inc(ev("ffn1_loads"), 16)
            for i in range(LEVELS):
                for side, (name, level) in enumerate((("down", LEVELS - 1 - i), ("up", i))):
                    if i >= 2:
                        sp.wait_ge(ev(f"{name}_level"), i - 1)
                    sp.dma_start(bf_w[name][i % 2].rearrange("p i j n -> p (i j n)"),
                                 t[f"{name}_w"][level].partition_broadcast(P)).then_inc(ev(f"{name}_weights_{i % 2}"), 16)
            sp.wait_ge(ev("ones_row_set"), 1)
            sp.dma_start(ones_d, ones_row).then_inc(ev("ones_out"), 16)
            sp.wait_ge(ev("mod_rows"), 1)
            for g in range(4):
                l, kind = g // 2, (2, 5)[g % 2]
                sp.dma_start(gate_d[g], mod_row[:, l, kind * C:kind * C + C]).then_inc(ev("gates_out"), 16)
            sp.wait_ge(ev("ones_out"), 16)

            with sp.Fori(0, B, 1) as b:
                ROWS = len(PIECE_OF[0])
                value = {(c.sem.name, n): sp.snap(c.at(b, n)) for c, n in (
                    *[(piece3, u + 1) for u in range(4)], (piece1, 4), (piece2, 4), (stacks_in, 2 * ROWS),
                    *[(negm_split, hg + 1) for hg in range(H // HG)])}

                def wait(c, n):
                    sp.wait_ge(c.sem, value[c.sem.name, n])

                def stack_piece(m, n, e):
                    stack = (q_st, k_st)[m]
                    for i in range(ROWS):
                        if PIECE_OF[m][i] == n:
                            row = DH * i + DE * e
                            stacks_in.step(sp.dma_start(stack[row:row + DE], pieces[m][:, n, e, :]))

                for e in range(2):
                    wait(piece3, e + 1)
                    for n in range(PIECES):
                        stack_piece(0, n, e)
                wait(stacks_in, 2 * ROWS)
                stacks_in.step(sp.dma_start(k_st[KROWS:NEAR].rearrange("n h t -> n (h t)"),
                                            ones_d.rearrange("a c -> (a c)").rearrange("(n x) -> n x", n=PIECES)))
                wait(piece3, 3)
                for n in range(PIECES):
                    stack_piece(1, n, 0)
                for n in range(PIECES):
                    wait((piece1, piece2, piece3)[n], 4)
                    stack_piece(1, n, 1)
                for hg in range(H // HG):
                    wait(negm_split, hg + 1)
                    for n in range(PIECES):
                        row = KROWS + n
                        negm_in.step(sp.dma_start(
                            q_st[row:row + 1, hg * HG:(hg + 1) * HG].rearrange("n h t -> n (h t)"),
                            n_pieces[:, n, :]))

        @block.gpsimd
        def _(pool):
            pool.memset(bd.rearrange("p m n -> p (m n)"), 0.0).then_inc(ev("cleared"), 1)
            pool.memset(w_x[:, :, :], 0.0).then_inc(ev("cleared"), 1)
            pool.memset(ident[:, :], 0.0).then_inc(ev("made"), 1)
            pool.memset(mask_qk[:, :], 0.0).then_inc(ev("made"), 1)
            pool.memset(mask_kq[:, :], 0.0).then_inc(ev("made"), 1)
            pool.memset(sel[:, :, :], 0.0).then_inc(ev("made"), 1)
            pool.memset(ones[:, :], 1.0).then_inc(ev("made"), 1)
            pool.memset(slots[:, :, :], MASKED).then_inc(ev("made"), 1)
            pool.memset(ones_row, 1.0).then_inc(ev("ones_row_set"), 1)
            pool.wait_ge(ev("made"), 6)
            pool.affine_select(out=ident[:, :], in_=ident[:, :], compare_op=ALU.not_equal, fill=1.0, base=0,
                               pattern=[[-1, P]], channel_multiplier=1).then_inc(ev("made"), 1)
            pool.affine_select(out=mask_qk[:, :], in_=mask_qk[:, :], compare_op=ALU.is_ge, fill=MASKED, base=0,
                               pattern=[[-1, P]], channel_multiplier=1).then_inc(ev("made"), 1)
            pool.affine_select(out=mask_kq[:, :], in_=mask_kq[:, :], compare_op=ALU.is_ge, fill=MASKED, base=0,
                               pattern=[[1, P]], channel_multiplier=-1).then_inc(ev("made"), 1)
            for q in range(PIECES):
                pool.affine_select(out=sel[:, :, :], in_=sel[:, :, :], compare_op=ALU.not_equal, fill=1.0,
                                   base=-B_ROWS[q], pattern=[[-1, S], [0, P]],
                                   channel_multiplier=1).then_inc(ev("made"), 1)
                pool.wait_ge(ev("made"), 10 + q)
            for q in range(2):
                pool.memset(less[:, q:q + 1], -1.0).then_inc(ev("less_set"), 1)
                pool.wait_ge(ev("less_set"), 2 * q + 1)
                pool.affine_select(out=less[:, q:q + 1], in_=less[:, q:q + 1], compare_op=ALU.is_ge, fill=0.0,
                                   base=-B_ROWS[q + 1], pattern=[[0, 1]],
                                   channel_multiplier=1).then_inc(ev("less_set"), 1)
            pool.tensor_copy(identb[:, :], ident[:, :]).then_inc(ev("made"), 1)
            pool.wait_ge(ev("ffn1_loads"), 16 * 6)
            pool.tensor_tensor(bias_out1[:, :], bias_out1[:, :], dn_bias, ALU.add).then_inc(ev("made"), 1)
            steps = [0]

            def low(ins):
                steps[0] += 1
                ins.then_inc(ev("low"), 1)
                pool.wait_ge(ev("low"), steps[0])

            D = w_con[:, :, :].rearrange("p f c -> p (f c)")
            for i in range(LEVELS):
                s = 2 ** (LEVELS - 1 - i)
                pool.wait_ge(ev(f"down_weights_{i % 2}"), 16 * (i // 2 + 1))
                last = butterfly_level(pool, D, CT, s, bf_w["down"][i % 2], bf_t[1], True, low)
                last.then_inc(ev("down_level"), 1)
                pool.wait_ge(ev("down_level"), i + 1)

            with pool.Fori(0, B, 1) as b:
                pool.wait_ge(g_loaded.sem, g_loaded.at(b, 1))
                begins(pool, b, "project")
                ins = pool.tensor_tensor(w_g[:, 0:CT, :], w_c[:, :, :],
                                         gates[:, 0:1, :].broadcast_to([P, CT, C]), ALU.mult)
                w_g_ready.step(ins)
                pool.wait_ge(w_g_ready.sem, w_g_ready.at(b, 1))

                begins(pool, b, "ffn0")
                w_g_ready.step(pool.tensor_tensor(w_g[:, 0, :], w_out0[:, :], gates[:, 1, :], ALU.mult))
                own_step("pool", pool, b, pool.tensor_tensor(bias_g[:, :], bias_out0[:, :], gates[:, 1, :], ALU.mult))
                x_biased.step(pool.tensor_tensor(X[:, :, :], X[:, :, :],
                                                 bias_g[:, :].unsqueeze(1).broadcast_to([P, NT, C]), ALU.add))
                pool.wait_ge(x_biased.sem, x_biased.at(b, 1))

                begins(pool, b, "xproj")
                for d in range(DTL):
                    pool.wait_ge(dt_corr.sem, dt_corr.at(b, d + 1))
                    pool.wait_ge(dt_max.sem, dt_max.at(b, d + 1))
                    dt_sum.step(pool.tensor_tensor(dt_t[:, d], dt_t[:, d], sp_c[d % 2], ALU.add))

                pool.wait_ge(dt_sum.sem, dt_sum.at(b, DTL))

                for s in range(S):
                    pool.wait_ge(bb_ready.sem, bb_ready.at(b, s + 1))
                    for d in range(DTL):
                        n = s * DTL + d
                        if s == 0:
                            pool.wait_ge(dtx_ready.sem, dtx_ready.at(b, d + 1))
                        if n >= 2:
                            pool.wait_ge(h_ready.sem, h_ready.at(b, n - 1))
                        u_ready.step(pool.tensor_tensor(u_r[n % 2], dtx[:, d], bb[(s + 1) % 2], ALU.mult))

                pool.wait_ge(u_ready.sem, u_ready.at(b, S * DTL))
                w_g_ready.step(pool.tensor_tensor(w_g[:, 0:DTL, :], w_out1[:, :, :],
                                                  gates[:, 2:3, :].broadcast_to([P, DTL, C]), ALU.mult))

                begins(pool, b, "ffn1")
                w_g_ready.step(pool.tensor_tensor(w_g[:, :, :], w_con[:, :, :],
                                                  gates[:, 3:4, :].broadcast_to([P, FT, C]), ALU.mult))
                own_step("pool", pool, b, pool.tensor_tensor(bias_g[:, :], bias_out1[:, :], gates[:, 3, :], ALU.mult))
                x_biased.step(pool.tensor_tensor(X[:, :, :], X[:, :, :],
                                                 bias_g[:, :].unsqueeze(1).broadcast_to([P, NT, C]), ALU.add))
                pool.wait_ge(x_biased.sem, x_biased.at(b, 2))

        @block.scalar
        def _(act):
            A = nc.scalar.activation
            for c in x_stored:
                act.sem_inc(c.sem, c.start)
            act.sem_inc(x_added.sem, x_added.start)
            loads = [0]

            def pre(dst, src):
                loads[0] += 1
                act.dma_start(dst, src).then_inc(ev("pre_loads"), 16)

            act.wait_ge(ev("cleared"), 2)
            for m, n in enumerate("qkv"):
                pre(wT[:, m], t[f"W{n}T"].rearrange("(k p) c -> p k c", p=P))
            for h in range(2):
                rows = slice(L * h, L * h + L)
                for m, n in enumerate("qk"):
                    pre(bd[rows, m, DE * h:DE * h + DE], t[f"L0_attn_W{n}_up_c"])
                    pre(bd[rows, m, 16 + DE * h:16 + DE * h + DE], t[f"L0_attn_W{n}_up_e"])
                pre(bd[rows, 2, DH * h:DH * h + DH], t["L0_attn_Wv_up"])
                pre(bin2[rows, :], t["L0_ffn_bin_"].rearrange("(m o) -> m o", o=1))
                pre(b2[rows, :], t["L0_ffn_b2"].rearrange("(m o) -> m o", o=1))
                pre(w1[rows, :], t["L0_ffn_W1"])
                pre(b1[rows, :], t["L0_ffn_b1"])
                pre(w2[rows, :], t["L0_ffn_W2"])
                pre(w_out0[rows, :], t["L0_ffn_Wout"])
            for l in range(2):
                pre(cT[:, l], t[f"L{l}_cT"].rearrange("(k p) b -> p k b", p=P))
                pre(wmod[:, l], t[f"L{l}_wmod"].rearrange("(k p) n -> p k n", p=P))
            pre(cos[:, :], t["cos"])
            pre(sin[:, :], t["sin"])
            pre(w_c[:, :, :], t["L0_attn_Wc"].rearrange("(k p) n -> p k n", p=P))
            pre(w_in0[:, :, :], t["L0_ffn_Win"].rearrange("(k p) n -> p k n", p=P))
            pre(bias_out0[:, :], t["L0_ffn_bout"].partition_broadcast(P))
            pre(w_in1[:, :, :], t["L1_attn_W_inT"].rearrange("(k p) n -> p k n", p=P))
            pre(conv_w[:, :, :], t["L1_attn_conv_w"].rearrange("(k p) n -> p k n", p=P))
            pre(conv_b[:, :], t["conv_b"])
            pre(b_dt[:, :], t["b_dt"])
            pre(d_all[:, :], t["L1_attn_D"].partition_broadcast(P))
            pre(a_neg[:, :], t["L1_attn_A_log"].partition_broadcast(P))
            w_xT = t["L1_attn_W_xT"].rearrange("(k p) n -> p k n", p=P)
            pre(w_x[:, :, 0:R + 2 * S], w_xT)
            for q in range(1, PIECES):
                pre(w_x[:, :, B_ROWS[q]:B_ROWS[q] + S], w_xT[:, :, R:R + S])
            pre(w_dt[:, :], t["L1_attn_W_dtT"])
            pre(w_out1[:, :, :], t["L1_attn_W_outT"].rearrange("(k p) n -> p k n", p=P))
            assert loads[0] == N_LOADS, loads[0]
            act.wait_ge(ev("pre_loads"), 16 * N_LOADS)
            A(cT, cT, ACT.Silu).then_inc(ev("c_silu"), 1)
            A(a_neg[:, :], a_neg[:, :], ACT.Exp).then_inc(ev("a_exp"), 1)
            act.wait_ge(ev("a_exp"), 1)
            A(a_neg[:, :], a_neg[:, :], ACT.Copy, scale=-1.0).then_inc(ev("a_exp"), 1)
            act.wait_ge(ev("mod_psum"), 2)
            for l in range(2):
                for n in range(3):
                    last = A(mod_row[:, l, n * 512:n * 512 + 512], PS[0:B, 3 * l + n, :], ACT.Copy)
            last.then_inc(ev("mod_copied"), 1)
            act.wait_ge(ev("a_exp"), 2)
            act.wait_ge(ev("gates_out"), 64)
            act.wait_ge(ev("ones_out"), 16)
            act.wait_ge(ev("bf_ready"), 1)

            with act.Fori(0, B, 1) as b:
                begins(act, b, "load")
                for h in range(NH):
                    act.wait_ge(x_stored[h].sem, x_stored[h].at(b, 0))
                    x_loaded[h].step(act.dma_start(X[:, half_tiles(h), :], tokens(t["L0_attn_x"], b, h)))
                g_loaded.step(act.dma_start(gates[:, :, :], gate_d[:, b].partition_broadcast(P)))

                def ln(n, name):
                    l, kind = n // 2, (n % 2) * 2
                    act.wait_ge(mod_b_ready.sem, mod_b_ready.at(b, 1))
                    act.wait_ge(norm_ready.sem, norm_ready.at(b, n + 1))
                    for i in range(1, NT, 2):
                        xn_odd.step(A(xn[:, i], X[:, i], ACT.Identity, bias=norm[:, 5, i:i + 1],
                                      scale=norm[:, 4, i:i + 1]))
                    for g in range(NH):
                        act.wait_ge(hT_psum.sem, hT_psum.at(b, n * NT + (g + 1) * NT // NH))
                        for k in range(CT):
                            ins = A(hT[:, k, g * HALF:(g + 1) * HALF], PS[:, 2 * k + g, :], ACT.Identity,
                                    bias=mod_b[:, l, kind + 1, k:k + 1], scale=mod_b[:, l, kind, k:k + 1])
                            hT_ready.step(ins)
                    act.wait_ge(hT_ready.sem, hT_ready.at(b, (n + 1) * CT * NH))

                ln(0, "ln_a0")

                begins(act, b, "qkv")

                def first_piece(u):
                    m, e = divmod(u, 2)
                    if e:
                        act.wait_ge(roped.sem, roped.at(b, m + 1))
                        src = rope_e[m]
                    else:
                        act.wait_ge(qk_psum.sem, qk_psum.at(b, 3 * m + 1))
                        src = qk_psum_c(m)
                    piece1.step(A(pieces[m][:, 0, e], src, ACT.Copy))

                def second_piece(u):
                    m, e = divmod(u, 2)
                    act.wait_ge(rest1.sem, rest1.at(b, u + 1))
                    piece2.step(A(pieces[m][:, 1, e], qk_rest[m][:, e], ACT.Copy))

                first_piece(0)
                second_piece(0)
                first_piece(1)
                first_piece(2)
                second_piece(1)
                second_piece(2)
                first_piece(3)
                second_piece(3)
                for i in range(NT):
                    act.wait_ge(v_psum.sem, v_psum.at(b, i + 1))
                    ins = A(v_aug[:, i, :, 0:DH], PS[:, 4 + i % 4, 0:C].rearrange("p (h d) -> p h d", h=H), ACT.Copy)
                    v_ready.step(ins)
                act.wait_ge(v_ready.sem, v_ready.at(b, NT))

                begins(act, b, "attend")
                for g in range(CHUNKS):
                    act.wait_ge(s_psum.sem, s_psum.at(b, g + 1))
                    if g >= P_RING:
                        act.wait_ge(pv_done.sem, pv_done.at(b, g - P_RING + 1))
                    ins = A(pT[g % P_RING], PS[:, 2 * (g % 2):2 * (g % 2) + 2, :].rearrange("p a n -> p (a n)"),
                            ACT.Exp, scale=SCALE)
                    p_ready.step(ins)
                act.wait_ge(p_ready.sem, p_ready.at(b, CHUNKS))

                begins(act, b, "project")
                for g in range(NH):
                    for k in range(CT):
                        act.wait_ge(yT_psum.sem, yT_psum.at(b, g * CT + k + 1))
                        yT_ready.step(A(yT[:, k, g * HALF:(g + 1) * HALF], PS[:, 2 * k + g, :], ACT.Copy))
                act.wait_ge(yT_ready.sem, yT_ready.at(b, CT * NH))

                ln(1, "ln_b0")

                begins(act, b, "ffn0")
                act.wait_ge(s0_psum.sem, s0_psum.at(b, 1))
                s0_ready.step(A(s0, PS[:, 0, :], ACT.Identity, bias=bin2[:, 0:1]))
                act.wait_ge(s0_ready.sem, s0_ready.at(b, 1))
                for j in range(J):
                    if j >= 4:
                        act.wait_ge(r0_used.sem, r0_used.at(b, j - 3))
                    r0_ready.step(A(r0[j % 4], s0, ACT.Relu, bias=b1[:, j:j + 1], scale=w1[:, j:j + 1]))
                act.wait_ge(r0_used.sem, r0_used.at(b, J))
                g0_ready.step(A(g0, PS[:, 1, :], ACT.Identity, bias=b2[:, 0:1]))
                act.wait_ge(g0_ready.sem, g0_ready.at(b, 1))

                ln(2, "ln_a1")

                begins(act, b, "xproj")

                def conv_start(d):
                    act.wait_ge(xr_psum.sem, xr_psum.at(b, d + 1))
                    if d >= 2:
                        act.wait_ge(xs_ready.sem, xs_ready.at(b, d - 1))
                    conv0.step(A(conv_t[d % 2], PS[:, 2 * (d % 2):2 * (d % 2) + 2, :].rearrange("p a n -> p (a n)"),
                                 ACT.Identity, bias=conv_b[:, d:d + 1], scale=conv_w[:, d, TAPS - 1:TAPS]))

                def conv_end(d):
                    act.wait_ge(conv_done.sem, conv_done.at(b, d + 1))
                    xs_ready.step(A(xs[:, d], conv_t[d % 2], ACT.Silu))

                conv_start(0)
                for d in range(1, DTL):
                    conv_start(d)
                    conv_end(d - 1)
                conv_end(DTL - 1)
                act.wait_ge(xd_psum.sem, xd_psum.at(b, 1))
                x_rows_ready.step(A(x_rows, PS[0:XR, 6:8, :].rearrange("p a n -> p (a n)"), ACT.Copy))
                for d in range(DTL):
                    psum = PS[:, 2 * (d % 2):2 * (d % 2) + 2, :].rearrange("p a n -> p (a n)")
                    act.wait_ge(dt_psum.sem, dt_psum.at(b, d + 1))
                    dt_abs.step(A(sp_e[d], psum, ACT.Abs, bias=b_dt[:, d:d + 1]))
                    dt_max.step(A(dt_t[:, d], psum, ACT.Relu, bias=b_dt[:, d:d + 1]))
                    act.wait_ge(dt_abs.sem, dt_abs.at(b, d + 1))
                    dt_exp.step(A(sp_e[d], sp_e[d], ACT.Exp, scale=-1.0))
                for d in range(DTL):
                    act.wait_ge(dt_corr.sem, dt_corr.at(b, d + 1))
                    dt_ln.step(A(sp_e[d], sp_e[d], ACT.Ln, bias=1.0))


                def bb_copy(s):
                    act.wait_ge(bb_psum.sem, bb_psum.at(b, s + 1))
                    if s >= 2:
                        act.wait_ge(u_ready.sem, u_ready.at(b, (s - 1) * DTL))
                    bb_ready.step(A(bb[(s + 1) % 2], PS[:, 6:8, :].rearrange("p a n -> p (a n)"), ACT.Copy))

                def keep_z(i):
                    act.wait_ge(z_psum.sem, z_psum.at(b, i + 1))
                    z_kept.step(A(z_tiles[i], PS[:, ZBANK, :] if i < NT - 1 else
                                  PS[:, ZBANK, :].rearrange("p (k n) -> p k n", k=CT), ACT.Copy))

                bb_copy(0)
                for s in range(S):
                    for d in range(DTL):
                        n = s * DTL + d
                        if n >= 2:
                            act.wait_ge(h_ready.sem, h_ready.at(b, n - 1))
                        if s == 0:
                            act.wait_ge(dt_ready.sem, dt_ready.at(b, d + 1))
                        if n == 1:
                            act.wait_ge(dt_sum.sem, dt_sum.at(b, DTL))
                        a_ready.step(A(a_r[n % 2], dt_t[:, d], ACT.Exp, scale=a_neg[:, s:s + 1]))
                        if d == 1 and s + 1 < S:
                            bb_copy(s + 1)
                        if d == DTL - 1 and s and s % 2 == 0:
                            keep_z(s // 2 - 1)
                keep_z(NT - 1)
                act.wait_ge(a_ready.sem, a_ready.at(b, S * DTL))
                act.wait_ge(z_kept.sem, z_kept.at(b, NT))

                for i in range(NT + 1):
                    if i < NT:
                        z_ready.step(A(z_tiles[i], z_tiles[i], ACT.Silu))
                    if i >= 1:
                        j = i - 1
                        act.wait_ge(ygT_psum.sem, ygT_psum.at(b, j + 1))
                        if j >= 2:
                            act.wait_ge(res_psum.sem, res_psum.at(b, 2 * NT + j - 1))
                        ygT_ready.step(A(ygT[j % 2].rearrange("p d t -> p (d t)"), PS[:, 6 + j % 2, :], ACT.Copy))
                act.wait_ge(ygT_ready.sem, ygT_ready.at(b, NT))

                ln(3, "ln_b1")

                begins(act, b, "ffn1")
                for g in range(NH):
                    for f in range(FT):
                        n = g * FT + f
                        act.wait_ge(f_psum.sem, f_psum.at(b, n + 1))
                        f_ready.step(A(gl[:, f, g * HALF:(g + 1) * HALF], PS[:, n % 4, :], ACT.Gelu,
                                       bias=gelu_b[:, f:f + 1]))
                for h in range(NH):
                    act.wait_ge(x_added.sem, x_added.at(b, 3 * NT + (h + 1) * NT // NH))
                    x_stored[h].step(act.dma_start(tokens(t["out"], b, h), X[:, half_tiles(h), :]))
            for c in x_stored:
                act.wait_ge(c.sem, c.at(B, 0))

        @block.vector
        def _(dve):
            V = nc.vector
            steps = [0]

            def up(ins):
                steps[0] += 1
                ins.then_inc(ev("up"), 1)
                dve.wait_ge(ev("up"), steps[0])

            dve.wait_ge(ev("pre_loads"), 16 * N_LOADS)
            for m in range(2):
                e = bd[:, m, 16:32].rearrange("p (n two) -> p n two", two=2)
                r = bd[:, m, 32:48].rearrange("p (n two) -> p n two", two=2)
                V.tensor_scalar(r[:, :, 0], e[:, :, 1], -1.0, None, ALU.mult).then_inc(ev("bd_ready"), 1)
                V.tensor_copy(r[:, :, 1], e[:, :, 0]).then_inc(ev("bd_ready"), 1)
            dve.wait_ge(ev("made"), 14)
            for j in range(J):
                V.tensor_scalar(diag_w2[:, j], ident[:, :], w2[:, j:j + 1], None, ALU.mult)
            dve.wait_ge(ev("fold_psum"), 1)
            for k in range(CT):
                for m in range(2):
                    src = PS[:, 2 * m + k, 0:384].rearrange("p (a n j) -> p a n j", a=8, n=3)
                    for n in range(3):
                        dst = w_qk[:, k, m, n, :].rearrange("p (r a h) -> p h a r", a=8, h=2)
                        for h in range(2):
                            V.tensor_copy(dst[:, h], src[:, :, n, DE * h:DE * h + DE])
                last = V.tensor_copy(w_v[:, k, :], PS[:, 4 + k, 0:C])
            last.then_inc(ev("folded"), 1)
            dve.wait_ge(ev("ffn1_loads"), 16 * 6)
            U = w_exp[:, :, :].rearrange("p k n -> p (k n)")
            for i in range(LEVELS):
                dve.wait_ge(ev(f"up_weights_{i % 2}"), 16 * (i // 2 + 1))
                up(butterfly_level(dve, U, CT, 2 ** i, bf_w["up"][i % 2], bf_t[0], False, up))
                butterfly_level(dve, bexp, 1, 2 ** i, bf_w["up"][i % 2], bf_t[0], False, up).then_inc(ev("up_level"), 1)
                dve.wait_ge(ev("up_level"), i + 1)
            dve.wait_ge(ev("mod_copied"), 1)
            for l in range(2):
                for kind in (2, 5):
                    g = mod_row[:, l, kind * C:kind * C + C]
                    sign, size = bf_t[0][0][0:B, 0, 0:C], bf_t[0][1][0:B, 0, 0:C]
                    up(V.tensor_scalar(sign, g, 0.0, 2.0, ALU.is_ge, ALU.mult))
                    up(V.scalar_tensor_tensor(out=size, in0=g, scalar=-1.0, in1=g, op0=ALU.mult, op1=ALU.max))
                    up(V.tensor_scalar(size, size, 0.25, None, ALU.max))
                    up(V.scalar_tensor_tensor(out=g, in0=sign, scalar=1.0, in1=size, op0=ALU.subtract, op1=ALU.mult))
            V.memset(recip[:, 0, 0:1], 0.0).then_inc(ev("mod_rows"), 1)
            dve.wait_ge(ev("mod_T"), 1)
            cols = mod_col[:, :, :, :, :].rearrange("p l n k b -> p (l n k b)").rearrange("p (a two x) -> p a two x", two=2, x=CT * B)
            src = PS[:, 6, 0:2 * 4 * CT * B].rearrange("p (a two x) -> p a two x", two=2, x=CT * B)
            V.tensor_scalar(cols[:, :, 0, :], src[:, :, 0, :], 1.0, None, ALU.add)
            V.tensor_copy(cols[:, :, 1, :], src[:, :, 1, :]).then_inc(ev("mod_ready"), 1)
            dve.wait_ge(ev("down_T"), 1)
            V.tensor_copy(w_con[:, :, :].rearrange("p f c -> p (f c)"), PS[:, 0:4, :].rearrange("p a n -> p (a n)"))
            V.tensor_tensor(gelu_b[:, :], PS[:, 4, 0:FT], up_bias, ALU.add).then_inc(ev("bf_ready"), 1)
            dve.wait_ge(ev("bf_ready"), 1)
            dve.wait_ge(ev("mod_ready"), 1)
            dve.wait_ge(ev("less_set"), 4)

            with dve.Fori(0, B, 1) as b:
                def wait(c, n):
                    dve.wait_ge(c.sem, c.at(b, n))

                def own_(ins):
                    own_step("dve", dve, b, ins)

                begins(dve, b, "load")
                mod_b_ready.step(V.tensor_copy(mod_b[:, :, :, :].rearrange("p l n k -> p (l n k)"),
                                               mod_col[:, :, :, :, bass.ds(b, 1)].rearrange("p l n k b -> p (l n k b)")))

                def stats(i):
                    return V.bn_stats(bn[:, i], X[:, i])

                def normalize(n):
                    V.memset(spare[:, :], 0.0)
                    for i in range(NT):
                        last = V.bn_aggr(mv[:, i], bn[:, i])
                    own_(last)
                    var, less_half, bits, y, r, less_mean = (norm[:, i] for i in range(6))
                    own_(V.tensor_scalar(var, mv[:, :, 1], LN_EPS, None, ALU.add))
                    V.tensor_scalar(less_half, var, -0.5, None, ALU.mult)
                    own_(V.tensor_scalar(bits.bitcast(I32), var.bitcast(I32), 1, None, ALU.logical_shift_right))
                    own_(V.tensor_scalar(r.bitcast(I32), bits.bitcast(I32), -1.0, float(0x5f3759df),
                                         ALU.mult, ALU.add))
                    for _ in range(3):
                        own_(V.tensor_tensor(y, r, r, ALU.mult))
                        own_(V.tensor_tensor(y, y, less_half, ALU.mult))
                        own_(V.scalar_tensor_tensor(out=r, in0=y, scalar=1.5, in1=r, op0=ALU.add, op1=ALU.mult))
                    norm_ready.step(V.scalar_tensor_tensor(out=less_mean, in0=mv[:, :, 0], scalar=-1.0, in1=r,
                                                           op0=ALU.mult, op1=ALU.mult))
                    for i in range(0, NT, 2):
                        xn_even.step(V.tensor_scalar(xn[:, i], X[:, i], mv[:, i, 0:1], r[:, i:i + 1],
                                                     ALU.subtract, ALU.mult))

                def add_residuals(n, i, bank):
                    wait(res_psum, n * NT + i + 1)
                    x_added.step(V.tensor_tensor(X[:, i], X[:, i], PS[:, bank, 0:C], ALU.add))
                    if n < 3 and i:
                        wait(x_added, n * NT + i)
                        stats(i - 1)
                    if n < 3 and i == NT - 1:
                        wait(x_added, (n + 1) * NT)
                        own_(stats(i))
                        normalize(n + 1)
                        wait(xn_even, (n + 2) * NT // 2)

                for h in range(NH):
                    wait(x_loaded[h], 1)
                    for i in range(h * NT // NH, (h + 1) * NT // NH):
                        last = stats(i)
                own_(last)
                normalize(0)
                wait(xn_even, NT // 2)

                begins(dve, b, "qkv")
                v_one = v_aug[:, :, :, DH:DH + 1].rearrange("p i h o -> p (i h) o")
                V.memset(v_one, 1.0)
                V.memset(v_flat[:, V_COLS:V_COLS + 16], 0.0)

                def times_cos(m):
                    wait(qk_psum, 3 * m + 2)
                    e = PS[:, (2, 0)[m]:(2, 0)[m] + 2, :].rearrange("p a n -> p (a n)")
                    qk_e_read.step(V.tensor_tensor(rope_e[m], e, cos[:, :], ALU.mult))

                def turned(m):
                    wait(qk_psum, 3 * m + 3)
                    r = PS[:, (4, 2)[m]:(4, 2)[m] + 2, :].rearrange("p a n -> p (a n)")
                    qk_r_read.step(V.tensor_tensor(rope_r[m], r, sin[:, :], ALU.mult))
                    wait(qk_e_read, m + 1)
                    wait(qk_r_read, m + 1)
                    roped.step(V.tensor_tensor(rope_e[m], rope_e[m], rope_r[m], ALU.add))

                def rest(u):
                    m, e = divmod(u, 2)
                    if e:
                        wait(roped, m + 1)
                    wait(piece1, u + 1)
                    src = rope_e[m] if e else qk_psum_c(m)
                    rest1.step(V.tensor_tensor(qk_rest[m][:, e], src, pieces[m][:, 0, e], ALU.subtract))

                def third_piece(u):
                    m, e = divmod(u, 2)
                    wait(piece2, u + 1)
                    wait(rest1, u + 1)
                    piece3.step(V.tensor_tensor(pieces[m][:, 2, e], qk_rest[m][:, e], pieces[m][:, 1, e],
                                                ALU.subtract))

                rest(0)
                times_cos(0)
                third_piece(0)
                turned(0)
                rest(1)
                rest(2)
                third_piece(1)
                times_cos(1)
                third_piece(2)
                turned(1)
                rest(3)
                third_piece(3)
                wait(piece3, 4)

                begins(dve, b, "attend")

                def row_maxima(n):
                    h, q, a, z = SPARTS[n]
                    wait(smax_psum, n + 1)
                    smax_read.step(V.tensor_reduce(slots[:, h * NT + q, a // HALF:a // HALF + 1],
                                                   PS[:, max_bank(n), 0:z - a], AX_X, ALU.max))

                def split_maxima(hg):
                    wait(smax_read, (hg + 1) * MAXES)
                    negm_ready.step(V.tensor_reduce(negm[:, :], slots[:, hg * HG * NT:(hg + 1) * HG * NT, :],
                                                    AX_X, ALU.max, negate=True))
                    wait(negm_T, hg + 1)
                    if hg:
                        wait(negm_in, PIECES * hg)
                    rows = PS[0:HG * NT, 6, 0:P]
                    own_(V.tensor_copy(n_pieces[:, 0], rows))
                    own_(V.tensor_tensor(n_rest[:, :], rows, n_pieces[:, 0], ALU.subtract))
                    own_(V.tensor_copy(n_pieces[:, 1], n_rest[:, :]))
                    negm_split.step(V.tensor_tensor(n_pieces[:, 2], n_rest[:, :], n_pieces[:, 1], ALU.subtract))

                def outputs_to_sbuf(n):
                    wait(pv_done, half_ends[n] + 1)
                    if n:
                        wait(o_psum, n)
                    oT_ready.step(V.tensor_copy(oT[0], PS[:, 4, :]))

                def divide(n):
                    hg, half = n // NH, n % NH
                    wait(o_psum, n + 1)
                    o = PS[:, 5, :].rearrange("p (i h d) -> p i h d", i=4, h=HG)
                    own_(V.reciprocal(o_rec, o[:, :, :, DH]))
                    for i in range(4):
                        ins = V.tensor_tensor(
                            y_at[:, 4 * half + i, hg * HG * DH:(hg + 1) * HG * DH].rearrange("p (h d) -> p h d", h=HG),
                            o[:, i, :, 0:DH], o_rec[:, i, :].unsqueeze(2).broadcast_to([P, HG, DH]), ALU.mult)
                    o_read.step(ins)

                for st in range(STEPS):
                    hg, j = divmod(st, GROUP_CHUNKS)
                    if hg < H // HG and j < MAX_STEPS:
                        for n in range(4):
                            row_maxima(hg * MAXES + 4 * j + n)
                    if hg < H // HG and j == MAX_STEPS:
                        split_maxima(hg)
                    g = st - GROUP_CHUNKS - LAG
                    if g in half_ends:
                        outputs_to_sbuf(half_ends.index(g))
                    if g - 1 in half_ends:
                        divide(half_ends.index(g - 1))

                begins(dve, b, "project")
                for i in range(NT):
                    add_residuals(0, i, 4 + i % 4)

                begins(dve, b, "ffn0")
                wait(x_biased, 1)
                for i in range(NT):
                    add_residuals(1, i, 4 + i % 4)

                begins(dve, b, "xproj")
                for d in range(DTL):
                    xr = PS[:, 2 * (d % 2):2 * (d % 2) + 2, :].rearrange("p a n -> p (a n)")
                    wait(conv0, d + 1)
                    for j in range(1, TAPS):
                        ins = V.scalar_tensor_tensor(out=conv_t[d % 2][:, j:T], in0=xr[:, 0:T - j],
                                                     scalar=conv_w[:, d, TAPS - 1 - j:TAPS - j],
                                                     in1=conv_t[d % 2][:, j:T], op0=ALU.mult, op1=ALU.add)
                        if j < TAPS - 1:
                            own_(ins)
                        else:
                            conv_done.step(ins)
                psb = PS[:, 6:8, :].rearrange("p a n -> p (a n)")
                wait(x_rows_ready, 1)
                own_(V.tensor_copy(b_piece, psb))
                own_(V.scalar_tensor_tensor(out=b_rest, in0=b_piece, scalar=less[:, 0:1], in1=psb,
                                            op0=ALU.mult, op1=ALU.add))
                own_(V.tensor_copy(b_piece, b_rest))
                b_split.step(V.scalar_tensor_tensor(out=b_st[:, :], in0=b_piece, scalar=less[:, 1:2], in1=b_rest,
                                                    op0=ALU.mult, op1=ALU.add))

                def lost_in_sum(d):
                    e, c = sp_e[d], sp_c[d % 2]
                    wait(dt_exp, d + 1)
                    if d >= 2:
                        wait(dt_sum, d - 1)
                    own_(V.tensor_scalar(c, e, 1.0, -1.0, ALU.add, ALU.add))
                    dt_corr.step(V.tensor_tensor(c, e, c, ALU.subtract))

                def times_d(i):
                    wait(d_psum, i + 1)
                    d_read.step(V.tensor_tensor(y_s[:, i], PS[:, 5 + i % 3, :], d_all[:, :], ALU.mult))

                wait(c_psum, 1)
                V.tensor_copy(c_t[:, :, :], PS[:, 4, 0:NT * 2 * S].rearrange("p (i s) -> p i s", i=NT)[:, :, S:2 * S])
                times_d(0)
                lost_in_sum(0)
                times_d(1)
                times_d(2)
                lost_in_sum(1)
                times_d(3)
                times_d(4)
                lost_in_sum(2)
                times_d(5)
                times_d(6)
                lost_in_sum(3)
                times_d(7)
                for d in range(DTL):
                    wait(dt_ln, d + 1)
                    wait(dt_sum, d + 1)
                    dt_ready.step(V.tensor_tensor(dt_t[:, d], dt_t[:, d], sp_e[d], ALU.add))
                    wait(dt_ready, d + 1)
                    dtx_ready.step(V.tensor_tensor(dtx[:, d], dt_t[:, d], xs[:, d], ALU.mult))


                def add_y(s, i):
                    n = s * NT + i
                    wait(h_T, n + 1)
                    if s:
                        wait(y_added, n - NT + 1)
                    y_added.step(V.scalar_tensor_tensor(out=y_s[:, i], in0=PS[:, n % HBANKS, :],
                                                        scalar=c_t[:, i, s:s + 1], in1=y_s[:, i],
                                                        op0=ALU.mult, op1=ALU.add))

                for s in range(S):
                    for d in range(DTL):
                        n = s * DTL + d
                        wait(a_ready, n + 1)
                        wait(u_ready, n + 1)
                        if n >= HRING:
                            wait(h_T, ((n - HRING) // DTL + 1) * NT)
                        h_ready.step(V.tensor_tensor_scan(h_r[n % HRING], a_r[n % 2], u_r[n % 2], 0.0,
                                                          ALU.mult, ALU.add))
                        if s:
                            for i in range(d * NT // DTL, (d + 1) * NT // DTL):
                                add_y(s - 1, i)

                add_y(S - 1, 0)
                for i in range(NT + 2):
                    if i + 1 < NT:
                        add_y(S - 1, i + 1)
                    if i < NT:
                        wait(z_ready, i + 1)
                        wait(y_added, (S - 1) * NT + i + 1)
                        if i >= 2:
                            wait(ygT_psum, i - 1)
                        if i < NT - 1:
                            yg_ready.step(V.tensor_tensor(yg[i % 2], y_s[:, i], z_tiles[i], ALU.mult))
                        else:
                            yg_ready.step(V.tensor_tensor(yg[i % 2].rearrange("p (k n) -> p k n", k=CT),
                                                          y_s[:, i].rearrange("p (k n) -> p k n", k=CT),
                                                          z_tiles[i], ALU.mult))
                    if i >= 2:
                        add_residuals(2, i - 2, OUT_BANKS[i % 2])

                begins(dve, b, "ffn1")
                wait(x_biased, 2)
                for i in range(NT):
                    add_residuals(3, i, 4 + i % 4)
                wait(x_added, 4 * NT)

        @block.tensor
        def _(pe):
            mm, tr = nc.tensor.matmul, nc.tensor.transpose
            pe.wait_ge(ev("pre_loads"), 16 * N_LOADS)
            pe.wait_ge(ev("bd_ready"), 4)
            for k in range(CT):
                for m in range(3):
                    w = 32 if m == 2 else 48
                    for a in range(8):
                        last = mm(PS[:, 4 + k if m == 2 else 2 * m + k, a * w:(a + 1) * w],
                                  wT[:, m, a, k * P:(k + 1) * P], bd[:, m, 0:w], start=True, stop=True)
            last.then_inc(ev("fold_psum"), 1)
            pe.wait_ge(ev("folded"), 1)
            pe.wait_ge(ev("c_silu"), 1)
            for l in range(2):
                for n in range(3):
                    for k in range(CT):
                        last = mm(PS[0:B, 3 * l + n, :], cT[:, l, k, :], wmod[:, l, k, n * 512:(n + 1) * 512],
                                  start=(k == 0), stop=(k == CT - 1))
                last.then_inc(ev("mod_psum"), 1)
            pe.wait_ge(ev("mod_rows"), 1)
            pe.wait_ge(ev("made"), 14)
            for l in range(2):
                for n, kind in enumerate((1, 0, 4, 3)):
                    for k in range(CT):
                        c = kind * C + k * P
                        o = ((l * 4 + n) * CT + k) * B
                        last = tr(PS[:, 6, o:o + B], mod_row[:, l, c:c + P], ident[0:B, 0:B])
            last.then_inc(ev("mod_T"), 1)
            pe.wait_ge(ev("down_level"), LEVELS)
            D = w_con[:, :, :].rearrange("p f c -> p (f c)").rearrange("p (k n) -> p k n", k=CT)
            for f in range(FT):
                for k in range(CT):
                    tr(PS[:, f // 2, (f % 2) * C + k * P:(f % 2) * C + (k + 1) * P],
                       D[:, k, f * P:(f + 1) * P], ident[:, :])
            pe.wait_ge(ev("up_level"), LEVELS)
            for f in range(FT):
                last = mm(PS[:, 4, f:f + 1], bexp[0:1, f * P:(f + 1) * P], ones[0:1, 0:1], start=True, stop=True)
            last.then_inc(ev("down_T"), 1)
            pe.wait_ge(ev("bf_ready"), 1)

            with pe.Fori(0, B, 1) as b:
                def wait(c, n):
                    pe.wait_ge(c.sem, c.at(b, n))

                def ln(n, name):
                    for i in range(NT):
                        wait((xn_even, xn_odd)[i % 2], n * NT // 2 + i // 2 + 1)
                        for k in range(CT):
                            last = tr(PS[:, 2 * k + i // 4, (i % 4) * P:(i % 4 + 1) * P],
                                      xn[:, i, k * P:(k + 1) * P], ident[:, :])
                        hT_psum.step(last)
                    wait(hT_ready, (n + 1) * CT * NH)

                ln(0, "ln_a0")

                begins(pe, b, "qkv")
                for m in range(2):
                    for n in range(3):
                        bank = ((0, 2, 4), (6, 0, 2))[m][n]
                        if m and n == 1:
                            wait(rest1, 1)
                        if m and n == 2:
                            wait(qk_e_read, 1)
                        for g in range(NH):
                            for k in range(CT):
                                last = mm(PS[:, bank + g, :], w_qk[:, k, m, n, :], hT[:, k, g * HALF:(g + 1) * HALF],
                                          start=(k == 0), stop=(k == CT - 1))
                        qk_psum.step(last)
                for i in range(NT):
                    if i == 0:
                        wait(qk_r_read, 1)
                    if i == 2:
                        wait(rest1, 3)
                    if i >= 4:
                        wait(v_ready, i - 3)
                    for k in range(CT):
                        last = mm(PS[:, 4 + i % 4, 0:C], hT[:, k, i * P:(i + 1) * P], w_v[:, k, :],
                                  start=(k == 0), stop=(k == CT - 1))
                    v_psum.step(last)
                wait(qk_r_read, 2)

                begins(pe, b, "attend")
                wait(v_ready, NT)
                wait(stacks_in, 4 * len(PIECE_OF[0]) + 1)

                def scores_for_max(n):
                    h, q, a, z = SPARTS[n]
                    if n % MAXES == 0 and n:
                        wait(negm_split, n // MAXES)
                    ring = len(MAX_BANKS) if n < MAXES else 2
                    if n >= ring:
                        wait(smax_read, n - ring + 1)
                    bank = max_bank(n)
                    diag = z == (q + 1) * P
                    last = mm(PS[:, bank, 0:z - a], q_st[0:KROWS, h, q * P:(q + 1) * P], k_st[0:KROWS, h, a:z],
                              start=True, stop=not diag)
                    if diag:
                        last = mm(PS[:, bank, z - a - P:z - a], identb[:, :], mask_qk[:, :], start=False, stop=True)
                    smax_psum.step(last)

                def scores(g):
                    if g >= 2:
                        wait(p_ready, g - 1)
                    for n in range(PER_CHUNK):
                        h, q, k = BLOCKS[PER_CHUNK * g + n]
                        o = PS[:, 2 * (g % 2) + n // 4, (n % 4) * P:(n % 4 + 1) * P]
                        last = mm(o, k_st[0:NEAR, h, k * P:(k + 1) * P], q_st[0:NEAR, h, q * P:(q + 1) * P],
                                  start=True, stop=k < q)
                        if k == q:
                            last = mm(o, identb[:, :], mask_kq[:, :], start=False, stop=True)
                    s_psum.step(last)

                def turn(n):
                    wait(oT_ready, n + 1)
                    if n:
                        wait(o_read, n)
                    for i in range(4):
                        last = tr(PS[:, 5, i * P:(i + 1) * P], oT[0][:, i * P:(i + 1) * P], ident[:, :])
                    o_psum.step(last)

                def times_v(g):
                    wait(p_ready, g + 1)
                    for n in range(PER_CHUNK * g, PER_CHUNK * (g + 1)):
                        h, q, k = BLOCKS[n]
                        half, r = NH * (h // HG) + q // 4, 32 * (h % HG)
                        if half and k == 0 and q % 4 == 0 and r == 0:
                            wait(oT_ready, half)
                        v = (k * H + h) * (DH + 1)
                        last = mm(PS[r:r + 32, 4, (q % 4) * P:(q % 4 + 1) * P], v_flat[:, v:v + 32],
                                  pT[(n // PER_CHUNK) % P_RING][:, (n % PER_CHUNK) * P:(n % PER_CHUNK + 1) * P],
                                  start=(k == 0), stop=(k == q), tile_position=(0, r))
                    pv_done.step(last)

                for st in range(STEPS):
                    hg, j = divmod(st, GROUP_CHUNKS)
                    g = st - GROUP_CHUNKS
                    if 0 <= g < CHUNKS:
                        if g % GROUP_CHUNKS == 0:
                            wait(negm_in, PIECES * (g // GROUP_CHUNKS + 1))
                        scores(g)
                    if hg < H // HG and j < MAX_STEPS:
                        for n in range(4):
                            scores_for_max(hg * MAXES + 4 * j + n)
                    if hg < H // HG and j == MAX_STEPS:
                        wait(negm_ready, hg + 1)
                        negm_T.step(tr(PS[0:HG * NT, 6, 0:P], negm[:, :], ident[:, :]))
                    if g - LAG - 1 in half_ends:
                        turn(half_ends.index(g - LAG - 1))
                    if 0 <= g - LAG < CHUNKS:
                        times_v(g - LAG)

                begins(pe, b, "project")
                for g in range(NH):
                    for k in range(CT):
                        for i in range(4):
                            last = tr(PS[:, 2 * k + g, i * P:(i + 1) * P],
                                      y_at[:, 4 * g + i, k * P:(k + 1) * P], ident[:, :])
                        yT_psum.step(last)
                wait(w_g_ready, 1)
                for i in range(NT):
                    wait(yT_ready, CT * (i // 4 + 1))
                    if i >= 4:
                        wait(x_added, i - 3)
                    for k in range(CT):
                        last = mm(PS[:, 4 + i % 4, 0:C], yT[:, k, i * P:(i + 1) * P], w_g[:, k, :],
                                  start=(k == 0), stop=(k == CT - 1))
                    res_psum.step(last)
                ln(1, "ln_b0")

                begins(pe, b, "ffn0")
                for g in range(NH):
                    for k in range(CT):
                        last = mm(PS[M * g:M * g + M, 0, :], w_in0[:, k, :], hT[:, k, g * HALF:(g + 1) * HALF],
                                  start=(k == 0), stop=(k == CT - 1))
                s0_psum.step(last)
                for j in range(J):
                    wait(r0_ready, j + 1)
                    last = mm(PS[:, 1, :], diag_w2[:, j], r0[j % 4], start=(j == 0), stop=(j == J - 1))
                    r0_used.step(last)
                wait(g0_ready, 1)
                wait(w_g_ready, 2)
                for i in range(NT):
                    rows = slice(M * (i // 4), M * (i // 4) + M)
                    if i >= 4:
                        wait(x_added, NT + i - 3)
                    res_psum.step(mm(PS[:, 4 + i % 4, 0:C], g0[rows, (i % 4) * P:(i % 4 + 1) * P], w_g[rows, 0, :],
                                     start=True, stop=True))
                ln(2, "ln_a1")

                begins(pe, b, "xproj")

                def from_h(d):
                    if d >= 2:
                        wait(conv_done, d - 1)
                    for g in range(NH):
                        for k in range(CT):
                            last = mm(PS[:, 2 * (d % 2) + g, :], w_in1[:, k, d * P:(d + 1) * P],
                                      hT[:, k, g * HALF:(g + 1) * HALF], start=(k == 0), stop=(k == CT - 1))
                    xr_psum.step(last)

                def from_x(d):
                    wait(xs_ready, d + 1)
                    for g in range(NH):
                        last = mm(PS[:, 6 + g, :], w_x[:, d, :], xs[:, d, g * HALF:(g + 1) * HALF],
                                  start=(d == 0), stop=(d == DTL - 1))
                    if d == DTL - 1:
                        xd_psum.step(last)

                def to_dt(d):
                    if d >= 2:
                        wait(dt_max, d - 1)
                    for g in range(NH):
                        last = mm(PS[:, 2 * (d % 2) + g, :], w_dt[:, d * P:(d + 1) * P],
                                  x_rows[0:R, g * HALF:(g + 1) * HALF], start=True, stop=True)
                    dt_psum.step(last)

                def turn_x(i):
                    if i >= 3:
                        wait(d_read, i - 2)
                    for d in range(DTL):
                        last = tr(PS[:, 5 + i % 3, d * P:(d + 1) * P], xs[:, d, i * P:(i + 1) * P], ident[:, :])
                    d_psum.step(last)

                for d in range(DTL):
                    from_h(d)
                    if d >= 2:
                        from_x(d - 2)
                from_x(2)
                from_x(3)
                wait(x_rows_ready, 1)
                to_dt(0)
                for i in range(NT):
                    last = tr(PS[:, 4, i * 2 * S:(i + 1) * 2 * S], x_rows[R:XR, i * P:(i + 1) * P],
                              ident[R:XR, R:XR])
                c_psum.step(last)
                to_dt(1)
                turn_x(0)
                wait(b_split, 1)
                turn_x(1)
                to_dt(2)
                turn_x(2)
                turn_x(3)
                to_dt(3)
                for i in range(4, NT):
                    turn_x(i)

                def spread_b(s):
                    if s:
                        wait(bb_ready, s)
                    else:
                        wait(d_read, NT)
                    for g in range(NH):
                        last = mm(PS[:, 6 + g, :], sel[:, s], b_st[:, g * HALF:(g + 1) * HALF], start=True, stop=True)
                    bb_psum.step(last)

                spread_b(0)
                spread_b(1)
                for s in range(S):
                    if s % 2 == 0:
                        i = s // 2
                        if i:
                            wait(z_kept, i)
                        for k in range(CT):
                            last = mm(PS[:, ZBANK, :], hT[:, k, i * P:(i + 1) * P], w_in1[:, k, DI:2 * DI],
                                      start=(k == 0), stop=(k == CT - 1))
                        z_psum.step(last)
                    wait(h_ready, (s + 1) * DTL)
                    for i in range(NT):
                        n = s * NT + i
                        if i == 3 and s + 2 < S:
                            spread_b(s + 2)
                        if n >= HBANKS:
                            wait(y_added, n - HBANKS + 1)
                        for d in range(DTL):
                            last = tr(PS[:, n % HBANKS, d * P:(d + 1) * P],
                                      h_r[(s * DTL + d) % HRING][:, i * P:(i + 1) * P], ident[:, :])
                        h_T.step(last)
                wait(z_kept, NT)
                for i in range(NT + 2):
                    if i == 2:
                        wait(w_g_ready, 3)
                    if 1 <= i <= NT:
                        j = i - 1
                        wait(yg_ready, j + 1)
                        if j >= 2:
                            wait(ygT_ready, j - 1)
                        for d in range(DTL):
                            last = tr(PS[:, 6 + j % 2, d * P:(d + 1) * P], yg[j % 2][:, d * P:(d + 1) * P], ident[:, :])
                        ygT_psum.step(last)
                    if i >= 2:
                        j = i - 2
                        wait(ygT_ready, j + 1)
                        if j >= 2:
                            wait(x_added, 2 * NT + j - 1)
                        if j == 1:
                            wait(y_added, (S - 1) * NT + OUT_BANKS[1] + 1)
                        for d in range(DTL):
                            last = mm(PS[:, OUT_BANKS[j % 2], 0:C], ygT[j % 2][:, d], w_g[:, d, :],
                                      start=(d == 0), stop=(d == DTL - 1))
                        res_psum.step(last)
                ln(3, "ln_b1")

                begins(pe, b, "ffn1")
                for g in range(NH):
                    for f in range(FT):
                        n = g * FT + f
                        if n >= 4:
                            wait(f_ready, n - 3)
                        for k in range(CT):
                            last = mm(PS[:, n % 4, :], w_exp[:, k, f * P:(f + 1) * P], hT[:, k, g * HALF:(g + 1) * HALF],
                                      start=(k == 0), stop=(k == CT - 1))
                        f_psum.step(last)
                wait(w_g_ready, 4)
                for i in range(NT):
                    wait(f_ready, FT * (i // 4 + 1))
                    if i >= 4:
                        wait(x_added, 3 * NT + i - 3)
                    for f in range(FT):
                        last = mm(PS[:, 4 + i % 4, 0:C], gl[:, f, i * P:(i + 1) * P], w_g[:, f, :],
                                  start=(f == 0), stop=(f == FT - 1))
                    res_psum.step(last)
                wait(x_added, 4 * NT)

        wrong = {n: c.made for n, c in counts if c.made != c.per}
        assert not wrong, wrong


def butterfly_level(eng, x, k, s, w, tmp, transposed, step):
    n = x.shape[1] // k
    v = x.rearrange("p (a two s) -> p a two s", two=2, s=s)
    a, b = v[:, :, 0, :], v[:, :, 1, :]
    na = n // (2 * s)

    def weight(i, j):
        i, j = (j, i) if transposed else (i, j)
        return w[:, i, j, :].rearrange("p (a s) -> p a s", s=s)

    def tile(j):
        return tmp[j].rearrange("p k n -> p (k n)")[:, 0:k * n // 2].rearrange("p (a s) -> p a s", s=s)

    def times(dst, src, wt):
        for c in range(k):
            r = slice(c * na, (c + 1) * na)
            ins = eng.tensor_tensor(dst[:, r, :], src[:, r, :], wt, ALU.mult)
            if c < k - 1:
                step(ins)
        return ins

    t0, t1, t2 = (tile(j) for j in range(3))
    step(times(t0, a, weight(0, 0)))
    step(times(t1, b, weight(0, 1)))
    step(times(t2, a, weight(1, 0)))
    step(eng.tensor_tensor(a, t0, t1, ALU.add))
    step(times(t0, b, weight(1, 1)))
    return eng.tensor_tensor(b, t2, t0, ALU.add)


N_LOADS = 45

_LAYOUT = {
    "WqT": ("L0_attn_Wq_down", lambda a: a.T), "WkT": ("L0_attn_Wk_down", lambda a: a.T),
    "WvT": ("L0_attn_Wv_down", lambda a: a.T), "L0_cT": ("L0_c", lambda a: a.T), "L1_cT": ("L1_c", lambda a: a.T),
    "L1_attn_W_inT": ("L1_attn_W_in", lambda a: a.T), "L1_attn_W_xT": ("L1_attn_W_x", lambda a: a.T),
    "L1_attn_W_dtT": ("L1_attn_W_dt", lambda a: a.T), "L1_attn_W_outT": ("L1_attn_W_out", lambda a: a.T),
    "L1_ffn_W_conT": ("L1_ffn_W_con", lambda a: a.T),
    "conv_b": ("L1_attn_conv_b", lambda a: a.reshape(-1, P).T), "b_dt": ("L1_attn_b_dt", lambda a: a.reshape(-1, P).T),
    "up_bias": ("L1_ffn_up_bias", lambda a: a.reshape(-1, P).T),
    "up_w": ("L1_ffn_up_weights", lambda a: a.transpose(0, 2, 3, 1).reshape(a.shape[0], -1)),
    "down_w": ("L1_ffn_down_weights", lambda a: a.transpose(0, 2, 3, 1).reshape(a.shape[0], -1)),
}
_AS_THEY_COME = [
    "L0_attn_x", "L0_attn_Wq_up_c", "L0_attn_Wq_up_e", "L0_attn_Wk_up_c", "L0_attn_Wk_up_e", "L0_attn_Wv_up",
    "L0_attn_Wc", "L0_ffn_Win", "L0_ffn_bin_", "L0_ffn_W1", "L0_ffn_b1", "L0_ffn_W2", "L0_ffn_b2", "L0_ffn_Wout",
    "L0_ffn_bout", "L0_wmod", "L1_wmod", "L1_attn_conv_w", "L1_attn_A_log", "L1_ffn_W_exp", "L1_ffn_b_exp",
    "L1_ffn_b_con", "L1_ffn_down_bias", "L1_attn_D",
]


def kernel(**inputs):
    import numpy as np
    import concourse.bacc as _bacc
    from concourse import mybir as _mybir
    from concourse.bass_utils import run_bass_kernel_spmd as _run

    nc = _bacc.Bacc("TRN2", target_bir_lowering=False, num_devices=1)
    arrays, t = {}, {}

    def give(name, a):
        a = np.ascontiguousarray(a)
        arrays[f"in_{name}"] = a
        t[name] = nc.dram_tensor(f"in_{name}", a.shape, _mybir.dt.from_np(a.dtype), kind="ExternalInput").ap()

    for name in _AS_THEY_COME:
        give(name, np.asarray(inputs[name]))
    for name, (source, layout) in _LAYOUT.items():
        give(name, layout(np.asarray(inputs[source])))
    T, DE = inputs["L0_attn_x"].shape[1], 8
    inv = (1.0 / np.float32(10000.0) ** (np.arange(0, DE, 2, dtype=np.float32) / np.float32(DE))).astype(np.float32)
    angle = (np.arange(T, dtype=np.float32)[:, None] * inv[None, :]).astype(np.float32)
    rows = np.repeat(np.concatenate([angle, angle], axis=1).T, 16, axis=0)
    give("cos", np.cos(rows).astype(np.float32))
    give("sin", np.sin(rows).astype(np.float32))
    shape = inputs["L0_attn_x"].shape
    t["out"] = nc.dram_tensor("out_0", shape, _mybir.dt.float32, kind="ExternalOutput").ap()
    adaln_kernel(nc, t)
    r = _run(nc, [arrays], core_ids=[0])
    return r.results[0]["out_0"]
```

```python
from contextlib import ExitStack

import concourse.bass as bass
from concourse import mybir

P = 128
ALU = mybir.AluOpType
ACT = mybir.ActivationFunctionType
F32 = mybir.dt.float32
BF16 = mybir.dt.bfloat16
I32 = mybir.dt.int32
AX_X = mybir.AxisListType.X

MASKED = -1e30
LN_EPS = 1e-5
HALF = 512

OWN_STEPS = {"dve": 108, "pool": 2}


class Count:

    def __init__(self, sem, per, unit=1, start=0, early=0):
        self.sem, self.per, self.unit, self.start, self.early, self.made = sem, per, unit, start, early, 0

    def step(self, ins):
        self.made += 1
        ins.then_inc(self.sem, self.unit)

    def at(self, b, n):
        return b * (self.per * self.unit) + n * self.unit + self.start


def adaln_kernel(nc, t):
    B, T, C = t["out"].shape
    H, L, DH, DE = 16, 64, 16, 8
    NT, CT, NH = T // P, C // P, T // HALF
    SCALE = float(DH) ** -0.5
    M, J = t["L0_ffn_W1"].shape
    DI, TAPS = t["L1_attn_conv_w"].shape
    R = t["L1_attn_W_dtT"].shape[0]
    S = t["L1_attn_A_log"].shape[0]
    DTL = DI // P
    F = t["L1_ffn_W_exp"].shape[1]
    FT = F // P
    LEVELS = t["up_w"].shape[0]
    PIECES = 3
    PIECE_OF = ((0, 0, 0, 1, 1, 2), (0, 1, 2, 0, 1, 0))
    KROWS = len(PIECE_OF[0]) * DH
    NEAR = KROWS + PIECES
    HG = 4
    BLOCKS = [(g * HG + h, q, k) for g in range(H // HG) for q in range(NT) for k in range(q + 1) for h in range(HG)]
    PER_CHUNK = 8
    CHUNKS = len(BLOCKS) // PER_CHUNK
    SPARTS = [(h, q, a, min(a + HALF, (q + 1) * P)) for h in range(H) for q in range(NT)
              for a in range(0, (q + 1) * P, HALF)]
    half_ends = [n // PER_CHUNK for n, (h, q, k) in enumerate(BLOCKS) if k == q and q % 4 == 3 and h % HG == HG - 1]
    GROUP_CHUNKS, MAXES, LAG = CHUNKS * HG // H, len(SPARTS) * HG // H, 2
    MAX_PER_STEP, LEAD = 4, 16
    MAX_STEPS = MAXES // MAX_PER_STEP
    STEPS = LEAD + CHUNKS + LAG + 1
    J_PE = J - 6
    HRING, HBANKS, ZBANK = 7, 5, 5
    OUT_BANKS = (ZBANK, 3)
    assert ((S - 1) * NT + OUT_BANKS[1]) % HBANKS == OUT_BANKS[1] and OUT_BANKS[1] + HBANKS >= NT
    XR = R + 2 * S
    B_ROWS = (R, XR, XR + S)
    assert XR % 32 == 0 and XR + 2 * S == P
    MAX_BANKS = (6, 7, 0, 1, 2, 3)

    def max_bank(n):
        return MAX_BANKS[n % len(MAX_BANKS)] if n < MAXES else MAX_BANKS[n % 2]

    with ExitStack() as ctx:
        def sb(name, shape, dt=F32):
            return ctx.enter_context(nc.sbuf_tensor(name, shape, dt))

        sems = {}

        def ev(name):
            if name not in sems:
                sems[name] = ctx.enter_context(nc.semaphore(name))
            return sems[name]

        counts = []

        def count(name, per, unit=1, start=0, early=0):
            counts.append((name, Count(ev(name), per, unit, start, early)))
            return counts[-1][1]

        PS = ctx.enter_context(nc.psum_tensor("PS", [P, 8, 512], F32))

        ident = sb("ident", [P, P])
        identb = sb("identb", [P, P], BF16)
        mask_qk = sb("mask_qk", [P, P], BF16)
        mask_kq = sb("mask_kq", [P, P], BF16)
        ones = sb("ones", [P, 1])
        cos = sb("cos", [P, T])
        sin = sb("sin", [P, T])
        w_qk = sb("w_qk", [P, CT, 2, 3, H * DE])
        w_v = sb("w_v", [P, CT, C])
        w_c = sb("w_c", [P, CT, C])
        w_in0 = sb("w_in0", [P, CT, M])
        bin2 = sb("bin2", [P, 1])
        w1 = sb("w1", [P, J])
        b1 = sb("b1", [P, J])
        w2 = sb("w2", [P, J])
        diag_w2 = sb("diag_w2", [P, J_PE, P])
        b2 = sb("b2", [P, 1])
        w_out0 = sb("w_out0", [P, C])
        bias_out0 = sb("bias_out0", [P, C])
        w_in1 = sb("w_in1", [P, CT, 2 * DI])
        conv_w = sb("conv_w", [P, DTL, TAPS])
        conv_b = sb("conv_b", [P, DTL])
        a_neg = sb("a_neg", [P, S])
        d_all = sb("d_all", [P, DI])
        w_x = sb("w_x", [P, DTL, P])
        w_dt = sb("w_dt", [R, DI])
        b_dt = sb("b_dt", [P, DTL])
        w_out1 = sb("w_out1", [P, DTL, C])
        sel = sb("sel", [P, S, P], BF16)
        w_exp = sb("w_exp", [P, CT, F])
        gelu_b = sb("gelu_b", [P, FT])
        w_con = sb("w_con", [P, FT, C])
        bias_out1 = sb("bias_out1", [P, C])
        mod_col = sb("mod_col", [P, 2, 4, CT, B + 1])
        mod_b = sb("mod_b", [P, 2, 4, CT])
        gates = sb("gates", [P, 4, C])
        bias_g = sb("bias_g", [P, C])
        X = sb("X", [P, NT, C])
        hT = sb("hT", [P, CT, T])
        bn = sb("bn", [P, NT, 6])
        mv = sb("mv", [P, NT, 2])
        spare = sb("spare", [P, 1])
        less = sb("less", [P, 2])
        norm = sb("norm", [P, 6, NT])
        slots = sb("slots", [P, H * NT, 2])
        negm = sb("negm", [P, HG * NT])
        n_rest = sb("n_rest", [HG * NT, P])
        n_pieces = sb("n_pieces", [HG * NT, PIECES, P], BF16)
        recip = sb("recip", [P, 2, NT])
        c_t = sb("c_t", [P, NT, S])
        b_st = sb("b_st", [P, T], BF16)

        z_first = sb("z_first", [P, 5, DI])
        z_tiles = [z_first[:, i] for i in range(5)]
        z_tiles += [hT[:, k, 0:DI] for k in range(CT)] + [hT[:, :, DI:DI + DI // CT]]
        x_in = z_first[:, :, :].rearrange("p i d -> p (i d)")[:, 0:NT * C].rearrange("p (i c) -> p i c", i=NT)
        assert len(z_tiles) == NT and DI + DI // CT <= 6 * P

        ARENA = 25856
        arena = sb("arena", [P, ARENA])

        def part(at, cols, dt=F32, rows=P):
            words = cols if dt == F32 else cols // 2
            assert at + words <= ARENA, (at, words)
            v = arena[0:rows, at:at + words]
            return v if dt == F32 else v.bitcast(dt)

        at = 0
        bd = part(at, 3 * 48).rearrange("p (m n) -> p m n", m=3)
        at += 144
        wT = part(at, 3 * 8 * C).rearrange("p (m k c) -> p m k c", m=3, k=8)
        mod_row = part(at, 2 * 6 * C, rows=B).rearrange("p (l n) -> p l n", l=2)
        at += 3 * 8 * C
        cT = part(at, 2 * CT * B).rearrange("p (l k b) -> p l k b", l=2, k=CT)
        at += 2 * CT * B
        wmod = part(at, 2 * CT * 6 * C).rearrange("p (l k n) -> p l k n", l=2, k=CT)
        at += 2 * CT * 6 * C
        bf_w = {n: [v.rearrange("p (i j n) -> p i j n", i=2, j=2) for v in (
                part(at + 2048 * i, 4 * (F // 2)), other[:, :, :].rearrange("p a n -> p (a n)"))]
                for i, (n, other) in enumerate((("up", X), ("down", hT)))}
        at += 4096
        bf_t = [[part(at + 1024 * (3 * i + j), CT * F // 2).rearrange("p (k n) -> p k n", k=CT)
                 for j in range(3)] for i in range(2)]
        at += 6144
        bexp = part(at, F)
        at += F
        ones_row = part(at, 384, BF16)
        at += 192
        dn_bias = part(at, C)
        up_bias = part(at + C, FT)
        xn = part(10240, NT * C).rearrange("p (i c) -> p i c", i=NT)
        q_st = part(0, H * T, BF16).rearrange("p (h t) -> p h t", h=H)
        k_st = part(8192, H * T, BF16).rearrange("p (h t) -> p h t", h=H)
        V_COLS = NT * H * (DH + 1)
        v_flat = part(16384, V_COLS + 16)
        v_aug = v_flat[:, 0:V_COLS].rearrange("p (i h d) -> p i h d", i=NT, h=H)
        P_AT, P_RING = 16384 + V_COLS + 16, 4
        rope_e, rope_r, qk_rest, pieces = [], [], [], []
        for at in (8192, P_AT):
            rope_e.append(part(at, T))
            rope_r.append(part(at + T, T))
            qk_rest.append(part(at + 2 * T, 2 * T).rearrange("p (e t) -> p e t", e=2))
            pieces.append(part(at + 4 * T, PIECES * 2 * T, BF16).rearrange("p (n e t) -> p n e t", n=PIECES, e=2))
        pT = [part(P_AT + i * PER_CHUNK * P, PER_CHUNK * P) for i in range(P_RING)]
        y_at = part(P_AT + P_RING * PER_CHUNK * P, NT * C).rearrange("p (i c) -> p i c", i=NT)
        oT = [part(P_AT + P_RING * PER_CHUNK * P + NT * C + HALF * i, HALF) for i in range(1)]
        o_rec = recip[:, :, :].rearrange("p a i -> p (a i)").rearrange("p (i h) -> p i h", h=HG)
        w_g = part(8192, FT * C).rearrange("p (k c) -> p k c", k=FT)
        yT = part(0, CT * T).rearrange("p (k t) -> p k t", k=CT)
        s0, g0 = part(0, HALF), part(512, HALF)
        r0 = [part(1024 + HALF * i, HALF) for i in range(4)]
        r0_v = [part(3072 + HALF * i, HALF) for i in range(2)]
        g0_v = part(4096, HALF)
        h_r = [part(T * i, T) for i in range(HRING)]
        bb = [part(T * (HRING + i), T) for i in range(2)]
        xs = part(0, DTL * T).rearrange("p (d t) -> p d t", d=DTL)
        conv_t = [part(4096 + T * i, T) for i in range(2)]
        at = T * (HRING + 2)
        dt_t = part(at, DTL * T).rearrange("p (d t) -> p d t", d=DTL)
        dtx = part(at + DTL * T, DTL * T).rearrange("p (d t) -> p d t", d=DTL)
        y_s = part(at + 2 * DTL * T, NT * DI).rearrange("p (i d) -> p i d", i=NT)
        at += 3 * DTL * T
        a_r = [part(at + i * T, T) for i in range(2)]
        u_r = [part(at + (2 + i) * T, T) for i in range(2)]
        sp_e = [part(4096 + T * i, T) for i in (2, 3, 0, 1)]
        sp_c = [a_r[1], u_r[1]]
        x_rows = dtx[0:XR, 3]
        b_rest = dtx[:, 2]
        b_piece = dtx[:, 1].bitcast(BF16)[:, 0:T]
        yg = [part((2 + i) * DI, DI) for i in range(2)]
        ygT = [part((4 + i) * DI, DI).rearrange("p (d t) -> p d t", d=DTL) for i in range(2)]
        gl = part(0, FT * T).rearrange("p (f t) -> p f t", f=FT)

        def qk_psum_c(m):
            return PS[:, (0, 6)[m]:(0, 6)[m] + 2, :].rearrange("p a n -> p (a n)")

        def half_tiles(h):
            return slice(h * NT // NH, (h + 1) * NT // NH)

        def tokens(x, b, h):
            return x[b].rearrange("(i p) c -> p i c", p=P)[:, half_tiles(h), :]

        def dram(name, shape, dt=F32):
            return nc.dram_tensor(name, shape, dt, kind="Internal").ap()

        gate_d = dram("gate_d", (4, B, C))
        ones_d = dram("ones_d", (P, 384), BF16)

        x_loaded = [count(f"x_loaded_{h}", 1, 16, early=1) for h in range(NH)]
        g_loaded = count("g_loaded", 1, 16)
        x_stored = [count(f"x_stored_{h}", 1, 16, start=16) for h in range(NH)]
        mod_b_ready = count("mod_b_ready", 1, early=1)
        own = {e: count(f"{e}_own", OWN_STEPS[e]) for e in OWN_STEPS}
        norm_ready = count("norm_ready", 4, early=1)
        xn_even = count("xn_even", 4 * NT // 2, early=NT // 2)
        xn_odd = count("xn_odd", 4 * NT // 2, early=NT // 2)
        hT_psum = count("hT_psum", 4 * NT, early=NT)
        hT_ready = count("hT_ready", 4 * CT * NH, early=CT * NH)
        qk_psum = count("qk_psum", 6)
        qk_e_read = count("qk_e_read", 2)
        qk_r_read = count("qk_r_read", 2)
        v_psum = count("v_psum", NT)
        v_ready = count("v_ready", NT)
        roped = count("roped", 2)
        piece1 = count("piece1", 4)
        rest1 = count("rest1", 4)
        piece2 = count("piece2", 4)
        piece3 = count("piece3", 4)
        stacks_in = count("stacks_in", 4 * len(PIECE_OF[0]) + 1, 16)
        smax_psum = count("smax_psum", len(SPARTS))
        smax_read = count("smax_read", len(SPARTS))
        negm_ready = count("negm_ready", H // HG)
        negm_T = count("negm_T", H // HG)
        negm_split = count("negm_split", H // HG)
        negm_in = count("negm_in", PIECES * H // HG, 16)
        s_psum = count("s_psum", CHUNKS)
        p_ready = count("p_ready", CHUNKS)
        pv_done = count("pv_done", CHUNKS)
        oT_ready = count("oT_ready", NH * H // HG)
        o_psum = count("o_psum", NH * H // HG)
        o_read = count("o_read", NH * H // HG)
        yT_psum = count("yT_psum", CT * NH)
        yT_ready = count("yT_ready", CT * NH)
        w_g_ready = count("w_g_ready", 4)
        x_biased = count("x_biased", 2)
        res_psum = count("res_psum", 4 * NT)
        x_added = count("x_added", 4 * NT, start=1)
        s0_psum = count("s0_psum", 1)
        s0_ready = count("s0_ready", 1)
        r0_ready = count("r0_ready", J_PE)
        r0_used = count("r0_used", J_PE)
        g0_ready = count("g0_ready", 1)
        xr_psum = count("xr_psum", DTL)
        conv0 = count("conv0", DTL)
        conv_done = count("conv_done", DTL)
        xs_ready = count("xs_ready", DTL)
        xd_psum = count("xd_psum", 1)
        x_rows_ready = count("x_rows_ready", 1)
        b_split = count("b_split", 1)
        c_psum = count("c_psum", 1)
        dt_psum = count("dt_psum", DTL)
        dt_max = count("dt_max", DTL)
        dt_abs = count("dt_abs", DTL)
        dt_exp = count("dt_exp", DTL)
        dt_ln = count("dt_ln", DTL)
        dt_corr = count("dt_corr", DTL)
        dt_sum = count("dt_sum", DTL)
        dt_ready = count("dt_ready", DTL)
        dtx_ready = count("dtx_ready", DTL)
        d_psum = count("d_psum", NT)
        d_read = count("d_read", NT)
        bb_psum = count("bb_psum", S)
        bb_ready = count("bb_ready", S)
        a_ready = count("a_ready", S * DTL)
        u_ready = count("u_ready", S * DTL)
        h_ready = count("h_ready", S * DTL)
        h_T = count("h_T", S * NT)
        y_added = count("y_added", S * NT)
        z_psum = count("z_psum", NT)
        z_kept = count("z_kept", NT)
        z_ready = count("z_ready", NT)
        yg_ready = count("yg_ready", NT)
        ygT_psum = count("ygT_psum", NT)
        ygT_ready = count("ygT_ready", NT)
        f_psum = count("f_psum", FT * NH)
        f_ready = count("f_ready", FT * NH)

        last_of = {
            "ln_a0": [(hT_ready, CT * NH)],
            "qkv": [(piece3, 4), (v_ready, NT)],
            "attend": [(o_read, NH * H // HG)],
            "project": [(x_added, NT)],
            "ln_b0": [(hT_ready, 2 * CT * NH)],
            "ffn0": [(x_added, 2 * NT)],
            "ln_a1": [(hT_ready, 3 * CT * NH)],
            "xproj": [(d_read, NT), (dtx_ready, DTL)],
            "out": [(x_added, 3 * NT)],
            "ln_b1": [(hT_ready, 4 * CT * NH)],
            "ffn1": [],
        }

        def begins(eng, b, name):
            names = list(last_of)
            for c, n in last_of[names[names.index(name) - 1]]:
                eng.wait_ge(c.sem, c.at(b, n))

        def own_step(engine, eng, b, ins):
            o = own[engine]
            o.step(ins)
            eng.wait_ge(o.sem, o.at(b, o.made))

        block = ctx.enter_context(nc.Block())

        @block.sync
        def _(sp):
            for dst, src in (
                    (w_con[:, :, :].rearrange("p f c -> p (f c)").rearrange("p (k n) -> p k n", k=CT),
                     t["L1_ffn_W_conT"].rearrange("(k p) n -> p k n", p=P)),
                    (w_exp[:, :, :], t["L1_ffn_W_exp"].rearrange("(k p) n -> p k n", p=P)),
                    (bexp, t["L1_ffn_b_exp"].partition_broadcast(P)),
                    (up_bias, t["up_bias"]),
                    (bias_out1[:, :], t["L1_ffn_b_con"].partition_broadcast(P)),
                    (dn_bias, t["L1_ffn_down_bias"].partition_broadcast(P))):
                sp.dma_start(dst, src).then_inc(ev("ffn1_loads"), 16)
            for i in range(LEVELS):
                for side, (name, level) in enumerate((("down", LEVELS - 1 - i), ("up", i))):
                    if i >= 2:
                        sp.wait_ge(ev(f"{name}_level"), i - 1)
                    sp.dma_start(bf_w[name][i % 2].rearrange("p i j n -> p (i j n)"),
                                 t[f"{name}_w"][level].partition_broadcast(P)).then_inc(ev(f"{name}_weights_{i % 2}"), 16)
            sp.wait_ge(ev("ones_row_set"), 1)
            sp.dma_start(ones_d, ones_row).then_inc(ev("ones_out"), 16)
            sp.wait_ge(ev("mod_rows"), 1)
            for g in range(4):
                l, kind = g // 2, (2, 5)[g % 2]
                sp.dma_start(gate_d[g], mod_row[:, l, kind * C:kind * C + C]).then_inc(ev("gates_out"), 16)
            sp.wait_ge(ev("ones_out"), 16)

            with sp.Fori(0, B, 1) as b:
                ROWS = len(PIECE_OF[0])
                value = {(c.sem.name, n): sp.snap(c.at(b, n)) for c, n in (
                    *[(piece3, u + 1) for u in range(4)], (piece1, 4), (piece2, 4), (stacks_in, 2 * ROWS),
                    *[(negm_split, hg + 1) for hg in range(H // HG)])}

                def wait(c, n):
                    sp.wait_ge(c.sem, value[c.sem.name, n])

                def stack_piece(m, n, e):
                    stack = (q_st, k_st)[m]
                    for i in range(ROWS):
                        if PIECE_OF[m][i] == n:
                            row = DH * i + DE * e
                            stacks_in.step(sp.dma_start(stack[row:row + DE], pieces[m][:, n, e, :]))

                for e in range(2):
                    wait(piece3, e + 1)
                    for n in range(PIECES):
                        stack_piece(0, n, e)
                wait(stacks_in, 2 * ROWS)
                stacks_in.step(sp.dma_start(k_st[KROWS:NEAR].rearrange("n h t -> n (h t)"),
                                            ones_d.rearrange("a c -> (a c)").rearrange("(n x) -> n x", n=PIECES)))
                wait(piece3, 3)
                for n in range(PIECES):
                    stack_piece(1, n, 0)
                for n in range(PIECES):
                    wait((piece1, piece2, piece3)[n], 4)
                    stack_piece(1, n, 1)
                for hg in range(H // HG):
                    wait(negm_split, hg + 1)
                    for n in range(PIECES):
                        row = KROWS + n
                        negm_in.step(sp.dma_start(
                            q_st[row:row + 1, hg * HG:(hg + 1) * HG].rearrange("n h t -> n (h t)"),
                            n_pieces[:, n, :]))

        @block.gpsimd
        def _(pool):
            pool.memset(bd.rearrange("p m n -> p (m n)"), 0.0).then_inc(ev("cleared"), 1)
            pool.memset(w_x[:, :, :], 0.0).then_inc(ev("cleared"), 1)
            pool.memset(ident[:, :], 0.0).then_inc(ev("made"), 1)
            pool.memset(mask_qk[:, :], 0.0).then_inc(ev("made"), 1)
            pool.memset(mask_kq[:, :], 0.0).then_inc(ev("made"), 1)
            pool.memset(sel[:, :, :], 0.0).then_inc(ev("made"), 1)
            pool.memset(ones[:, :], 1.0).then_inc(ev("made"), 1)
            pool.memset(slots[:, :, :], MASKED).then_inc(ev("made"), 1)
            pool.memset(mod_col[:, :, :, :, B:B + 1].rearrange("p l n k b -> p (l n k) b"),
                        0.0).then_inc(ev("mod_end"), 1)
            pool.memset(ones_row, 1.0).then_inc(ev("ones_row_set"), 1)
            pool.wait_ge(ev("made"), 6)
            pool.affine_select(out=ident[:, :], in_=ident[:, :], compare_op=ALU.not_equal, fill=1.0, base=0,
                               pattern=[[-1, P]], channel_multiplier=1).then_inc(ev("made"), 1)
            pool.affine_select(out=mask_qk[:, :], in_=mask_qk[:, :], compare_op=ALU.is_ge, fill=MASKED, base=0,
                               pattern=[[-1, P]], channel_multiplier=1).then_inc(ev("made"), 1)
            pool.affine_select(out=mask_kq[:, :], in_=mask_kq[:, :], compare_op=ALU.is_ge, fill=MASKED, base=0,
                               pattern=[[1, P]], channel_multiplier=-1).then_inc(ev("made"), 1)
            for q in range(PIECES):
                pool.affine_select(out=sel[:, :, :], in_=sel[:, :, :], compare_op=ALU.not_equal, fill=1.0,
                                   base=-B_ROWS[q], pattern=[[-1, S], [0, P]],
                                   channel_multiplier=1).then_inc(ev("made"), 1)
                pool.wait_ge(ev("made"), 10 + q)
            for q in range(2):
                pool.memset(less[:, q:q + 1], -1.0).then_inc(ev("less_set"), 1)
                pool.wait_ge(ev("less_set"), 2 * q + 1)
                pool.affine_select(out=less[:, q:q + 1], in_=less[:, q:q + 1], compare_op=ALU.is_ge, fill=0.0,
                                   base=-B_ROWS[q + 1], pattern=[[0, 1]],
                                   channel_multiplier=1).then_inc(ev("less_set"), 1)
            pool.tensor_copy(identb[:, :], ident[:, :]).then_inc(ev("made"), 1)
            pool.wait_ge(ev("ffn1_loads"), 16 * 6)
            pool.tensor_tensor(bias_out1[:, :], bias_out1[:, :], dn_bias, ALU.add).then_inc(ev("made"), 1)
            steps = [0]

            def low(ins):
                steps[0] += 1
                ins.then_inc(ev("low"), 1)

            def low_done():
                pool.wait_ge(ev("low"), steps[0])

            D = w_con[:, :, :].rearrange("p f c -> p (f c)")
            for i in range(LEVELS):
                s = 2 ** (LEVELS - 1 - i)
                pool.wait_ge(ev(f"down_weights_{i % 2}"), 16 * (i // 2 + 1))
                last = butterfly_level(pool, D, CT, s, bf_w["down"][i % 2], bf_t[1], True, low, low_done)
                last.then_inc(ev("down_level"), 1)
                pool.wait_ge(ev("down_level"), i + 1)

            with pool.Fori(0, B, 1) as b:
                pool.wait_ge(g_loaded.sem, g_loaded.at(b, 1))
                begins(pool, b, "project")
                ins = pool.tensor_tensor(w_g[:, 0:CT, :], w_c[:, :, :],
                                         gates[:, 0:1, :].broadcast_to([P, CT, C]), ALU.mult)
                w_g_ready.step(ins)
                pool.wait_ge(w_g_ready.sem, w_g_ready.at(b, 1))

                begins(pool, b, "ffn0")
                w_g_ready.step(pool.tensor_tensor(w_g[:, 0, :], w_out0[:, :], gates[:, 1, :], ALU.mult))
                own_step("pool", pool, b, pool.tensor_tensor(bias_g[:, :], bias_out0[:, :], gates[:, 1, :], ALU.mult))
                x_biased.step(pool.tensor_tensor(X[:, :, :], X[:, :, :],
                                                 bias_g[:, :].unsqueeze(1).broadcast_to([P, NT, C]), ALU.add))
                pool.wait_ge(x_biased.sem, x_biased.at(b, 1))

                begins(pool, b, "xproj")
                for d in range(DTL):
                    pool.wait_ge(dt_corr.sem, dt_corr.at(b, d + 1))
                    pool.wait_ge(dt_max.sem, dt_max.at(b, d + 1))
                    dt_sum.step(pool.tensor_tensor(dt_t[:, d], dt_t[:, d], sp_c[d % 2], ALU.add))

                pool.wait_ge(dt_sum.sem, dt_sum.at(b, DTL))

                for s in range(S):
                    pool.wait_ge(bb_ready.sem, bb_ready.at(b, s + 1))
                    for d in range(DTL):
                        n = s * DTL + d
                        if s == 0:
                            pool.wait_ge(dtx_ready.sem, dtx_ready.at(b, d + 1))
                        if n >= 2:
                            pool.wait_ge(h_ready.sem, h_ready.at(b, n - 1))
                        u_ready.step(pool.tensor_tensor(u_r[n % 2], dtx[:, d], bb[(s + 1) % 2], ALU.mult))

                pool.wait_ge(u_ready.sem, u_ready.at(b, S * DTL))
                w_g_ready.step(pool.tensor_tensor(w_g[:, 0:DTL, :], w_out1[:, :, :],
                                                  gates[:, 2:3, :].broadcast_to([P, DTL, C]), ALU.mult))

                begins(pool, b, "ffn1")
                w_g_ready.step(pool.tensor_tensor(w_g[:, :, :], w_con[:, :, :],
                                                  gates[:, 3:4, :].broadcast_to([P, FT, C]), ALU.mult))
                own_step("pool", pool, b, pool.tensor_tensor(bias_g[:, :], bias_out1[:, :], gates[:, 3, :], ALU.mult))
                x_biased.step(pool.tensor_tensor(X[:, :, :], X[:, :, :],
                                                 bias_g[:, :].unsqueeze(1).broadcast_to([P, NT, C]), ALU.add))
                pool.wait_ge(x_biased.sem, x_biased.at(b, 2))

        @block.scalar
        def _(act):
            A = nc.scalar.activation
            for c in x_stored:
                act.sem_inc(c.sem, c.start)
            act.sem_inc(x_added.sem, x_added.start)
            loads = [0]

            def pre(dst, src):
                loads[0] += 1
                act.dma_start(dst, src).then_inc(ev("pre_loads"), 16)

            act.wait_ge(ev("cleared"), 2)
            for m, n in enumerate("qkv"):
                pre(wT[:, m], t[f"W{n}T"].rearrange("(k p) c -> p k c", p=P))
            for h in range(2):
                rows = slice(L * h, L * h + L)
                for m, n in enumerate("qk"):
                    pre(bd[rows, m, DE * h:DE * h + DE], t[f"L0_attn_W{n}_up_c"])
                    pre(bd[rows, m, 16 + DE * h:16 + DE * h + DE], t[f"L0_attn_W{n}_up_e"])
                pre(bd[rows, 2, DH * h:DH * h + DH], t["L0_attn_Wv_up"])
                pre(bin2[rows, :], t["L0_ffn_bin_"].rearrange("(m o) -> m o", o=1))
                pre(b2[rows, :], t["L0_ffn_b2"].rearrange("(m o) -> m o", o=1))
                pre(w1[rows, :], t["L0_ffn_W1"])
                pre(b1[rows, :], t["L0_ffn_b1"])
                pre(w2[rows, :], t["L0_ffn_W2"])
                pre(w_out0[rows, :], t["L0_ffn_Wout"])
            for l in range(2):
                pre(cT[:, l], t[f"L{l}_cT"].rearrange("(k p) b -> p k b", p=P))
                pre(wmod[:, l], t[f"L{l}_wmod"].rearrange("(k p) n -> p k n", p=P))
            pre(cos[:, :], t["cos"])
            pre(sin[:, :], t["sin"])
            pre(w_c[:, :, :], t["L0_attn_Wc"].rearrange("(k p) n -> p k n", p=P))
            pre(w_in0[:, :, :], t["L0_ffn_Win"].rearrange("(k p) n -> p k n", p=P))
            pre(bias_out0[:, :], t["L0_ffn_bout"].partition_broadcast(P))
            pre(w_in1[:, :, :], t["L1_attn_W_inT"].rearrange("(k p) n -> p k n", p=P))
            pre(conv_w[:, :, :], t["L1_attn_conv_w"].rearrange("(k p) n -> p k n", p=P))
            pre(conv_b[:, :], t["conv_b"])
            pre(b_dt[:, :], t["b_dt"])
            pre(d_all[:, :], t["L1_attn_D"].partition_broadcast(P))
            pre(a_neg[:, :], t["L1_attn_A_log"].partition_broadcast(P))
            w_xT = t["L1_attn_W_xT"].rearrange("(k p) n -> p k n", p=P)
            pre(w_x[:, :, 0:R + 2 * S], w_xT)
            for q in range(1, PIECES):
                pre(w_x[:, :, B_ROWS[q]:B_ROWS[q] + S], w_xT[:, :, R:R + S])
            pre(w_dt[:, :], t["L1_attn_W_dtT"])
            pre(w_out1[:, :, :], t["L1_attn_W_outT"].rearrange("(k p) n -> p k n", p=P))
            assert loads[0] == N_LOADS, loads[0]
            act.wait_ge(ev("pre_loads"), 16 * N_LOADS)
            A(cT, cT, ACT.Silu).then_inc(ev("c_silu"), 1)
            A(a_neg[:, :], a_neg[:, :], ACT.Exp).then_inc(ev("a_exp"), 1)
            act.wait_ge(ev("a_exp"), 1)
            A(a_neg[:, :], a_neg[:, :], ACT.Copy, scale=-1.0).then_inc(ev("a_exp"), 1)
            act.wait_ge(ev("mod_psum"), 2)
            for l in range(2):
                for n in range(3):
                    last = A(mod_row[:, l, n * 512:n * 512 + 512], PS[0:B, 3 * l + n, :], ACT.Copy)
            last.then_inc(ev("mod_copied"), 1)
            act.wait_ge(ev("a_exp"), 2)
            act.wait_ge(ev("gates_out"), 64)
            act.wait_ge(ev("ones_out"), 16)
            act.wait_ge(ev("bf_ready"), 1)

            def load_x(b):
                for h in range(NH):
                    x_loaded[h].step(act.dma_start(x_in[:, half_tiles(h), :], tokens(t["L0_attn_x"], b, h)))

            def ln(b, n):
                x, l, kind = (X if n % 4 else x_in), n % 4 // 2, (n % 2) * 2
                act.wait_ge(mod_b_ready.sem, mod_b_ready.at(b, n // 4 + 1))
                act.wait_ge(norm_ready.sem, norm_ready.at(b, n + 1))
                for i in range(1, NT, 2):
                    xn_odd.step(A(xn[:, i], x[:, i], ACT.Identity, bias=norm[:, 5, i:i + 1],
                                  scale=norm[:, 4, i:i + 1]))
                for g in range(NH):
                    act.wait_ge(hT_psum.sem, hT_psum.at(b, n * NT + (g + 1) * NT // NH))
                    for k in range(CT):
                        hT_ready.step(A(hT[:, k, g * HALF:(g + 1) * HALF], PS[:, 2 * k + g, :], ACT.Identity,
                                        bias=mod_b[:, l, kind + 1, k:k + 1], scale=mod_b[:, l, kind, k:k + 1]))
                act.wait_ge(hT_ready.sem, hT_ready.at(b, (n + 1) * CT * NH))

            load_x(0)
            ln(0, 0)

            with act.Fori(0, B, 1) as b:
                act.wait_ge(x_added.sem, x_added.at(b, 0))
                g_loaded.step(act.dma_start(gates[:, :, :], gate_d[:, b].partition_broadcast(P)))

                begins(act, b, "qkv")

                def first_piece(u):
                    m, e = divmod(u, 2)
                    if e:
                        act.wait_ge(roped.sem, roped.at(b, m + 1))
                        src = rope_e[m]
                    else:
                        act.wait_ge(qk_psum.sem, qk_psum.at(b, 3 * m + 1))
                        src = qk_psum_c(m)
                    piece1.step(A(pieces[m][:, 0, e], src, ACT.Copy))

                def second_piece(u):
                    m, e = divmod(u, 2)
                    act.wait_ge(rest1.sem, rest1.at(b, u + 1))
                    piece2.step(A(pieces[m][:, 1, e], qk_rest[m][:, e], ACT.Copy))

                first_piece(0)
                second_piece(0)
                first_piece(1)
                first_piece(2)
                second_piece(1)
                second_piece(2)
                first_piece(3)
                second_piece(3)
                for i in range(NT):
                    act.wait_ge(v_psum.sem, v_psum.at(b, i + 1))
                    ins = A(v_aug[:, i, :, 0:DH], PS[:, 4 + i % 4, 0:C].rearrange("p (h d) -> p h d", h=H), ACT.Copy)
                    v_ready.step(ins)
                act.wait_ge(v_ready.sem, v_ready.at(b, NT))

                begins(act, b, "attend")
                for g in range(CHUNKS):
                    act.wait_ge(s_psum.sem, s_psum.at(b, g + 1))
                    if g >= P_RING:
                        act.wait_ge(pv_done.sem, pv_done.at(b, g - P_RING + 1))
                    ins = A(pT[g % P_RING], PS[:, 2 * (g % 2):2 * (g % 2) + 2, :].rearrange("p a n -> p (a n)"),
                            ACT.Exp, scale=SCALE)
                    p_ready.step(ins)
                act.wait_ge(p_ready.sem, p_ready.at(b, CHUNKS))

                begins(act, b, "project")
                for g in range(NH):
                    for k in range(CT):
                        act.wait_ge(yT_psum.sem, yT_psum.at(b, g * CT + k + 1))
                        yT_ready.step(A(yT[:, k, g * HALF:(g + 1) * HALF], PS[:, 2 * k + g, :], ACT.Copy))
                act.wait_ge(yT_ready.sem, yT_ready.at(b, CT * NH))

                ln(b, 1)

                begins(act, b, "ffn0")
                act.wait_ge(s0_psum.sem, s0_psum.at(b, 1))
                s0_ready.step(A(s0, PS[:, 0, :], ACT.Identity, bias=bin2[:, 0:1]))
                act.wait_ge(s0_ready.sem, s0_ready.at(b, 1))
                for j in range(J_PE):
                    if j >= 4:
                        act.wait_ge(r0_used.sem, r0_used.at(b, j - 3))
                    r0_ready.step(A(r0[j % 4], s0, ACT.Relu, bias=b1[:, j:j + 1], scale=w1[:, j:j + 1]))
                ln(b, 2)

                begins(act, b, "xproj")

                def conv_start(d):
                    act.wait_ge(xr_psum.sem, xr_psum.at(b, d + 1))
                    if d >= 2:
                        act.wait_ge(xs_ready.sem, xs_ready.at(b, d - 1))
                    conv0.step(A(conv_t[d % 2], PS[:, 2 * (d % 2):2 * (d % 2) + 2, :].rearrange("p a n -> p (a n)"),
                                 ACT.Identity, bias=conv_b[:, d:d + 1], scale=conv_w[:, d, TAPS - 1:TAPS]))

                def conv_end(d):
                    act.wait_ge(conv_done.sem, conv_done.at(b, d + 1))
                    xs_ready.step(A(xs[:, d], conv_t[d % 2], ACT.Silu))

                conv_start(0)
                for d in range(1, DTL):
                    conv_start(d)
                    conv_end(d - 1)
                conv_end(DTL - 1)
                act.wait_ge(xd_psum.sem, xd_psum.at(b, 1))
                x_rows_ready.step(A(x_rows, PS[0:XR, 6:8, :].rearrange("p a n -> p (a n)"), ACT.Copy))
                for d in range(DTL):
                    psum = PS[:, 2 * (d % 2):2 * (d % 2) + 2, :].rearrange("p a n -> p (a n)")
                    act.wait_ge(dt_psum.sem, dt_psum.at(b, d + 1))
                    dt_abs.step(A(sp_e[d], psum, ACT.Abs, bias=b_dt[:, d:d + 1]))
                    dt_max.step(A(dt_t[:, d], psum, ACT.Relu, bias=b_dt[:, d:d + 1]))
                    act.wait_ge(dt_abs.sem, dt_abs.at(b, d + 1))
                    dt_exp.step(A(sp_e[d], sp_e[d], ACT.Exp, scale=-1.0))
                for d in range(DTL):
                    act.wait_ge(dt_corr.sem, dt_corr.at(b, d + 1))
                    dt_ln.step(A(sp_e[d], sp_e[d], ACT.Ln, bias=1.0))


                def bb_copy(s):
                    act.wait_ge(bb_psum.sem, bb_psum.at(b, s + 1))
                    if s >= 2:
                        act.wait_ge(u_ready.sem, u_ready.at(b, (s - 1) * DTL))
                    bb_ready.step(A(bb[(s + 1) % 2], PS[:, 6:8, :].rearrange("p a n -> p (a n)"), ACT.Copy))

                def keep_z(i):
                    act.wait_ge(z_psum.sem, z_psum.at(b, i + 1))
                    z_kept.step(A(z_tiles[i], PS[:, ZBANK, :] if i < NT - 1 else
                                  PS[:, ZBANK, :].rearrange("p (k n) -> p k n", k=CT), ACT.Copy))

                bb_copy(0)
                for s in range(S):
                    for d in range(DTL):
                        n = s * DTL + d
                        if n >= 2:
                            act.wait_ge(h_ready.sem, h_ready.at(b, n - 1))
                        if s == 0:
                            act.wait_ge(dt_ready.sem, dt_ready.at(b, d + 1))
                        if n == 1:
                            act.wait_ge(dt_sum.sem, dt_sum.at(b, DTL))
                        a_ready.step(A(a_r[n % 2], dt_t[:, d], ACT.Exp, scale=a_neg[:, s:s + 1]))
                        if d == 1 and s + 1 < S:
                            bb_copy(s + 1)
                        if d == DTL - 1 and s and s % 2 == 0:
                            keep_z(s // 2 - 1)
                keep_z(NT - 1)
                act.wait_ge(a_ready.sem, a_ready.at(b, S * DTL))
                act.wait_ge(z_kept.sem, z_kept.at(b, NT))

                for i in range(NT + 1):
                    if i < NT:
                        z_ready.step(A(z_tiles[i], z_tiles[i], ACT.Silu))
                    if i >= 1:
                        j = i - 1
                        act.wait_ge(ygT_psum.sem, ygT_psum.at(b, j + 1))
                        if j >= 2:
                            act.wait_ge(res_psum.sem, res_psum.at(b, 2 * NT + j - 1))
                        ygT_ready.step(A(ygT[j % 2].rearrange("p d t -> p (d t)"), PS[:, 6 + j % 2, :], ACT.Copy))
                act.wait_ge(ygT_ready.sem, ygT_ready.at(b, NT))

                ln(b, 3)

                begins(act, b, "ffn1")
                load_x(b + 1)
                for g in range(NH):
                    for f in range(FT):
                        n = g * FT + f
                        act.wait_ge(f_psum.sem, f_psum.at(b, n + 1))
                        f_ready.step(A(gl[:, f, g * HALF:(g + 1) * HALF], PS[:, n % 4, :], ACT.Gelu,
                                       bias=gelu_b[:, f:f + 1]))
                ln(b, 4)
                for h in range(NH):
                    act.wait_ge(x_added.sem, x_added.at(b, 3 * NT + (h + 1) * NT // NH))
                    x_stored[h].step(act.dma_start(tokens(t["out"], b, h), X[:, half_tiles(h), :]))
            for c in x_stored:
                act.wait_ge(c.sem, c.at(B, 0))

        @block.vector
        def _(dve):
            V = nc.vector
            steps = [0]

            def tick(ins):
                steps[0] += 1
                ins.then_inc(ev("up"), 1)

            def up_done():
                dve.wait_ge(ev("up"), steps[0])

            def up(ins):
                tick(ins)
                up_done()

            def rotated_columns():
                dve.wait_ge(ev("pre_loads"), 16 * N_LOADS)
                for m in range(2):
                    e = bd[:, m, 16:32].rearrange("p (n two) -> p n two", two=2)
                    r = bd[:, m, 32:48].rearrange("p (n two) -> p n two", two=2)
                    V.tensor_scalar(r[:, :, 0], e[:, :, 1], -1.0, None, ALU.mult).then_inc(ev("bd_ready"), 1)
                    V.tensor_copy(r[:, :, 1], e[:, :, 0]).then_inc(ev("bd_ready"), 1)

            def folded_weights():
                dve.wait_ge(ev("made"), 14)
                for j in range(J_PE):
                    V.tensor_scalar(diag_w2[:, j], ident[:, :], w2[:, j:j + 1], None, ALU.mult)
                dve.wait_ge(ev("fold_psum"), 1)
                for k in range(CT):
                    for m in range(2):
                        src = PS[:, 2 * m + k, 0:384].rearrange("p (a n j) -> p a n j", a=8, n=3)
                        for n in range(3):
                            dst = w_qk[:, k, m, n, :].rearrange("p (r a h) -> p h a r", a=8, h=2)
                            for h in range(2):
                                V.tensor_copy(dst[:, h], src[:, :, n, DE * h:DE * h + DE])
                    last = V.tensor_copy(w_v[:, k, :], PS[:, 4 + k, 0:C])
                last.then_inc(ev("folded"), 1)

            dve.wait_ge(ev("ffn1_loads"), 16 * 6)
            U = w_exp[:, :, :].rearrange("p k n -> p (k n)")
            for i in range(LEVELS):
                dve.wait_ge(ev(f"up_weights_{i % 2}"), 16 * (i // 2 + 1))
                tick(butterfly_level(dve, U, CT, 2 ** i, bf_w["up"][i % 2], bf_t[0], False, tick, up_done))
                up_done()
                butterfly_level(dve, bexp, 1, 2 ** i, bf_w["up"][i % 2], bf_t[0], False,
                                tick, up_done).then_inc(ev("up_level"), 1)
                dve.wait_ge(ev("up_level"), i + 1)
                if i == 3:
                    rotated_columns()
                if i == 5:
                    folded_weights()
            dve.wait_ge(ev("mod_copied"), 1)
            for l in range(2):
                for kind in (2, 5):
                    g = mod_row[:, l, kind * C:kind * C + C]
                    sign, size = bf_t[0][0][0:B, 0, 0:C], bf_t[0][1][0:B, 0, 0:C]
                    up(V.tensor_scalar(sign, g, 0.0, 2.0, ALU.is_ge, ALU.mult))
                    up(V.scalar_tensor_tensor(out=size, in0=g, scalar=-1.0, in1=g, op0=ALU.mult, op1=ALU.max))
                    up(V.tensor_scalar(size, size, 0.25, None, ALU.max))
                    up(V.scalar_tensor_tensor(out=g, in0=sign, scalar=1.0, in1=size, op0=ALU.subtract, op1=ALU.mult))
            V.memset(recip[:, 0, 0:1], 0.0).then_inc(ev("mod_rows"), 1)
            dve.wait_ge(ev("mod_T"), 1)
            dve.wait_ge(ev("mod_end"), 1)
            for l in range(2):
                for n in range(4):
                    dst = mod_col[:, l, n, :, 0:B]
                    src = PS[:, 6, (l * 4 + n) * CT * B:(l * 4 + n + 1) * CT * B].rearrange("p (k b) -> p k b", k=CT)
                    if n % 2:
                        last = V.tensor_copy(dst, src)
                    else:
                        V.tensor_scalar(dst, src, 1.0, None, ALU.add)
            last.then_inc(ev("mod_ready"), 1)
            dve.wait_ge(ev("down_T"), 1)
            V.tensor_copy(w_con[:, :, :].rearrange("p f c -> p (f c)"), PS[:, 0:4, :].rearrange("p a n -> p (a n)"))
            V.tensor_tensor(gelu_b[:, :], PS[:, 4, 0:FT], up_bias, ALU.add).then_inc(ev("bf_ready"), 1)
            dve.wait_ge(ev("bf_ready"), 1)
            dve.wait_ge(ev("mod_ready"), 1)
            dve.wait_ge(ev("less_set"), 4)

            def modulation(b):
                mod_b_ready.step(V.tensor_copy(mod_b[:, :, :, :].rearrange("p l n k -> p (l n k)"),
                                               mod_col[:, :, :, :, bass.ds(b, 1)].rearrange("p l n k b -> p (l n k b)")))

            def normalize(b, n, x, chain):
                V.memset(spare[:, :], 0.0)
                for i in range(NT):
                    last = V.bn_aggr(mv[:, i], bn[:, i])
                chain(last)
                var, less_half, bits, y, r, less_mean = (norm[:, i] for i in range(6))
                chain(V.tensor_scalar(var, mv[:, :, 1], LN_EPS, None, ALU.add))
                V.tensor_scalar(less_half, var, -0.5, None, ALU.mult)
                chain(V.tensor_scalar(bits.bitcast(I32), var.bitcast(I32), 1, None, ALU.logical_shift_right))
                chain(V.tensor_scalar(r.bitcast(I32), bits.bitcast(I32), -1.0, float(0x5f3759df),
                                      ALU.mult, ALU.add))
                for _ in range(3):
                    chain(V.tensor_tensor(y, r, r, ALU.mult))
                    chain(V.tensor_tensor(y, y, less_half, ALU.mult))
                    chain(V.scalar_tensor_tensor(out=r, in0=y, scalar=1.5, in1=r, op0=ALU.add, op1=ALU.mult))
                norm_ready.step(V.scalar_tensor_tensor(out=less_mean, in0=mv[:, :, 0], scalar=-1.0, in1=r,
                                                       op0=ALU.mult, op1=ALU.mult))
                for i in range(0, NT, 2):
                    xn_even.step(V.tensor_scalar(xn[:, i], x[:, i], mv[:, i, 0:1], r[:, i:i + 1],
                                                 ALU.subtract, ALU.mult))
                dve.wait_ge(xn_even.sem, xn_even.at(b, (n + 1) * NT // 2))

            def normalize_input(b, n, chain):
                for h in range(NH):
                    dve.wait_ge(x_loaded[h].sem, x_loaded[h].at(b, n // 4 + 1))
                    for i in range(h * NT // NH, (h + 1) * NT // NH):
                        last = V.bn_stats(bn[:, i], x_in[:, i])
                chain(last)
                normalize(b, n, x_in, chain)

            modulation(0)
            normalize_input(0, 0, up)

            with dve.Fori(0, B, 1) as b:
                def wait(c, n):
                    dve.wait_ge(c.sem, c.at(b, n))

                def own_(ins):
                    own_step("dve", dve, b, ins)

                def add_residuals(n, i, bank):
                    wait(res_psum, n * NT + i + 1)
                    x_added.step(V.tensor_tensor(X[:, i], X[:, i] if n else x_in[:, i], PS[:, bank, 0:C], ALU.add))
                    if n < 3 and i:
                        wait(x_added, n * NT + i)
                        V.bn_stats(bn[:, i - 1], X[:, i - 1])
                    if n < 3 and i == NT - 1:
                        wait(x_added, (n + 1) * NT)
                        own_(V.bn_stats(bn[:, i], X[:, i]))
                        normalize(b, n + 1, X, own_)

                begins(dve, b, "qkv")
                v_one = v_aug[:, :, :, DH:DH + 1].rearrange("p i h o -> p (i h) o")
                V.memset(v_one, 1.0)
                V.memset(v_flat[:, V_COLS:V_COLS + 16], 0.0)

                def times_cos(m):
                    wait(qk_psum, 3 * m + 2)
                    e = PS[:, (2, 0)[m]:(2, 0)[m] + 2, :].rearrange("p a n -> p (a n)")
                    qk_e_read.step(V.tensor_tensor(rope_e[m], e, cos[:, :], ALU.mult))

                def turned(m):
                    wait(qk_psum, 3 * m + 3)
                    r = PS[:, (4, 2)[m]:(4, 2)[m] + 2, :].rearrange("p a n -> p (a n)")
                    qk_r_read.step(V.tensor_tensor(rope_r[m], r, sin[:, :], ALU.mult))
                    wait(qk_e_read, m + 1)
                    wait(qk_r_read, m + 1)
                    roped.step(V.tensor_tensor(rope_e[m], rope_e[m], rope_r[m], ALU.add))

                def rest(u):
                    m, e = divmod(u, 2)
                    if e:
                        wait(roped, m + 1)
                    wait(piece1, u + 1)
                    src = rope_e[m] if e else qk_psum_c(m)
                    rest1.step(V.tensor_tensor(qk_rest[m][:, e], src, pieces[m][:, 0, e], ALU.subtract))

                def third_piece(u):
                    m, e = divmod(u, 2)
                    wait(piece2, u + 1)
                    wait(rest1, u + 1)
                    piece3.step(V.tensor_tensor(pieces[m][:, 2, e], qk_rest[m][:, e], pieces[m][:, 1, e],
                                                ALU.subtract))

                rest(0)
                times_cos(0)
                third_piece(0)
                turned(0)
                rest(1)
                rest(2)
                third_piece(1)
                times_cos(1)
                third_piece(2)
                turned(1)
                rest(3)
                third_piece(3)
                wait(piece3, 4)

                begins(dve, b, "attend")

                def row_maxima(n):
                    h, q, a, z = SPARTS[n]
                    wait(smax_psum, n + 1)
                    smax_read.step(V.tensor_reduce(slots[:, h * NT + q, a // HALF:a // HALF + 1],
                                                   PS[:, max_bank(n), 0:z - a], AX_X, ALU.max))

                def split_maxima(hg):
                    wait(smax_read, (hg + 1) * MAXES)
                    negm_ready.step(V.tensor_reduce(negm[:, :], slots[:, hg * HG * NT:(hg + 1) * HG * NT, :],
                                                    AX_X, ALU.max, negate=True))
                    wait(negm_T, hg + 1)
                    if hg:
                        wait(negm_in, PIECES * hg)
                    rows = PS[0:HG * NT, 6, 0:P]
                    own_(V.tensor_copy(n_pieces[:, 0], rows))
                    own_(V.tensor_tensor(n_rest[:, :], rows, n_pieces[:, 0], ALU.subtract))
                    own_(V.tensor_copy(n_pieces[:, 1], n_rest[:, :]))
                    negm_split.step(V.tensor_tensor(n_pieces[:, 2], n_rest[:, :], n_pieces[:, 1], ALU.subtract))

                def outputs_to_sbuf(n):
                    wait(pv_done, half_ends[n] + 1)
                    if n:
                        wait(o_psum, n)
                    oT_ready.step(V.tensor_copy(oT[0], PS[:, 4, :]))

                def divide(n):
                    hg, half = n // NH, n % NH
                    wait(o_psum, n + 1)
                    o = PS[:, 5, :].rearrange("p (i h d) -> p i h d", i=4, h=HG)
                    own_(V.reciprocal(o_rec, o[:, :, :, DH]))
                    for i in range(4):
                        ins = V.tensor_tensor(
                            y_at[:, 4 * half + i, hg * HG * DH:(hg + 1) * HG * DH].rearrange("p (h d) -> p h d", h=HG),
                            o[:, i, :, 0:DH], o_rec[:, i, :].unsqueeze(2).broadcast_to([P, HG, DH]), ALU.mult)
                    o_read.step(ins)

                for st in range(STEPS):
                    hg, j = divmod(st, MAX_STEPS + 2)
                    if hg < H // HG and j < MAX_STEPS:
                        for n in range(MAX_PER_STEP):
                            row_maxima(hg * MAXES + MAX_PER_STEP * j + n)
                    if hg < H // HG and j == MAX_STEPS:
                        split_maxima(hg)
                    g = st - LEAD - LAG
                    if g in half_ends:
                        outputs_to_sbuf(half_ends.index(g))
                    if g - 1 in half_ends:
                        divide(half_ends.index(g - 1))

                begins(dve, b, "project")
                for c in x_stored:
                    wait(c, 0)
                for i in range(NT):
                    add_residuals(0, i, 4 + i % 4)

                begins(dve, b, "ffn0")
                wait(s0_ready, 1)
                for j in range(J_PE, J):
                    r = r0_v[j % 2]
                    own_(V.tensor_scalar(r, s0, w1[:, j:j + 1], b1[:, j:j + 1], ALU.mult, ALU.add))
                    if j == J_PE:
                        own_(V.tensor_scalar(g0_v, r, 0.0, w2[:, j:j + 1], ALU.max, ALU.mult))
                    else:
                        own_(V.tensor_scalar(r, r, 0.0, w2[:, j:j + 1], ALU.max, ALU.mult))
                        own_(V.tensor_tensor(g0_v, g0_v, r, ALU.add))
                wait(r0_used, J_PE)
                g0_ready.step(V.scalar_tensor_tensor(out=g0, in0=PS[:, 1, :], scalar=b2[:, 0:1], in1=g0_v,
                                                     op0=ALU.add, op1=ALU.add))
                wait(x_biased, 1)
                for i in range(NT):
                    add_residuals(1, i, 4 + i % 4)

                begins(dve, b, "xproj")
                for d in range(DTL):
                    xr = PS[:, 2 * (d % 2):2 * (d % 2) + 2, :].rearrange("p a n -> p (a n)")
                    wait(conv0, d + 1)
                    for j in range(1, TAPS):
                        ins = V.scalar_tensor_tensor(out=conv_t[d % 2][:, j:T], in0=xr[:, 0:T - j],
                                                     scalar=conv_w[:, d, TAPS - 1 - j:TAPS - j],
                                                     in1=conv_t[d % 2][:, j:T], op0=ALU.mult, op1=ALU.add)
                        if j < TAPS - 1:
                            own_(ins)
                        else:
                            conv_done.step(ins)
                psb = PS[:, 6:8, :].rearrange("p a n -> p (a n)")
                wait(x_rows_ready, 1)
                own_(V.tensor_copy(b_piece, psb))
                own_(V.scalar_tensor_tensor(out=b_rest, in0=b_piece, scalar=less[:, 0:1], in1=psb,
                                            op0=ALU.mult, op1=ALU.add))
                own_(V.tensor_copy(b_piece, b_rest))
                b_split.step(V.scalar_tensor_tensor(out=b_st[:, :], in0=b_piece, scalar=less[:, 1:2], in1=b_rest,
                                                    op0=ALU.mult, op1=ALU.add))

                def lost_in_sum(d):
                    e, c = sp_e[d], sp_c[d % 2]
                    wait(dt_exp, d + 1)
                    if d >= 2:
                        wait(dt_sum, d - 1)
                    own_(V.tensor_scalar(c, e, 1.0, -1.0, ALU.add, ALU.add))
                    dt_corr.step(V.tensor_tensor(c, e, c, ALU.subtract))

                def times_d(i):
                    wait(d_psum, i + 1)
                    d_read.step(V.tensor_tensor(y_s[:, i], PS[:, 5 + i % 3, :], d_all[:, :], ALU.mult))

                wait(c_psum, 1)
                V.tensor_copy(c_t[:, :, :], PS[:, 4, 0:NT * 2 * S].rearrange("p (i s) -> p i s", i=NT)[:, :, S:2 * S])
                times_d(0)
                lost_in_sum(0)
                times_d(1)
                times_d(2)
                lost_in_sum(1)
                times_d(3)
                times_d(4)
                lost_in_sum(2)
                times_d(5)
                times_d(6)
                lost_in_sum(3)
                times_d(7)
                for d in range(DTL):
                    wait(dt_ln, d + 1)
                    wait(dt_sum, d + 1)
                    dt_ready.step(V.tensor_tensor(dt_t[:, d], dt_t[:, d], sp_e[d], ALU.add))
                    wait(dt_ready, d + 1)
                    dtx_ready.step(V.tensor_tensor(dtx[:, d], dt_t[:, d], xs[:, d], ALU.mult))


                def add_y(s, i):
                    n = s * NT + i
                    wait(h_T, n + 1)
                    if s:
                        wait(y_added, n - NT + 1)
                    y_added.step(V.scalar_tensor_tensor(out=y_s[:, i], in0=PS[:, n % HBANKS, :],
                                                        scalar=c_t[:, i, s:s + 1], in1=y_s[:, i],
                                                        op0=ALU.mult, op1=ALU.add))

                for s in range(S):
                    for d in range(DTL):
                        n = s * DTL + d
                        wait(a_ready, n + 1)
                        wait(u_ready, n + 1)
                        if n >= HRING:
                            wait(h_T, ((n - HRING) // DTL + 1) * NT)
                        h_ready.step(V.tensor_tensor_scan(h_r[n % HRING], a_r[n % 2], u_r[n % 2], 0.0,
                                                          ALU.mult, ALU.add))
                        if s:
                            for i in range(d * NT // DTL, (d + 1) * NT // DTL):
                                add_y(s - 1, i)

                add_y(S - 1, 0)
                for i in range(NT + 2):
                    if i + 1 < NT:
                        add_y(S - 1, i + 1)
                    if i < NT:
                        wait(z_ready, i + 1)
                        wait(y_added, (S - 1) * NT + i + 1)
                        if i >= 2:
                            wait(ygT_psum, i - 1)
                        if i < NT - 1:
                            yg_ready.step(V.tensor_tensor(yg[i % 2], y_s[:, i], z_tiles[i], ALU.mult))
                        else:
                            yg_ready.step(V.tensor_tensor(yg[i % 2].rearrange("p (k n) -> p k n", k=CT),
                                                          y_s[:, i].rearrange("p (k n) -> p k n", k=CT),
                                                          z_tiles[i], ALU.mult))
                    if i >= 2:
                        add_residuals(2, i - 2, OUT_BANKS[i % 2])

                begins(dve, b, "ffn1")
                modulation(b + 1)
                normalize_input(b, 4, own_)
                wait(x_biased, 2)
                for i in range(NT):
                    add_residuals(3, i, 4 + i % 4)
                wait(x_added, 4 * NT)

        @block.tensor
        def _(pe):
            mm, tr = nc.tensor.matmul, nc.tensor.transpose
            pe.wait_ge(ev("pre_loads"), 16 * N_LOADS)
            pe.wait_ge(ev("bd_ready"), 4)
            for k in range(CT):
                for m in range(3):
                    w = 32 if m == 2 else 48
                    for a in range(8):
                        last = mm(PS[:, 4 + k if m == 2 else 2 * m + k, a * w:(a + 1) * w],
                                  wT[:, m, a, k * P:(k + 1) * P], bd[:, m, 0:w], start=True, stop=True)
            last.then_inc(ev("fold_psum"), 1)
            pe.wait_ge(ev("folded"), 1)
            pe.wait_ge(ev("c_silu"), 1)
            for l in range(2):
                for n in range(3):
                    for k in range(CT):
                        last = mm(PS[0:B, 3 * l + n, :], cT[:, l, k, :], wmod[:, l, k, n * 512:(n + 1) * 512],
                                  start=(k == 0), stop=(k == CT - 1))
                last.then_inc(ev("mod_psum"), 1)
            pe.wait_ge(ev("mod_rows"), 1)
            pe.wait_ge(ev("made"), 14)
            for l in range(2):
                for n, kind in enumerate((1, 0, 4, 3)):
                    for k in range(CT):
                        c = kind * C + k * P
                        o = ((l * 4 + n) * CT + k) * B
                        last = tr(PS[:, 6, o:o + B], mod_row[:, l, c:c + P], ident[0:B, 0:B])
            last.then_inc(ev("mod_T"), 1)
            pe.wait_ge(ev("down_level"), LEVELS)
            D = w_con[:, :, :].rearrange("p f c -> p (f c)").rearrange("p (k n) -> p k n", k=CT)
            for f in range(FT):
                for k in range(CT):
                    tr(PS[:, f // 2, (f % 2) * C + k * P:(f % 2) * C + (k + 1) * P],
                       D[:, k, f * P:(f + 1) * P], ident[:, :])
            pe.wait_ge(ev("up_level"), LEVELS)
            for f in range(FT):
                last = mm(PS[:, 4, f:f + 1], bexp[0:1, f * P:(f + 1) * P], ones[0:1, 0:1], start=True, stop=True)
            last.then_inc(ev("down_T"), 1)
            pe.wait_ge(ev("bf_ready"), 1)

            def turn_xn(b, n, g):
                for i in range(g * NT // NH, (g + 1) * NT // NH):
                    c = (xn_even, xn_odd)[i % 2]
                    pe.wait_ge(c.sem, c.at(b, n * NT // 2 + i // 2 + 1))
                    for k in range(CT):
                        last = tr(PS[:, 2 * k + g, (i % 4) * P:(i % 4 + 1) * P],
                                  xn[:, i, k * P:(k + 1) * P], ident[:, :])
                    hT_psum.step(last)

            def ln(b, n):
                for g in range(NH):
                    turn_xn(b, n, g)
                pe.wait_ge(hT_ready.sem, hT_ready.at(b, (n + 1) * CT * NH))

            ln(0, 0)

            with pe.Fori(0, B, 1) as b:
                def wait(c, n):
                    pe.wait_ge(c.sem, c.at(b, n))

                begins(pe, b, "qkv")
                for m in range(2):
                    for n in range(3):
                        bank = ((0, 2, 4), (6, 0, 2))[m][n]
                        if not m and n == 2:
                            wait(x_added, 0)
                        if m and n == 1:
                            wait(rest1, 1)
                        if m and n == 2:
                            wait(qk_e_read, 1)
                        for g in range(NH):
                            for k in range(CT):
                                last = mm(PS[:, bank + g, :], w_qk[:, k, m, n, :], hT[:, k, g * HALF:(g + 1) * HALF],
                                          start=(k == 0), stop=(k == CT - 1))
                        qk_psum.step(last)
                for i in range(NT):
                    if i == 0:
                        wait(qk_r_read, 1)
                    if i == 2:
                        wait(rest1, 3)
                    if i >= 4:
                        wait(v_ready, i - 3)
                    for k in range(CT):
                        last = mm(PS[:, 4 + i % 4, 0:C], hT[:, k, i * P:(i + 1) * P], w_v[:, k, :],
                                  start=(k == 0), stop=(k == CT - 1))
                    v_psum.step(last)
                wait(qk_r_read, 2)

                begins(pe, b, "attend")
                wait(v_ready, NT)
                wait(stacks_in, 4 * len(PIECE_OF[0]) + 1)

                def scores_for_max(n):
                    h, q, a, z = SPARTS[n]
                    if n % MAXES == 0 and n:
                        wait(negm_split, n // MAXES)
                    ring = len(MAX_BANKS) if n < MAXES else 2
                    if n >= ring:
                        wait(smax_read, n - ring + 1)
                    bank = max_bank(n)
                    diag = z == (q + 1) * P
                    last = mm(PS[:, bank, 0:z - a], q_st[0:KROWS, h, q * P:(q + 1) * P], k_st[0:KROWS, h, a:z],
                              start=True, stop=not diag)
                    if diag:
                        last = mm(PS[:, bank, z - a - P:z - a], identb[:, :], mask_qk[:, :], start=False, stop=True)
                    smax_psum.step(last)

                def scores(g, part_of):
                    if g >= 2 and part_of == 0:
                        wait(p_ready, g - 1)
                    for n in range(part_of * PER_CHUNK // 2, (part_of + 1) * PER_CHUNK // 2):
                        h, q, k = BLOCKS[PER_CHUNK * g + n]
                        o = PS[:, 2 * (g % 2) + n // 4, (n % 4) * P:(n % 4 + 1) * P]
                        last = mm(o, k_st[0:NEAR, h, k * P:(k + 1) * P], q_st[0:NEAR, h, q * P:(q + 1) * P],
                                  start=True, stop=k < q)
                        if k == q:
                            last = mm(o, identb[:, :], mask_kq[:, :], start=False, stop=True)
                    if part_of:
                        s_psum.step(last)

                def turn(n):
                    wait(oT_ready, n + 1)
                    if n:
                        wait(o_read, n)
                    for i in range(4):
                        last = tr(PS[:, 5, i * P:(i + 1) * P], oT[0][:, i * P:(i + 1) * P], ident[:, :])
                    o_psum.step(last)

                def times_v(g, part_of):
                    if part_of == 0:
                        wait(p_ready, g + 1)
                    start = PER_CHUNK * g + part_of * PER_CHUNK // 2
                    for n in range(start, start + PER_CHUNK // 2):
                        h, q, k = BLOCKS[n]
                        half, r = NH * (h // HG) + q // 4, 32 * (h % HG)
                        if half and k == 0 and q % 4 == 0 and r == 0:
                            wait(oT_ready, half)
                        v = (k * H + h) * (DH + 1)
                        last = mm(PS[r:r + 32, 4, (q % 4) * P:(q % 4 + 1) * P], v_flat[:, v:v + 32],
                                  pT[(n // PER_CHUNK) % P_RING][:, (n % PER_CHUNK) * P:(n % PER_CHUNK + 1) * P],
                                  start=(k == 0), stop=(k == q), tile_position=(0, r))
                    if part_of:
                        pv_done.step(last)

                for st in range(STEPS):
                    hg, j = divmod(st, MAX_STEPS + 2)
                    g = st - LEAD
                    maxima = hg < H // HG and j < MAX_STEPS
                    if 0 <= g < CHUNKS and g % GROUP_CHUNKS == 0:
                        wait(negm_in, PIECES * (g // GROUP_CHUNKS + 1))
                    for part_of in range(2):
                        if 0 <= g < CHUNKS:
                            scores(g, part_of)
                        if maxima:
                            scores_for_max(hg * MAXES + MAX_PER_STEP * j + part_of)
                    if hg < H // HG and j == MAX_STEPS:
                        wait(negm_ready, hg + 1)
                        negm_T.step(tr(PS[0:HG * NT, 6, 0:P], negm[:, :], ident[:, :]))
                    if g - LAG - 1 in half_ends:
                        turn(half_ends.index(g - LAG - 1))
                    for part_of in range(2):
                        if 0 <= g - LAG < CHUNKS:
                            times_v(g - LAG, part_of)
                        if maxima and 2 + part_of < MAX_PER_STEP:
                            scores_for_max(hg * MAXES + MAX_PER_STEP * j + 2 + part_of)

                begins(pe, b, "project")
                for g in range(NH):
                    for k in range(CT):
                        for i in range(4):
                            last = tr(PS[:, 2 * k + g, i * P:(i + 1) * P],
                                      y_at[:, 4 * g + i, k * P:(k + 1) * P], ident[:, :])
                        yT_psum.step(last)
                wait(w_g_ready, 1)
                for i in range(NT):
                    wait(yT_ready, CT * (i // 4 + 1))
                    if i >= 4:
                        wait(x_added, i - 3)
                    for k in range(CT):
                        last = mm(PS[:, 4 + i % 4, 0:C], yT[:, k, i * P:(i + 1) * P], w_g[:, k, :],
                                  start=(k == 0), stop=(k == CT - 1))
                    res_psum.step(last)
                ln(b, 1)

                begins(pe, b, "ffn0")
                for g in range(NH):
                    for k in range(CT):
                        last = mm(PS[M * g:M * g + M, 0, :], w_in0[:, k, :], hT[:, k, g * HALF:(g + 1) * HALF],
                                  start=(k == 0), stop=(k == CT - 1))
                s0_psum.step(last)
                for j in range(J_PE):
                    wait(r0_ready, j + 1)
                    last = mm(PS[:, 1, :], diag_w2[:, j], r0[j % 4], start=(j == 0), stop=(j == J_PE - 1))
                    r0_used.step(last)
                wait(g0_ready, 1)
                wait(w_g_ready, 2)
                for i in range(NT):
                    rows = slice(M * (i // 4), M * (i // 4) + M)
                    if i >= 4:
                        wait(x_added, NT + i - 3)
                    res_psum.step(mm(PS[:, 4 + i % 4, 0:C], g0[rows, (i % 4) * P:(i % 4 + 1) * P], w_g[rows, 0, :],
                                     start=True, stop=True))
                ln(b, 2)

                begins(pe, b, "xproj")

                def from_h(d):
                    if d >= 2:
                        wait(conv_done, d - 1)
                    for g in range(NH):
                        for k in range(CT):
                            last = mm(PS[:, 2 * (d % 2) + g, :], w_in1[:, k, d * P:(d + 1) * P],
                                      hT[:, k, g * HALF:(g + 1) * HALF], start=(k == 0), stop=(k == CT - 1))
                    xr_psum.step(last)

                def from_x(d):
                    wait(xs_ready, d + 1)
                    for g in range(NH):
                        last = mm(PS[:, 6 + g, :], w_x[:, d, :], xs[:, d, g * HALF:(g + 1) * HALF],
                                  start=(d == 0), stop=(d == DTL - 1))
                    if d == DTL - 1:
                        xd_psum.step(last)

                def to_dt(d):
                    if d >= 2:
                        wait(dt_max, d - 1)
                    for g in range(NH):
                        last = mm(PS[:, 2 * (d % 2) + g, :], w_dt[:, d * P:(d + 1) * P],
                                  x_rows[0:R, g * HALF:(g + 1) * HALF], start=True, stop=True)
                    dt_psum.step(last)

                def turn_x(i):
                    if i >= 3:
                        wait(d_read, i - 2)
                    for d in range(DTL):
                        last = tr(PS[:, 5 + i % 3, d * P:(d + 1) * P], xs[:, d, i * P:(i + 1) * P], ident[:, :])
                    d_psum.step(last)

                for d in range(DTL):
                    from_h(d)
                    if d >= 2:
                        from_x(d - 2)
                from_x(2)
                from_x(3)
                wait(x_rows_ready, 1)
                to_dt(0)
                for i in range(NT):
                    last = tr(PS[:, 4, i * 2 * S:(i + 1) * 2 * S], x_rows[R:XR, i * P:(i + 1) * P],
                              ident[R:XR, R:XR])
                c_psum.step(last)
                to_dt(1)
                turn_x(0)
                wait(b_split, 1)
                turn_x(1)
                to_dt(2)
                turn_x(2)
                turn_x(3)
                to_dt(3)
                for i in range(4, NT):
                    turn_x(i)

                def spread_b(s):
                    if s:
                        wait(bb_ready, s)
                    else:
                        wait(d_read, NT)
                    for g in range(NH):
                        last = mm(PS[:, 6 + g, :], sel[:, s], b_st[:, g * HALF:(g + 1) * HALF], start=True, stop=True)
                    bb_psum.step(last)

                spread_b(0)
                spread_b(1)
                for s in range(S):
                    if s % 2 == 0:
                        i = s // 2
                        if i:
                            wait(z_kept, i)
                        for k in range(CT):
                            last = mm(PS[:, ZBANK, :], hT[:, k, i * P:(i + 1) * P], w_in1[:, k, DI:2 * DI],
                                      start=(k == 0), stop=(k == CT - 1))
                        z_psum.step(last)
                    wait(h_ready, (s + 1) * DTL)
                    for i in range(NT):
                        n = s * NT + i
                        if i == 3 and s + 2 < S:
                            spread_b(s + 2)
                        if n >= HBANKS:
                            wait(y_added, n - HBANKS + 1)
                        for d in range(DTL):
                            last = tr(PS[:, n % HBANKS, d * P:(d + 1) * P],
                                      h_r[(s * DTL + d) % HRING][:, i * P:(i + 1) * P], ident[:, :])
                        h_T.step(last)
                wait(z_kept, NT)
                for i in range(NT + 2):
                    if i == 2:
                        wait(w_g_ready, 3)
                    if 1 <= i <= NT:
                        j = i - 1
                        wait(yg_ready, j + 1)
                        if j >= 2:
                            wait(ygT_ready, j - 1)
                        for d in range(DTL):
                            last = tr(PS[:, 6 + j % 2, d * P:(d + 1) * P], yg[j % 2][:, d * P:(d + 1) * P], ident[:, :])
                        ygT_psum.step(last)
                    if i >= 2:
                        j = i - 2
                        wait(ygT_ready, j + 1)
                        if j >= 2:
                            wait(x_added, 2 * NT + j - 1)
                        if j == 1:
                            wait(y_added, (S - 1) * NT + OUT_BANKS[1] + 1)
                        for d in range(DTL):
                            last = mm(PS[:, OUT_BANKS[j % 2], 0:C], ygT[j % 2][:, d], w_g[:, d, :],
                                      start=(d == 0), stop=(d == DTL - 1))
                        res_psum.step(last)
                ln(b, 3)

                begins(pe, b, "ffn1")
                for g in range(NH):
                    for f in range(FT):
                        n = g * FT + f
                        if n >= 4:
                            wait(f_ready, n - 3)
                        for k in range(CT):
                            last = mm(PS[:, n % 4, :], w_exp[:, k, f * P:(f + 1) * P], hT[:, k, g * HALF:(g + 1) * HALF],
                                      start=(k == 0), stop=(k == CT - 1))
                        f_psum.step(last)
                wait(w_g_ready, 4)
                for i in range(NT):
                    wait(f_ready, FT * (i // 4 + 1))
                    if i >= 4:
                        wait(x_added, 3 * NT + i - 3)
                    if i in (4, 5):
                        turn_xn(b, 4, i - 4)
                    for f in range(FT):
                        last = mm(PS[:, 4 + i % 4, 0:C], gl[:, f, i * P:(i + 1) * P], w_g[:, f, :],
                                  start=(f == 0), stop=(f == FT - 1))
                    res_psum.step(last)
                wait(hT_ready, 5 * CT * NH)

        wrong = {n: c.made for n, c in counts if c.made != c.per + c.early}
        assert not wrong, wrong


def butterfly_level(eng, x, k, s, w, tmp, transposed, tick, sync):
    n = x.shape[1] // k
    v = x.rearrange("p (a two s) -> p a two s", two=2, s=s)
    a, b = v[:, :, 0, :], v[:, :, 1, :]
    na = n // (2 * s)

    def weight(i, j):
        i, j = (j, i) if transposed else (i, j)
        return w[:, i, j, :].rearrange("p (a s) -> p a s", s=s)

    def tile(j):
        return tmp[j].rearrange("p k n -> p (k n)")[:, 0:k * n // 2].rearrange("p (a s) -> p a s", s=s)

    def times(dst, src, wt):
        for c in range(k):
            r = slice(c * na, (c + 1) * na)
            tick(eng.tensor_tensor(dst[:, r, :], src[:, r, :], wt, ALU.mult))

    t0, t1, t2 = (tile(j) for j in range(3))
    times(t0, a, weight(0, 0))
    times(t1, b, weight(0, 1))
    times(t2, a, weight(1, 0))
    sync()
    tick(eng.tensor_tensor(a, t0, t1, ALU.add))
    sync()
    times(t0, b, weight(1, 1))
    sync()
    return eng.tensor_tensor(b, t2, t0, ALU.add)


N_LOADS = 45

_LAYOUT = {
    "WqT": ("L0_attn_Wq_down", lambda a: a.T), "WkT": ("L0_attn_Wk_down", lambda a: a.T),
    "WvT": ("L0_attn_Wv_down", lambda a: a.T), "L0_cT": ("L0_c", lambda a: a.T), "L1_cT": ("L1_c", lambda a: a.T),
    "L1_attn_W_inT": ("L1_attn_W_in", lambda a: a.T), "L1_attn_W_xT": ("L1_attn_W_x", lambda a: a.T),
    "L1_attn_W_dtT": ("L1_attn_W_dt", lambda a: a.T), "L1_attn_W_outT": ("L1_attn_W_out", lambda a: a.T),
    "L1_ffn_W_conT": ("L1_ffn_W_con", lambda a: a.T),
    "conv_b": ("L1_attn_conv_b", lambda a: a.reshape(-1, P).T), "b_dt": ("L1_attn_b_dt", lambda a: a.reshape(-1, P).T),
    "up_bias": ("L1_ffn_up_bias", lambda a: a.reshape(-1, P).T),
    "up_w": ("L1_ffn_up_weights", lambda a: a.transpose(0, 2, 3, 1).reshape(a.shape[0], -1)),
    "down_w": ("L1_ffn_down_weights", lambda a: a.transpose(0, 2, 3, 1).reshape(a.shape[0], -1)),
}
_AS_THEY_COME = [
    "L0_attn_Wq_up_c", "L0_attn_Wq_up_e", "L0_attn_Wk_up_c", "L0_attn_Wk_up_e", "L0_attn_Wv_up",
    "L0_attn_Wc", "L0_ffn_Win", "L0_ffn_bin_", "L0_ffn_W1", "L0_ffn_b1", "L0_ffn_W2", "L0_ffn_b2", "L0_ffn_Wout",
    "L0_ffn_bout", "L0_wmod", "L1_wmod", "L1_attn_conv_w", "L1_attn_A_log", "L1_ffn_W_exp", "L1_ffn_b_exp",
    "L1_ffn_b_con", "L1_ffn_down_bias", "L1_attn_D",
]


def kernel(**inputs):
    import numpy as np
    import concourse.bacc as _bacc
    from concourse import mybir as _mybir
    from concourse.bass_utils import run_bass_kernel_spmd as _run

    nc = _bacc.Bacc("TRN2", target_bir_lowering=False, num_devices=1)
    arrays, t = {}, {}

    def give(name, a):
        a = np.ascontiguousarray(a)
        arrays[f"in_{name}"] = a
        t[name] = nc.dram_tensor(f"in_{name}", a.shape, _mybir.dt.from_np(a.dtype), kind="ExternalInput").ap()

    for name in _AS_THEY_COME:
        give(name, np.asarray(inputs[name]))
    x = np.asarray(inputs["L0_attn_x"])
    give("L0_attn_x", np.concatenate([x, x[:1]], axis=0))
    for name, (source, layout) in _LAYOUT.items():
        give(name, layout(np.asarray(inputs[source])))
    T, DE = inputs["L0_attn_x"].shape[1], 8
    inv = (1.0 / np.float32(10000.0) ** (np.arange(0, DE, 2, dtype=np.float32) / np.float32(DE))).astype(np.float32)
    angle = (np.arange(T, dtype=np.float32)[:, None] * inv[None, :]).astype(np.float32)
    rows = np.repeat(np.concatenate([angle, angle], axis=1).T, 16, axis=0)
    give("cos", np.cos(rows).astype(np.float32))
    give("sin", np.sin(rows).astype(np.float32))
    shape = inputs["L0_attn_x"].shape
    t["out"] = nc.dram_tensor("out_0", shape, _mybir.dt.float32, kind="ExternalOutput").ap()
    adaln_kernel(nc, t)
    r = _run(nc, [arrays], core_ids=[0])
    return r.results[0]["out_0"]
```
